# Optimizing a Trainium2 kernel written in Bass

```python
import numpy as np
import jax
import jax.numpy as jnp

def _softmax(x, axis=-1):
    return jax.nn.softmax(x, axis=axis)

def _gelu(x):
    return jax.nn.gelu(x, approximate=True)

def _silu(x):
    return jax.nn.silu(x)

def _sigmoid(x):
    return jax.nn.sigmoid(x)

def _layernorm(x, axis=-1, eps=1e-05):
    m = jnp.mean(x, axis=axis, keepdims=True)
    v = jnp.var(x, axis=axis, keepdims=True)
    return (x - m) / jnp.sqrt(v + eps)

def _scatter_add(tgt, idx, src, axis=0):
    return tgt.at[idx].add(src)

def _segment_sum(src, seg, n):
    return jax.ops.segment_sum(src, seg, n)
kernel_name = 'mk_adj_ffn_d2_adj_r2_5ee16c'

def setup_inputs(seed: int=0):
    np.random.seed(seed)
    _w = jnp.asarray

    def _rec_inputs():
        import jax
        import jax.numpy as jnp
        _gk = jax.random.key(seed)
        x = 0.0002141 + 1 * jax.random.normal(jax.random.fold_in(_gk, 1), (1536, 128), jnp.float32)
        _a = jax.random.bernoulli(jax.random.fold_in(_gk, 2), 0.00130208, (1536, 1536))
        adj = _a.astype(jnp.int32)
        return (x, adj)
    x, adj = _rec_inputs()

    def _L0_gnn_setup():
        import jax, jax.numpy as jnp
        import numpy as np
        N, C, H = (1536, 128, 8)
        D = C // H
        key = jax.random.key(seed)
        k = jax.random.split(key, 7)
        node_features = jax.random.normal(k[0], (N, C), dtype=jnp.float32)
        adjacency = jax.random.randint(k[1], (N, N), 0, 2, dtype=jnp.int32)
        W = jax.random.normal(k[2], (C, C), dtype=jnp.float32) * (1.0 / np.sqrt(C))
        bW = jax.random.normal(k[3], (C,), dtype=jnp.float32) * 0.02
        a1 = jax.random.normal(k[4], (D,), dtype=jnp.float32) * (1.0 / np.sqrt(2 * D))
        a2 = jax.random.normal(k[5], (D,), dtype=jnp.float32) * (1.0 / np.sqrt(2 * D))
        ab = jax.random.normal(k[6], (), dtype=jnp.float32) * 0.02
        return {'node_features': node_features, 'adjacency': adjacency, 'W': W, 'bW': bW, 'a1': a1, 'a2': a2, 'ab': ab}
    _L0_gnn_all = _L0_gnn_setup()
    _L0_gnn_in = {k: v for k, v in _L0_gnn_all.items() if k in ('W', 'bW', 'a1', 'a2', 'ab')}
    del _L0_gnn_all

    def _L0_ffn_setup():
        import jax, jax.numpy as jnp
        import numpy as np
        D_MODEL = 128
        N_EXPERTS = 16
        HIDDEN = 256
        SCALE = 0.02
        key = jax.random.key(seed)
        ks = jax.random.split(key, 5)
        x = jax.random.normal(ks[0], (4, 4096, D_MODEL), dtype=jnp.float32)
        gate_w = jax.random.normal(ks[1], (D_MODEL, N_EXPERTS), dtype=jnp.float32) * SCALE
        gate_b = jnp.zeros((N_EXPERTS,), dtype=jnp.float32)
        w1 = jax.random.normal(ks[2], (N_EXPERTS, D_MODEL, HIDDEN), dtype=jnp.float32) * SCALE
        w2 = jax.random.normal(ks[3], (N_EXPERTS, D_MODEL, HIDDEN), dtype=jnp.float32) * SCALE
        w3 = jax.random.normal(ks[4], (N_EXPERTS, HIDDEN, D_MODEL), dtype=jnp.float32) * SCALE
        return {'x': x, 'gate_w': gate_w, 'gate_b': gate_b, 'w1': w1, 'w2': w2, 'w3': w3}
    _L0_ffn_all = _L0_ffn_setup()
    _L0_ffn_in = {k: v for k, v in _L0_ffn_all.items() if k in ('gate_w', 'gate_b', 'w1', 'w2', 'w3')}
    del _L0_ffn_all

    def _L1_gnn_setup():
        import jax, jax.numpy as jnp
        import numpy as np
        N = 4096
        IN_DIM = 128
        OUT_DIM = 128
        NEG_INF = -9000000000000000.0
        key = jax.random.key(seed)
        k1, k2, k3, k4, k5 = jax.random.split(key, 5)
        worker_x = jax.random.normal(k1, (N, IN_DIM), dtype=jnp.float32)
        ww_adj = jax.random.randint(k2, (N, N), 0, 2, dtype=jnp.int32)
        W = jax.random.normal(k3, (IN_DIM, OUT_DIM), dtype=jnp.float32) * (1.0 / np.sqrt(IN_DIM))
        a_src = jax.random.normal(k4, (OUT_DIM, 1), dtype=jnp.float32) * (1.414 / np.sqrt(OUT_DIM))
        a_dst = jax.random.normal(k5, (OUT_DIM, 1), dtype=jnp.float32) * (1.414 / np.sqrt(OUT_DIM))
        return {'worker_x': worker_x, 'ww_adj': ww_adj, 'W': W, 'a_src': a_src, 'a_dst': a_dst}
    _L1_gnn_all = _L1_gnn_setup()
    _L1_gnn_in = {k: v for k, v in _L1_gnn_all.items() if k in ('W', 'a_src', 'a_dst')}
    del _L1_gnn_all

    def _L1_ffn_setup():
        import jax, jax.numpy as jnp
        import numpy as np
        B, T, IN_DIM = (64, 128, 128)
        HID, OUT_DIM = (256, 128)
        N_LAYERS, N_EXPERTS, N_SHARED = (2, 16, 1)
        key = jax.random.key(seed)
        ks = jax.random.split(key, 10)
        s = 0.02
        x = jax.random.normal(ks[0], (B, T, IN_DIM), dtype=jnp.float32)
        route_id = jax.random.randint(ks[1], (B,), 0, N_EXPERTS)
        Wi = jax.random.normal(ks[2], (HID, IN_DIM), dtype=jnp.float32) * s
        bi = jnp.zeros((HID,), dtype=jnp.float32)
        Wr = jax.random.normal(ks[3], (N_LAYERS, N_EXPERTS, HID, HID), dtype=jnp.float32) * s
        br = jax.random.normal(ks[4], (N_LAYERS, N_EXPERTS, HID), dtype=jnp.float32) * s
        Ws = jax.random.normal(ks[5], (N_LAYERS, N_SHARED, HID, HID), dtype=jnp.float32) * s
        bs = jax.random.normal(ks[6], (N_LAYERS, N_SHARED, HID), dtype=jnp.float32) * s
        Wo = jax.random.normal(ks[7], (OUT_DIM, HID), dtype=jnp.float32) * s
        bo = jnp.zeros((OUT_DIM,), dtype=jnp.float32)
        return {'x': x, 'route_id': route_id, 'Wi': Wi, 'bi': bi, 'Wr': Wr, 'br': br, 'Ws': Ws, 'bs': bs, 'Wo': Wo, 'bo': bo}
    _L1_ffn_all = _L1_ffn_setup()
    _L1_ffn_in = {k: v for k, v in _L1_ffn_all.items() if k in ('route_id', 'Wi', 'bi', 'Wr', 'br', 'Ws', 'bs', 'Wo', 'bo')}
    del _L1_ffn_all
    return {'x': x, 'adj': adj, 'L0_gnn_W': _L0_gnn_in['W'], 'L0_gnn_bW': _L0_gnn_in['bW'], 'L0_gnn_a1': _L0_gnn_in['a1'], 'L0_gnn_a2': _L0_gnn_in['a2'], 'L0_gnn_ab': _L0_gnn_in['ab'], 'L0_ffn_gate_w': _L0_ffn_in['gate_w'], 'L0_ffn_gate_b': _L0_ffn_in['gate_b'], 'L0_ffn_w1': _L0_ffn_in['w1'], 'L0_ffn_w2': _L0_ffn_in['w2'], 'L0_ffn_w3': _L0_ffn_in['w3'], 'L1_gnn_W': _L1_gnn_in['W'], 'L1_gnn_a_src': _L1_gnn_in['a_src'], 'L1_gnn_a_dst': _L1_gnn_in['a_dst'], 'L1_ffn_route_id': _L1_ffn_in['route_id'], 'L1_ffn_Wi': _L1_ffn_in['Wi'], 'L1_ffn_bi': _L1_ffn_in['bi'], 'L1_ffn_Wr': _L1_ffn_in['Wr'], 'L1_ffn_br': _L1_ffn_in['br'], 'L1_ffn_Ws': _L1_ffn_in['Ws'], 'L1_ffn_bs': _L1_ffn_in['bs'], 'L1_ffn_Wo': _L1_ffn_in['Wo'], 'L1_ffn_bo': _L1_ffn_in['bo']}

def reference(x, adj, L0_gnn_W, L0_gnn_bW, L0_gnn_a1, L0_gnn_a2, L0_gnn_ab, L0_ffn_gate_w, L0_ffn_gate_b, L0_ffn_w1, L0_ffn_w2, L0_ffn_w3, L1_gnn_W, L1_gnn_a_src, L1_gnn_a_dst, L1_ffn_route_id, L1_ffn_Wi, L1_ffn_bi, L1_ffn_Wr, L1_ffn_br, L1_ffn_Ws, L1_ffn_bs, L1_ffn_Wo, L1_ffn_bo):
    import jax
    import jax.numpy as jnp

    def _L0_gnn_ref(node_features, adjacency, W, bW, a1, a2, ab):
        import jax, jax.numpy as jnp
        import numpy as np
        N, C, H = (1536, 128, 8)
        D = C // H
        h = node_features @ W.T + bW
        hh = h.reshape(N, H, D)
        si = jnp.einsum('nhd,d->nh', hh, a1)
        sj = jnp.einsum('nhd,d->nh', hh, a2)
        raw = si[:, None, :] + sj[None, :, :] + ab
        raw = jnp.where(raw > 0, raw, 0.2 * raw)
        scores = jnp.transpose(raw, (2, 0, 1))
        scores = jnp.where(adjacency[None, :, :] == 0, jnp.float32(-1000000000.0), scores)
        attn = jax.nn.softmax(scores, axis=-1)
        agg = jnp.einsum('hij,jhd->ihd', attn, hh).reshape(N, C)
        out = agg + node_features
        return jax.nn.elu(out)

    def _L0_ffn_ref(x, gate_w, gate_b, w1, w2, w3):
        import jax, jax.numpy as jnp
        import numpy as np
        D_MODEL = 128
        N_EXPERTS = 16
        HIDDEN = 256
        SCALE = 0.02
        n_experts = w1.shape[0]
        logits = jnp.einsum('bsd,de->bse', x, gate_w) + gate_b
        probs = jax.nn.softmax(logits, axis=-1)
        top_probs, top_idx = jax.lax.top_k(probs, 2)
        top_probs = top_probs / jnp.sum(top_probs, axis=-1, keepdims=True)
        dispatch = jnp.sum(jax.nn.one_hot(top_idx, n_experts, dtype=x.dtype) * top_probs[..., None], axis=-2)
        h1 = jnp.einsum('bsd,edh->bseh', x, w1)
        h2 = jnp.einsum('bsd,edh->bseh', x, w2)
        hidden = jax.nn.silu(h1) * h2
        expert_out = jnp.einsum('bseh,eho->bseo', hidden, w3)
        return jnp.einsum('bseo,bse->bso', expert_out, dispatch)

    def _L1_gnn_ref(worker_x, ww_adj, W, a_src, a_dst):
        import jax, jax.numpy as jnp
        import numpy as np
        N = 4096
        IN_DIM = 128
        OUT_DIM = 128
        NEG_INF = -9000000000000000.0
        Wh = worker_x @ W
        f_src = Wh @ a_src
        f_dst = Wh @ a_dst
        e = jax.nn.leaky_relu(f_src + f_dst.T, negative_slope=0.2)
        attention = jnp.where(ww_adj > 0, e, NEG_INF)
        attention = jax.nn.softmax(attention, axis=-1)
        h_prime = attention @ Wh
        return jax.nn.elu(h_prime)

    def _L1_ffn_ref(x, route_id, Wi, bi, Wr, br, Ws, bs, Wo, bo):
        import jax, jax.numpy as jnp
        import numpy as np
        B, T, IN_DIM = (64, 128, 128)
        HID, OUT_DIM = (256, 128)
        N_LAYERS, N_EXPERTS, N_SHARED = (2, 16, 1)
        flat = x.reshape(-1, x.shape[-1])
        n_tok = flat.shape[0]
        route = jnp.repeat(route_id, n_tok // route_id.shape[0])
        h = jax.nn.relu(flat @ Wi.T + bi)
        n_layers, n_experts = (Wr.shape[0], Wr.shape[1])
        for l in range(n_layers):
            shared = (jnp.einsum('nd,shd->snh', h, Ws[l]) + bs[l][:, None, :]).mean(axis=0)
            routed = jnp.zeros_like(h)
            for e in range(n_experts):
                ye = h @ Wr[l, e].T + br[l, e]
                routed = routed + jnp.where((route == e)[:, None], ye, 0.0)
            h = jax.nn.relu(shared + routed + h)
        out = h @ Wo.T + bo
        return out.reshape(*x.shape[:-1], out.shape[-1])
    x = x + _L0_gnn_ref(_layernorm(x, axis=-1), adj, L0_gnn_W, L0_gnn_bW, L0_gnn_a1, L0_gnn_a2, L0_gnn_ab)
    x = x + _L0_ffn_ref(_layernorm(x, axis=-1)[None], L0_ffn_gate_w, L0_ffn_gate_b, L0_ffn_w1, L0_ffn_w2, L0_ffn_w3)[0]
    x = x + _L1_gnn_ref(_layernorm(x, axis=-1), adj, L1_gnn_W, L1_gnn_a_src, L1_gnn_a_dst)
    x = x + _L1_ffn_ref(_layernorm(x, axis=-1)[None], L1_ffn_route_id, L1_ffn_Wi, L1_ffn_bi, L1_ffn_Wr, L1_ffn_br, L1_ffn_Ws, L1_ffn_bs, L1_ffn_Wo, L1_ffn_bo)[0]
    return x

_drawn_inputs = setup_inputs


def setup_inputs(seed=0):
    import zlib

    import numpy as np

    out = dict(_drawn_inputs(seed))
    spreads = {'L0_ffn_gate_b': (0.0, 0.8), 'L1_ffn_bi': (0.0, 0.734), 'L1_ffn_bo': (0.0, 0.417)}
    factors = {'L0_gnn_bW': 6.025,
     'L0_ffn_gate_w': 8.0,
     'L0_ffn_w1': 8.0,
     'L0_ffn_w2': 8.0,
     'L0_ffn_w3': 8.0,
     'L1_ffn_Wr': 5.231,
     'L1_ffn_br': 25.871,
     'L1_ffn_Ws': 5.478,
     'L1_ffn_bs': 25.254,
     'L1_gnn_a_src': 3.612}
    for name, (base, spread) in spreads.items():
        noise = np.random.default_rng([zlib.crc32(name.encode()), seed]).standard_normal(out[name].shape)
        drawn = base * np.exp(spread * noise) if base else spread * noise
        out[name] = jnp.asarray(drawn.astype(out[name].dtype))
    for name, factor in factors.items():
        out[name] = (out[name] * factor).astype(out[name].dtype)
    return out
```

```python
from contextlib import ExitStack

import concourse.bass as bass
from concourse import mybir

F32 = mybir.dt.float32
BF16 = mybir.dt.bfloat16
I32 = mybir.dt.int32
U32 = mybir.dt.uint32
ALU = mybir.AluOpType
ACT = mybir.ActivationFunctionType
AX = mybir.AxisListType.X

P = 128
N = 1536
T = N // P
C = 128
H = 8
D = C // H
D1 = D + 1
E = 16
HID = 256
KC = HID // P
PARTS = 3
SLOT_TILES = 40
GROUPS = 64
GT = N // GROUPS
GPT = P // GT
TS = GPT * GT
FT = 26
BIG = 3.0e38
EPS = 1e-5
SLOPE = 0.2

K_ID, K_TRI, K_HM, K_IOTA, K_SLOT, K_FT = 0, 128, 256, 264, 280, 320
K_END = K_FT + FT

HS = 104
X_B, X_D, X_ONE = 0, PARTS * D1, 2 * PARTS * D1
R2 = 2 * D1
V1 = C + 1
VS = PARTS * V1 + 1
CW = 3 * P


def layernorm(nc, s, mem, name, sync=None, pool=None):
    xr, xn, xT, ident, st, mv, rstd, half, psum = mem
    stats, var, scale, normed, turned, taken = (s(f"{name}_{x}") for x in (
        "stats", "var", "scale", "normed", "turned", "taken"))
    clear = pool
    with nc.Block() as block:
        if sync is not None:
            @block.sync
            def _(sp):
                sync()

        @block.vector
        def _(dve):
            for t in range(T):
                nc.vector.bn_stats(st[:, t, :], xr[:, t, :]).then_inc(stats, 1)
            for t in range(T):
                dve.wait_ge(stats, t + 1)
                nc.vector.bn_aggr(mv[:, t, :], st[:, t, :]).then_inc(var, 1)
            dve.wait_ge(scale, 3)
            for t in range(T):
                nc.vector.tensor_scalar(xn[:, t, :], xr[:, t, :], mv[:, t, 0:1], rstd[:, t:t + 1],
                                        ALU.subtract, ALU.mult).then_inc(normed, 1)
            for q in range(T // 4):
                if q % 2 == 1:
                    dve.wait_ge(turned, q + 1)
                    nc.vector.tensor_copy(xT[:, 512 * q:512 * q + 512], psum[:, q, :]).then_inc(taken, 1)

        @block.gpsimd
        def _(pool):
            nc.gpsimd.memset(half[:], -0.5).then_inc(scale, 1)
            pool.wait_ge(var, T)
            nc.gpsimd.tensor_scalar(rstd[:], mv[:, :, 1], EPS, None, ALU.add).then_inc(scale, 1)
            pool.wait_ge(scale, 2)
            nc.gpsimd.tensor_tensor(rstd[:], rstd[:], half[:], ALU.pow).then_inc(scale, 1)
            if clear is not None:
                clear()

        @block.tensor
        def _(pe):
            for t in range(T):
                pe.wait_ge(normed, t + 1)
                last = nc.tensor.transpose(psum[:, t // 4, P * (t % 4):P * (t % 4) + P], xn[:, t, :], ident)
                if t % 4 == 3:
                    last.then_inc(turned, 1)

        @block.scalar
        def _(act):
            for q in range(0, T // 4, 2):
                act.wait_ge(turned, q + 1)
                nc.scalar.activation(xT[:, 512 * q:512 * q + 512], psum[:, q, :], ACT.Copy).then_inc(taken, 1)


def build(nc, x, adjT, gW, gb, ga1, ga2, gab, gate_w, gate_b, w1, w2, w3, uW, uas, uad,
          route, WiT, bi, WrT, WsT, WoT, bo, consts, out):
    with ExitStack() as ctx:
        def sb(name, shape, dt):
            return ctx.enter_context(nc.sbuf_tensor(name, shape, dt))

        def sem(name):
            return ctx.enter_context(nc.semaphore(name))

        arena = sb("arena", [P, 169 * 256], F32)

        def region(kb, shape, dt):
            n = 1
            for k in shape:
                n *= k
            words = n * (2 if dt == BF16 else 4) // 4
            a = arena[:, int(kb * 256):int(kb * 256) + words]
            if dt != F32:
                a = a.bitcast(dt)
            if len(shape) == 2:
                a = a.rearrange("p (a b) -> p a b", a=shape[0])
            if len(shape) == 3:
                a = a.rearrange("p (a b c) -> p a b c", a=shape[0], b=shape[1])
            return a

        def bump(kb, end):
            at = [kb * 1024]

            def small(shape, dt):
                t = region(at[0] / 1024, tuple(shape[1:]), dt)
                n = 2 if dt == BF16 else 4
                for k in shape[1:]:
                    n *= k
                at[0] += (n + 63) // 64 * 64
                assert at[0] <= end * 1024
                return t[0:shape[0]]
            return small

        psum = ctx.enter_context(nc.psum_tensor("psum", [P, 8, 512], F32))

        cst = sb("cst", [P, K_END], F32)
        xr = sb("xr", [P, T, C], F32)
        xn = sb("xn", [P, T, C], F32)
        xT = sb("xT", [P, N], F32)
        mT = sb("mT", [P, N], F32)
        hrow = sb("hrow", [P, T, C], F32)
        st = sb("st", [P, T, 6], F32)
        mv = sb("mv", [P, T, 2], F32)
        rstd = sb("rstd", [P, T], F32)
        half = sb("half", [P, T], F32)
        onesb = sb("onesb", [P, P], BF16)
        onesf = sb("onesf", [P, P], F32)
        trib = sb("trib", [P, P], BF16)
        ident = cst[:, K_ID:K_ID + P]
        ln_mem = (xr, xn, xT, ident, st, mv, rstd, half, psum)

        s_bcast = nc.dram_tensor("si_rows", (H, N), F32, kind="Internal").ap()
        slots_in = nc.dram_tensor("slots_in", (SLOT_TILES * P, C), F32, kind="Internal").ap()
        slots_out = nc.dram_tensor("slots_out", (SLOT_TILES * P, C), F32, kind="Internal").ap()

        uW_sb = sb("uW_sb", [P, C], F32)
        uas_sb, uad_sb = sb("uas_sb", [P, 1], F32), sb("uad_sb", [P, 1], F32)
        f1 = sb("f1", [P, 4, T], F32)
        nfd = sb("nfd", [P, T], F32)
        dg = sb("dg", [P, 2, T], F32)
        u_in, wall_in, l_in, cleared = sem("u_in"), sem("wall_in"), sem("l_in"), sem("cleared")
        zeroed, zero_set = sem("zeroed"), sem("zero_set")
        zero = sb("zero", [P, C], F32)
        x_in, weights_in, adj_in = sem("x_in"), sem("weights_in"), [sem("adj_in0"), sem("adj_in1")]

        M = region(0, (T, N), BF16)
        MB = region(36, (T, N), BF16)
        siB = region(72, (2, N), F32)
        S = region(84, (3, N), BF16)
        U = region(93, (4, N), BF16)
        stage = region(105, (2, N), I32)
        X = region(117, (T, H, HS), BF16)
        vv = region(136.5, (T * H, D1), F32)
        rr = region(143, (T * H, D1), F32)
        S34 = region(149.5, (T * H, R2), F32)
        YD = region(162.5, (T * H, D1), F32)

        early = bump(149.5, 162.5)
        gW_sb = early([P, C], F32)
        cols = sb("cols", [P, 8], F32)
        a16 = sb("a16", [P, 2 * H], F32)
        sc = sb("sc", [P, T, 2 * H], F32)
        gB = sb("gB", [P, 2 * H], F32)
        gcol = sb("gcol", [2 * H, 1], F32)
        gdiag = sb("gdiag", [2 * H, 2 * H], F32)
        srow = hrow[:, :, :].rearrange("p t c -> p (t c)")
        sjg = early([P, T, H], F32)
        nsj = sb("nsj", [P, T, H], F32)
        tA = early([P, T, H], F32)
        tC = early([P, T, H], F32)
        fB = sb("fB", [P, T * H], F32)
        fD = early([P, T * H], F32)
        fA = sb("fA", [P, T * H], F32)
        fC = sb("fC", [P, T * H], F32)
        deg = sb("deg", [P, T], F32)
        emp = sb("emp", [P, T], F32)
        hsum = sb("hsum", [P, C], F32)

        with nc.Block() as block:
            @block.sync
            def _(sp):
                sp.dma_start(xr[:], x.rearrange("(t p) c -> p t c", p=P)).then_inc(x_in, 16)
                sp.dma_start(cst[:], consts).then_inc(x_in, 16)
                for dst, src in ((gW_sb[:], gW), (cols[:, 0:1], gb), (cols[:, 1:2], ga1), (cols[:, 2:3], ga2),
                                 (cols[:, 3:4], gab.partition_broadcast(P))):
                    sp.dma_start(dst, src).then_inc(weights_in, 16)
                sp.wait_ge(zero_set, 1)
                sp.dma_start(slots_in.rearrange("(s p) c -> p s c", p=P),
                             zero[:].unsqueeze(1).to_broadcast([P, SLOT_TILES, C])).then_inc(zeroed, 16)
                sp.wait_ge(x_in, 32)
                sp.wait_ge(zeroed, 16)

            @block.gpsimd
            def _(pool):
                nc.gpsimd.memset(zero[:], 0.0).then_inc(zero_set, 1)

        layernorm(nc, sem, ln_mem, "ln1")

        m_made, mb_made, dch = sem("m_made"), sem("mb_made"), sem("p1_dch")
        a16_ready, hT_ps, hT_sb, hr_ps, sc_ps, sr_ps, g_ready, gB_ps, hsum_ps, sr_sb, sjg_ready, f_ready, hr_sb, \
            v_ready, split_a, split_d, si_out, hs_ready, sc_ready, ones_ready = (sem(f"p1_{n}") for n in (
                "a16", "hT_ps", "hT_sb", "hr_ps", "sc_ps", "sr_ps", "g", "gB_ps", "hsum_ps", "sr_sb", "sjg", "f",
                "hr_sb", "v", "split_a", "split_d", "si_out", "hs", "sc", "ones"))
        Xg = X.rearrange("p t h c -> p (t h) c")
        with nc.Block() as block:
            @block.sync
            def _(sp):
                for t in range(T):
                    if t >= 2:
                        sp.wait_ge(m_made, t - 1)
                        sp.wait_ge(mb_made, t - 1)
                    sp.dma_start(stage[:, t % 2, :], adjT[P * t:P * t + P, :]).then_inc(adj_in[t % 2], 16)
                    if t == 5:
                        sp.wait_ge(sr_sb, 3)
                        sp.dma_start(s_bcast, srow[0:H, :]).then_inc(si_out, 16)
                sp.wait_ge(si_out, 16)

            @block.gpsimd
            def _(pool):
                nc.gpsimd.memset(onesf[:], 1.0).then_inc(ones_ready, 1)
                nc.gpsimd.memset(onesb[:], 1.0).then_inc(ones_ready, 1)
                nc.gpsimd.memset(X[:, :, :, X_ONE:HS], 1.0).then_inc(ones_ready, 1)
                nc.gpsimd.tensor_copy(trib[:], cst[:, K_TRI:K_TRI + P]).then_inc(ones_ready, 1)
                for t in range(T):
                    pool.wait_ge(adj_in[t % 2], 16 * (t // 2 + 1))
                    nc.gpsimd.tensor_scalar(M[:, t, :], stage[:, t % 2, :], 0.0, 0.0, ALU.is_equal,
                                            ALU.is_equal).then_inc(m_made, 1)

            @block.tensor
            def _(pe):
                pe.wait_ge(weights_in, 80)
                for q in range(3):
                    nc.tensor.matmul(psum[:, q, :], gW_sb[:], xT[:, 512 * q:512 * q + 512], start=True,
                                     stop=True).then_inc(hT_ps, 1)
                pe.wait_ge(hT_sb, 3)
                pe.wait_ge(a16_ready, 2)
                for q in range(3):
                    nc.tensor.matmul(psum[0:2 * H, 3 + q, :], a16[:], mT[:, 512 * q:512 * q + 512], start=True,
                                     stop=True).then_inc(sr_ps, 1)
                for t in range(T):
                    last = nc.tensor.matmul(psum[:, 6, 2 * H * t:2 * H * t + 2 * H], mT[:, P * t:P * t + P],
                                            a16[:], start=(t == 0), stop=True, skip_group_check=True)
                last.then_inc(sc_ps, 1)
                for t in range(T):
                    last = nc.tensor.transpose(psum[:, t // 4, P * (t % 4):P * (t % 4) + P],
                                               mT[:, P * t:P * t + P], ident)
                    if t % 4 == 3:
                        last.then_inc(hr_ps, 1)
                pe.wait_ge(g_ready, 1)
                pe.wait_ge(ones_ready, 1)
                nc.tensor.matmul(psum[:, 7, 0:2 * H], onesf[0:2 * H, :], gdiag[:], start=True,
                                 stop=True).then_inc(gB_ps, 1)
                pe.wait_ge(hr_sb, 3)
                pe.wait_ge(sc_ready, 1)
                for t in range(T):
                    last = nc.tensor.matmul(psum[:, 6, 0:C], onesf[:], hrow[:, t, :], start=(t == 0),
                                            stop=(t == T - 1))
                last.then_inc(hsum_ps, 1)

            @block.scalar
            def _(act):
                for q in range(3):
                    act.wait_ge(hT_ps, q + 1)
                    nc.scalar.activation(mT[:, 512 * q:512 * q + 512], psum[:, q, :], ACT.Identity,
                                         bias=cols[:, 0:1]).then_inc(hT_sb, 1)
                for q in range(3):
                    act.wait_ge(sr_ps, q + 1)
                    nc.scalar.activation(srow[0:2 * H, 512 * q:512 * q + 512], psum[0:2 * H, 3 + q, :],
                                         ACT.Identity, bias=cols[0:2 * H, 3:4]).then_inc(sr_sb, 1)
                act.wait_ge(si_out, 16)
                act.wait_ge(dch, 1)
                for q in range(3):
                    act.wait_ge(hr_ps, q + 1)
                    nc.scalar.activation(hrow[:, 4 * q:4 * q + 4, :].rearrange("p t c -> p (t c)"), psum[:, q, :],
                                         ACT.Copy).then_inc(hr_sb, 1)
                act.wait_ge(sjg_ready, 3)
                flat = lambda a: a[:, :, :].rearrange("p t h -> p (t h)")
                nc.scalar.activation(fD[:], flat(sjg), ACT.Exp, scale=SLOPE).then_inc(f_ready, 1)
                nc.scalar.activation(fB[:], flat(sjg), ACT.Exp).then_inc(f_ready, 1)
                nc.scalar.activation(fA[:], flat(tA), ACT.Exp).then_inc(f_ready, 1)
                nc.scalar.activation(fC[:], flat(tC), ACT.Exp).then_inc(f_ready, 1)
                for k, at in enumerate((X_D, X_B)):
                    act.wait_ge(v_ready, 2 * (k + 1))
                    nc.scalar.activation(Xg[:, :, at:at + D1], vv, ACT.Copy).then_inc(split_a, 1)
                    act.wait_ge(split_d, 2 * k + 1)
                    nc.scalar.activation(Xg[:, :, at + D1:at + 2 * D1], rr, ACT.Copy).then_inc(split_a, 1)
                act.wait_ge(hsum_ps, 1)
                nc.scalar.activation(hsum[:], psum[:, 6, 0:C], ACT.Copy).then_inc(hs_ready, 1)

            @block.vector
            def _(dve):
                def masks(a, b):
                    for t in range(a, b):
                        dve.wait_ge(adj_in[t % 2], 16 * (t // 2 + 1))
                        nc.vector.tensor_scalar(MB[:, t, :], stage[:, t % 2, :], 0.0, BIG, ALU.is_equal,
                                                ALU.mult).then_inc(mb_made, 1)

                dve.wait_ge(weights_in, 80)
                for k in range(2):
                    nc.vector.tensor_scalar(a16[:, H * k:H * k + H], cst[:, K_HM:K_HM + H], cols[:, 1 + k:2 + k],
                                            None, ALU.mult).then_inc(a16_ready, 1)
                masks(0, 2)
                dve.wait_ge(sr_sb, 3)
                nc.vector.tensor_reduce(gcol[:], srow[0:2 * H, :], AX, ALU.max).then_inc(dch, 1)
                dve.wait_ge(dch, 1)
                nc.vector.tensor_scalar(gdiag[:], cst[0:2 * H, K_ID:K_ID + 2 * H], gcol[:], None,
                                        ALU.mult).then_inc(g_ready, 1)
                dve.wait_ge(sc_ps, 1)
                nc.vector.tensor_copy(sc[:, :, :].rearrange("p t h -> p (t h)"),
                                      psum[:, 6, 0:T * 2 * H]).then_inc(sc_ready, 1)
                dve.wait_ge(gB_ps, 1)
                nc.vector.tensor_copy(gB[:], psum[:, 7, 0:2 * H]).then_inc(dch, 1)
                dve.wait_ge(dch, 2)
                dve.wait_ge(sc_ready, 1)
                g3 = gB[:, H:2 * H].unsqueeze(1).to_broadcast([P, T, H])
                nc.vector.tensor_tensor(sjg[:], sc[:, :, H:2 * H], g3, ALU.subtract).then_inc(dch, 1)
                nc.vector.tensor_tensor(tA[:], sc[:, :, 0:H], g3, ALU.add).then_inc(dch, 1)
                nc.vector.tensor_scalar(nsj[:], sc[:, :, H:2 * H], -1.0, None, ALU.mult).then_inc(dch, 1)
                dve.wait_ge(dch, 5)
                nc.vector.tensor_scalar(sjg[:], sjg[:], cols[:, 3:4], None, ALU.add).then_inc(sjg_ready, 1)
                nc.vector.tensor_scalar(tC[:], tA[:], SLOPE - 1.0, 0.0, ALU.mult, ALU.min).then_inc(sjg_ready, 1)
                dve.wait_ge(sjg_ready, 2)
                nc.vector.tensor_scalar(tA[:], tA[:], 1.0 - SLOPE, 0.0, ALU.mult, ALU.min).then_inc(sjg_ready, 1)
                masks(2, 4)
                dve.wait_ge(hr_sb, 3)
                for k, (f, at) in enumerate(((fD, X_D), (fB, X_B))):
                    dve.wait_ge(f_ready, k + 1)
                    if k == 1:
                        dve.wait_ge(split_d, 1)
                        dve.wait_ge(split_a, 1)
                    nc.vector.tensor_tensor(vv[:, :, 0:D], hrow[:, :, :].rearrange("p t (h d) -> p (t h) d", h=H),
                                            f[:].unsqueeze(2).to_broadcast([P, T * H, D]),
                                            ALU.mult).then_inc(v_ready, 1)
                    nc.vector.tensor_copy(vv[:, :, D], f[:]).then_inc(v_ready, 1)
                    dve.wait_ge(v_ready, 2 * (k + 1))
                    dve.wait_ge(split_a, 2 * k + 1)
                    if k == 1:
                        dve.wait_ge(split_d, 2)
                    nc.vector.tensor_tensor(rr, vv, Xg[:, :, at:at + D1], ALU.subtract).then_inc(split_d, 1)
                    masks(4 + 2 * k, 6 + 2 * k)
                    dve.wait_ge(split_a, 2 * k + 2)
                    dve.wait_ge(split_d, 2 * k + 1)
                    nc.vector.tensor_tensor(Xg[:, :, at + 2 * D1:at + 3 * D1], rr, Xg[:, :, at + D1:at + 2 * D1],
                                            ALU.subtract).then_inc(split_d, 1)
                masks(8, T)

        ACT_TILES = [1, 2, 3, 5, 6, 7, 9, 10, 11]
        NA = len(ACT_TILES)
        si_in = [sem("si_in0"), sem("si_in1")]
        s_ready, u_ready, u_free, acc_full, acc_free, y_full, y_free = (sem(f"at_{n}") for n in (
            "s_ready", "u_ready", "u_free", "acc_full", "acc_free", "y_full", "y_free"))
        Sv = S34.rearrange("p (t h) c -> p t h c", h=H)
        YDv = YD.rearrange("p (t h) c -> p t h c", h=H)
        U0 = 2 * T
        MQ = T // (H // 2)
        with nc.Block() as block:
            @block.sync
            def _(sp):
                with sp.Fori(0, H // 2) as i:
                    for hh in range(2):
                        sp.wait_ge(u_ready, 2 * T * i + (U0 + T * (hh - 1)))
                        sp.dma_start(siB[:, hh, :], s_bcast[bass.ds(2 * i + hh, 1), :].squeeze(0)
                                     .partition_broadcast(P)).then_inc(si_in[hh], 16)

            @block.scalar
            def _(act):
                nc.scalar.preload_act_table(ACT.Exp)
                with act.Fori(0, H // 2) as i:
                    for hh in range(2):
                        act.wait_ge(si_in[hh], 16 * i + 16)
                        for k, t in enumerate(ACT_TILES):
                            back = ACT_TILES[k - 3] + 1 if k >= 3 else ACT_TILES[k - 3 + NA] + 1 - T
                            act.wait_ge(u_ready, T * (2 * i) + (U0 + T * hh + back))
                            nc.scalar.activation(S[:, k % 3, :], siB[:, hh, :], ACT.Identity,
                                                 bias=sc[:, t, bass.ds(2 * i + hh + H, 1)]).then_inc(s_ready, 1)

            @block.vector
            def _(dve):
                dve.sem_inc(u_ready, U0)
                dve.sem_inc(acc_free, 2)
                dve.sem_inc(y_free, 1)

                def take_y(i, q):
                    dve.wait_ge(y_full, MQ * i + q + 1)
                    yb = psum[:, 6, 0:H * 52].rearrange("p (h c) -> p h c", h=H)
                    m = MQ * i + q
                    nc.vector.tensor_reduce(
                        YDv[:, bass.ds(m, 1), :, :].squeeze(1),
                        yb[:, :, 0:PARTS * D1].rearrange("p h (k c) -> p h c k", k=PARTS), AX,
                        ALU.add)
                    nc.vector.tensor_copy(deg[:, bass.ds(m, 1)], yb[:, 0, 51:52]).then_inc(y_free, 1)

                def take_head(i, hh):
                    dve.wait_ge(acc_full, 2 * i + hh + 1)
                    for b in range(3):
                        last = nc.vector.tensor_reduce(
                            Sv[:, 4 * b:4 * b + 4, bass.ds(2 * i + hh, 1), :].squeeze(2)
                            .rearrange("p t (f c) -> p t f c", f=2)[:, :, 0, :],
                            psum[:, 3 * hh + b, :].rearrange("p (t c) -> p t c", t=4)[:, :, 0:PARTS * D1]
                            .rearrange("p t (k c) -> p t c k", k=PARTS), AX, ALU.add)
                        last = nc.vector.tensor_reduce(
                            Sv[:, 4 * b:4 * b + 4, bass.ds(2 * i + hh, 1), :].squeeze(2)
                            .rearrange("p t (f c) -> p t f c", f=2)[:, :, 1, :],
                            psum[:, 3 * hh + b, :].rearrange("p (t c) -> p t c", t=4)[:, :, X_D:X_D + PARTS * D1]
                            .rearrange("p t (k c) -> p t c k", k=PARTS), AX, ALU.add)
                    last.then_inc(acc_free, 1)

                with dve.Fori(0, H // 2) as i:
                    for hh in range(2):
                        dve.wait_ge(si_in[hh], 16 * i + 16)
                        for t in range(T):
                            dve.wait_ge(u_free, 2 * T * i + T * hh + t + 1)
                            if t in ACT_TILES:
                                k = ACT_TILES.index(t)
                                dve.wait_ge(s_ready, 2 * NA * i + NA * hh + k + 1)
                                nc.vector.tensor_tensor(U[:, t % 4, :], S[:, k % 3, :], MB[:, t, :],
                                                        ALU.is_gt).then_inc(u_ready, 1)
                            else:
                                nc.vector.scalar_tensor_tensor(
                                    U[:, t % 4, :], siB[:, hh, :], nsj[:, t, bass.ds(2 * i + hh, 1)], M[:, t, :],
                                    ALU.is_gt, ALU.mult).then_inc(u_ready, 1)
                            if hh == 0 and t in (5, 9):
                                take_y(i, (5, 9).index(t))
                            if hh == 1 and t == 1:
                                take_y(i, 2)
                            if hh == 1 and t == 4:
                                take_head(i, 0)
                    take_head(i, 1)

            @block.tensor
            def _(pe):
                pe.sem_inc(u_free, 4)
                with pe.Fori(0, H // 2) as i:
                    for hh in range(2):
                        pe.wait_ge(acc_free, 2 * i + hh + 1)
                        for t in range(T):
                            pe.wait_ge(u_ready, 2 * T * i + (U0 + T * hh + t + 1))
                            for b in range(T):
                                last = nc.tensor.matmul(
                                    psum[:, 3 * hh + b // 4, P * (b % 4):P * (b % 4) + 2 * PARTS * D1],
                                    U[:, t % 4, P * b:P * b + P],
                                    X[:, t, bass.ds(2 * i + hh, 1), 0:2 * PARTS * D1].squeeze(1),
                                    start=(t == 0 and b % 4 == 0), stop=(t == T - 1), skip_group_check=True)
                            last.then_inc(u_free, 1)
                            if (hh, t) in ((0, 1), (0, 5), (0, 9)):
                                q = (1, 5, 9).index(t)
                                pe.wait_ge(y_free, MQ * i + q + 1)
                                for j in range(T):
                                    y = nc.tensor.matmul(psum[:, 6, 0:H * 52],
                                                         M[:, j, bass.ds((MQ * i + q) * P, P)],
                                                         X[:, j, :, X_D:X_D + 52], start=(j == 0),
                                                         stop=(j == T - 1))
                                y.then_inc(y_full, 1)
                        nc.tensor.matmul(psum[:, 7, 0:2], onesb[:], onesb[:, 0:2], start=True,
                                         stop=True).then_inc(acc_full, 1)

        num = vv
        tmp = rr
        c2 = sem("p2_chain")
        num_ready, elu_e, xd = sem("p2_num"), sem("p2_elu"), sem("p2_x")
        chain = [0]
        agg = xT[:, :].rearrange("p (t c) -> p t c", t=T)
        expo = mT[:, :].rearrange("p (t c) -> p t c", t=T)
        with nc.Block() as block:
            @block.vector
            def _(dve):
                def link(ins):
                    chain[0] += 1
                    ins.then_inc(c2, 1)
                    dve.wait_ge(c2, chain[0])

                wide = lambda f: f[:].unsqueeze(2).to_broadcast([P, T * H, D1])
                link(nc.vector.tensor_tensor(num, YD, S34[:, :, D1:R2], ALU.subtract))
                link(nc.vector.tensor_tensor(num, num, wide(fC), ALU.mult))
                link(nc.vector.tensor_tensor(tmp, S34[:, :, 0:D1], wide(fA), ALU.mult))
                link(nc.vector.tensor_tensor(num, num, tmp, ALU.add))
                link(nc.vector.tensor_scalar(emp[:], deg[:], 0.0, None, ALU.is_equal))
                den = fB
                link(nc.vector.scalar_tensor_tensor(
                    den[:].rearrange("p (t h) -> p t h", h=H), emp[:].unsqueeze(2).to_broadcast([P, T, H]),
                    float(N), num[:, :, D].rearrange("p (t h) -> p t h", h=H), ALU.mult, ALU.add))
                link(nc.vector.reciprocal(den[:], den[:]))
                for t in range(T):
                    last = nc.vector.scalar_tensor_tensor(
                        agg[:, t, :].rearrange("p (h d) -> p h d", h=H),
                        hsum[:].rearrange("p (h d) -> p h d", h=H), emp[:, t:t + 1],
                        num[:, H * t:H * t + H, 0:D], ALU.mult, ALU.add)
                link(last)
                link(nc.vector.tensor_tensor(agg.rearrange("p t (h d) -> p (t h) d", h=H),
                                             agg.rearrange("p t (h d) -> p (t h) d", h=H),
                                             den[:].unsqueeze(2).to_broadcast([P, T * H, D]), ALU.mult))
                link(nc.vector.tensor_tensor(agg, agg, xn[:], ALU.add))
                nc.vector.tensor_scalar(expo, agg, 0.0, None, ALU.min).then_inc(num_ready, 1)
                link(nc.vector.tensor_scalar(agg, agg, 0.0, -1.0, ALU.max, ALU.add))
                link(nc.vector.tensor_tensor(xr[:], xr[:], agg, ALU.add))
                dve.wait_ge(elu_e, 1)
                link(nc.vector.tensor_tensor(xr[:], xr[:], hrow[:], ALU.add))

            @block.scalar
            def _(act):
                act.wait_ge(num_ready, 1)
                nc.scalar.activation(hrow[:], expo, ACT.Exp).then_inc(elu_e, 1)
        layernorm(nc, sem, ln_mem, "ln2")

        W12 = region(0, (E, 2 * HID), F32)
        W3 = region(32, (E, KC, C), F32)
        stage2 = region(48, (2, N), I32)
        M2 = region(72, (T, N), BF16)
        yall = region(144, (SLOT_TILES, C), F32)
        small = bump(120, 132)
        gates_w = small([P, E], F32)
        gates_b = small([P, E], F32)
        lg = small([P, T, E], F32)
        mx = small([P, T, 8], F32)
        ix = small([P, T, 8], U32)
        ixf = small([P, T, 2], F32)
        OH = small([P, 2, T, E], BF16)
        OHs = small([P, T, E], BF16)
        cnt = small([P, E], F32)
        over = small([P, E, T + 1], F32)
        padded = small([P, E], F32)
        ends = small([P, E], F32)
        rk = small([P, T, E], F32)
        rk2 = small([P, 2, T, E], F32)
        posf = small([P, 2, T], F32)
        pos = sb("pos", [P, 2, T], I32)
        wts = sb("wts", [P, 2, T], F32)
        e2 = small([P, T], F32)
        se = small([1, SLOT_TILES, E], F32)
        ef = small([1, SLOT_TILES], F32)
        eslot = sb("eslot", [1, SLOT_TILES], I32)
        route_i = small([GROUPS, 1], I32)
        route_f = small([GROUPS, 1], F32)
        OHg = small([GROUPS, E], BF16)
        gcnt = small([GROUPS, E], F32)
        gover = small([GROUPS, E, GROUPS // GPT + 1], F32)
        gpad = small([GROUPS, E], F32)
        gend = small([GROUPS, E], F32)
        grk = small([GROUPS, E], F32)
        gpos = small([GROUPS, 1], F32)
        gpos_i = sb("gpos_i", [1, GROUPS], I32)
        gef = small([1, FT], F32)
        ge = sb("ge", [1, FT], I32)
        gw_in, w12_in, w3_in, scattered, c3 = sem("gw_in"), sem("w12_in"), sem("w3_in"), sem("scattered"), sem("p3_c")
        lg_ps, oh_ready, rk_ps, pos_ready, d_e2, e2_ready, g_oh, g_ps, g_col, g_row = (sem(f"p3_{n}") for n in (
            "lg_ps", "oh", "rk_ps", "pos", "d", "e2", "g_oh", "g_ps", "g_col", "g_row"))
        with nc.Block() as block:
            @block.sync
            def _(sp):
                for dst, src in ((gates_w[:], gate_w), (gates_b[:], gate_b.squeeze(0).partition_broadcast(P)),
                                 (route_i[:], route)):
                    sp.dma_start(dst, src).then_inc(gw_in, 16)
                sp.dma_start(W12[:, :, 0:HID], w1).then_inc(w12_in, 16)
                sp.dma_start(W12[:, :, HID:2 * HID], w2).then_inc(w12_in, 16)
                sp.dma_start(W3.rearrange("p e k c -> p (e k c)"), w3.rearrange("p e k c -> p (e k c)"))\
                    .then_inc(w3_in, 16)

            @block.tensor
            def _(pe):
                pe.wait_ge(gw_in, 48)
                for t in range(T):
                    last = nc.tensor.matmul(psum[:, 0, E * t:E * t + E], xT[:, P * t:P * t + P], gates_w[:],
                                            start=(t == 0), stop=True, skip_group_check=True)
                last.then_inc(lg_ps, 1)
                pe.wait_ge(g_oh, 1)
                nc.tensor.matmul(psum[0:GROUPS, 3, 0:E], trib[0:GROUPS, 0:GROUPS], OHg[:], start=True, stop=True)
                nc.tensor.matmul(psum[0:GROUPS, 4, 0:E], onesb[0:GROUPS, 0:GROUPS], OHg[:], start=True,
                                 stop=True).then_inc(g_ps, 1)
                pe.wait_ge(oh_ready, 1)
                nc.tensor.matmul(psum[:, 1, 0:T * E], trib[:], OHs[:, :, :].rearrange("p t e -> p (t e)"),
                                 start=True, stop=False, skip_group_check=True)
                for d in range(1, T):
                    nc.tensor.matmul(psum[:, 1, d * E:T * E], onesb[:],
                                     OHs[:, 0:T - d, :].rearrange("p t e -> p (t e)"), start=False,
                                     stop=(d == T - 1), skip_group_check=True)
                for t in range(T):
                    last = nc.tensor.matmul(psum[:, 2, 0:E], onesb[:], OHs[:, t, :], start=(t == 0),
                                            stop=(t == T - 1))
                last.then_inc(rk_ps, 1)
                pe.wait_ge(g_col, 1)
                nc.tensor.matmul(psum[0:1, 5, 0:GROUPS], gpos[:], cst[0:GROUPS, K_ID:K_ID + GROUPS], start=True,
                                 stop=True).then_inc(g_row, 1)

            @block.scalar
            def _(act):
                act.wait_ge(d_e2, 1)
                nc.scalar.activation(e2[:], e2[:], ACT.Exp).then_inc(e2_ready, 1)

            @block.vector
            def _(dve):
                n = [0]

                def link(ins):
                    n[0] += 1
                    ins.then_inc(c3, 1)
                    dve.wait_ge(c3, n[0])

                dve.wait_ge(gw_in, 48)
                link(nc.vector.tensor_copy(route_f[:], route_i[:]))
                nc.vector.tensor_scalar(OHg[:], cst[0:GROUPS, K_IOTA:K_IOTA + E], route_f[:], None,
                                        ALU.is_equal).then_inc(g_oh, 1)
                dve.wait_ge(lg_ps, 1)
                link(nc.vector.tensor_tensor(lg[:], psum[:, 0, 0:T * E].rearrange("p (t e) -> p t e", t=T),
                                             gates_b[:].unsqueeze(1).to_broadcast([P, T, E]), ALU.add))
                for t in range(T):
                    last = nc.vector.max(mx[:, t, :], lg[:, t, :])
                link(last)
                for t in range(T):
                    last = nc.vector.max_index(ix[:, t, :], mx[:, t, :], lg[:, t, :])
                link(last)
                link(nc.vector.tensor_copy(ixf[:], ix[:, :, 0:2]))
                iota = cst[:, K_IOTA:K_IOTA + E].unsqueeze(1).to_broadcast([P, T, E])
                for k in range(2):
                    link(nc.vector.tensor_tensor(OH[:, k, :, :], iota,
                                                 ixf[:, :, k:k + 1].to_broadcast([P, T, E]), ALU.is_equal))
                nc.vector.tensor_tensor(OHs[:], OH[:, 0, :, :], OH[:, 1, :, :], ALU.add).then_inc(oh_ready, 1)
                nc.vector.tensor_tensor(e2[:], mx[:, :, 1], mx[:, :, 0], ALU.subtract).then_inc(d_e2, 1)
                dve.wait_ge(rk_ps, 1)
                link(nc.vector.tensor_copy(cnt[:], psum[:, 2, 0:E]))
                link(nc.vector.tensor_tensor(over[:], cnt[:].unsqueeze(2).to_broadcast([P, E, T + 1]),
                                             cst[:, K_SLOT:K_SLOT + T + 1].unsqueeze(1)
                                             .to_broadcast([P, E, T + 1]), ALU.is_gt))
                link(nc.vector.tensor_reduce(padded[:], over[:], AX, ALU.add))
                link(nc.vector.tensor_scalar(padded[:], padded[:], float(P), None, ALU.mult))
                link(nc.vector.tensor_tensor_scan(ends[:], onesf[:, 0:E], padded[:], 0.0, ALU.mult, ALU.add))
                link(nc.vector.tensor_tensor(padded[:], ends[:], padded[:], ALU.subtract))
                link(nc.vector.tensor_tensor(rk[:], psum[:, 1, 0:T * E].rearrange("p (t e) -> p t e", t=T),
                                             padded[:].unsqueeze(1).to_broadcast([P, T, E]), ALU.add))
                for k in range(2):
                    link(nc.vector.tensor_tensor(rk2[:, k, :, :], OH[:, k, :, :], rk[:], ALU.mult))
                link(nc.vector.tensor_reduce(posf[:, :, :].rearrange("p k t -> p (k t)"),
                                             rk2[:, :, :, :].rearrange("p k t e -> p (k t) e"), AX, ALU.add))
                nc.vector.tensor_copy(pos[:], posf[:]).then_inc(pos_ready, 1)
                link(nc.vector.tensor_tensor(se[:], ends[0:1, :].unsqueeze(1).to_broadcast([1, SLOT_TILES, E]),
                                             cst[0:1, K_SLOT:K_SLOT + SLOT_TILES].unsqueeze(2)
                                             .to_broadcast([1, SLOT_TILES, E]), ALU.is_le))
                link(nc.vector.tensor_reduce(ef[:], se[:], AX, ALU.add))
                link(nc.vector.tensor_scalar(eslot[:], ef[:], float(E - 1), None, ALU.min))
                dve.wait_ge(e2_ready, 1)
                link(nc.vector.tensor_scalar(wts[:, 0, :], e2[:], 1.0, None, ALU.add))
                link(nc.vector.reciprocal(wts[:, 0, :], wts[:, 0, :]))
                link(nc.vector.tensor_tensor(wts[:, 1, :], wts[:, 0, :], e2[:], ALU.mult))
                dve.wait_ge(g_ps, 1)
                link(nc.vector.tensor_scalar(gcnt[:], psum[0:GROUPS, 4, 0:E], float(GT), None, ALU.mult))
                nk = GROUPS // GPT + 1
                link(nc.vector.tensor_tensor(gover[:], gcnt[:].unsqueeze(2).to_broadcast([GROUPS, E, nk]),
                                             cst[0:GROUPS, K_FT:K_FT + nk].unsqueeze(1)
                                             .to_broadcast([GROUPS, E, nk]), ALU.is_gt))
                link(nc.vector.tensor_reduce(gpad[:], gover[:], AX, ALU.add))
                link(nc.vector.tensor_scalar(gpad[:], gpad[:], float(TS), None, ALU.mult))
                link(nc.vector.tensor_tensor_scan(gend[:], onesf[0:GROUPS, 0:E], gpad[:], 0.0, ALU.mult, ALU.add))
                link(nc.vector.tensor_tensor(gpad[:], gend[:], gpad[:], ALU.subtract))
                link(nc.vector.scalar_tensor_tensor(grk[:], psum[0:GROUPS, 3, 0:E], float(GT), gpad[:], ALU.mult,
                                                    ALU.add))
                link(nc.vector.tensor_tensor(grk[:], grk[:], OHg[:], ALU.mult))
                nc.vector.tensor_reduce(gpos[:], grk[:], AX, ALU.add).then_inc(g_col, 1)
                link(nc.vector.tensor_tensor(se[:, 0:FT, :], gend[0:1, :].unsqueeze(1).to_broadcast([1, FT, E]),
                                             cst[0:1, K_FT:K_FT + FT].unsqueeze(2).to_broadcast([1, FT, E]),
                                             ALU.is_le))
                link(nc.vector.tensor_reduce(gef[:], se[:, 0:FT, :], AX, ALU.add))
                link(nc.vector.tensor_scalar(ge[:], gef[:], float(E - 1), None, ALU.min))
                dve.wait_ge(g_row, 1)
                link(nc.vector.tensor_copy(gpos_i[:], psum[0:1, 5, 0:GROUPS]))

            @block.gpsimd
            def _(pool):
                pool.wait_ge(pos_ready, 1)
                for t in range(T):
                    for k in range(2):
                        nc.gpsimd.indirect_dma_start(
                            slots_in, bass.IndirectOffsetOnAxis(ap=pos[:, k, t:t + 1].bitcast(U32), axis=0),
                            xn[:, t, :], None).then_inc(scattered, 16)
                pool.wait_ge(scattered, 16 * 2 * T)

        L = 8
        xs = region(60, (L, P), F32)
        xsT = region(64, (2, P), F32)
        sil = region(65, (2, HID), F32)
        hid = region(67, (2, HID), F32)
        hT = region(69, (2, HID), F32)
        xs_in = [sem("xs_in0"), sem("xs_in1")]
        a_done, b_done, cc_done, d_done, xt_ready, sil_ready, hid_ready, ht_ready, y_ready, y_out, m2_made = (
            sem(f"p4_{n}") for n in ("a", "b", "c", "d", "xt", "sil", "hid", "ht", "y", "y_out", "m2"))
        adj2_in = [sem("adj2_in0"), sem("adj2_in1")]
        CR = 2
        slots_v = slots_in.rearrange("(s p) c -> p s c", p=P)
        out_v = slots_out.rearrange("(s p) c -> p s c", p=P)
        with nc.Block() as block:
            @block.sync
            def _(sp):
                with sp.Fori(0, SLOT_TILES // L) as i:
                    for half_ in range(2):
                        sp.wait_ge(a_done, i * L + (4 * half_ + 4))
                        sp.dma_start(xs[:, 4 * half_:4 * half_ + 4, :],
                                     slots_v[:, bass.ds(i * L + 4 * half_, 4), :]).then_inc(xs_in[half_], 16)

            @block.gpsimd
            def _(pool):
                for t in range(T):
                    if t >= 2:
                        pool.wait_ge(m2_made, t - 1)
                    pool.dma_start(stage2[:, t % 2, :], adjT[P * t:P * t + P, :]).then_inc(adj2_in[t % 2], 16)
                    if t >= 1:
                        pool.wait_ge(adj2_in[(t - 1) % 2], 16 * ((t - 1) // 2 + 1))
                        nc.gpsimd.tensor_scalar(M2[:, t - 1, :], stage2[:, (t - 1) % 2, :], 0.0, None,
                                                ALU.is_gt).then_inc(m2_made, 1)
                pool.wait_ge(adj2_in[(T - 1) % 2], 16 * ((T - 1) // 2 + 1))
                nc.gpsimd.tensor_scalar(M2[:, T - 1, :], stage2[:, (T - 1) % 2, :], 0.0, None,
                                        ALU.is_gt).then_inc(m2_made, 1)
                for j in range(SLOT_TILES // 4):
                    pool.wait_ge(y_ready, CR + 4 * j + 4)
                    pool.dma_start(out_v[:, 4 * j:4 * j + 4, :], yall[:, 4 * j:4 * j + 4, :]).then_inc(y_out, 16)
                pool.wait_ge(y_out, 16 * SLOT_TILES // 4)

            @block.tensor
            def _(pe):
                pe.sem_inc(a_done, L)
                pe.sem_inc(b_done, CR)
                pe.sem_inc(cc_done, CR)
                pe.sem_inc(d_done, CR)
                pe.wait_ge(w12_in, 32)
                pe.wait_ge(w3_in, 16)
                with pe.Fori(0, SLOT_TILES // L) as i:
                    _, ex = nc.values_load_multi_w_load_instructions(
                        eslot[0:1, bass.ds(i * L, L)], engines=[mybir.EngineType.PE], min_val=0, max_val=E - 1,
                        skip_runtime_bounds_check_because="clamped when made")
                    for k in range(L + 3):
                        if k < L:
                            pe.wait_ge(xs_in[k // 4], 16 * i + 16)
                            pe.wait_ge(xt_ready, L * i + k + 1)
                            nc.tensor.transpose(psum[:, k % 2, 0:P], xs[:, k, :], ident).then_inc(a_done, 1)
                        if 1 <= k < L + 1:
                            q = k - 1
                            pe.wait_ge(xt_ready, L * i + (CR + q + 1))
                            pe.wait_ge(hid_ready, L * i + q + 1)
                            nc.tensor.matmul(psum[:, 2 + q % 2, :], xsT[:, q % 2, :],
                                             W12[:, bass.ds(ex[q], 1), :].squeeze(1), start=True,
                                             stop=True).then_inc(b_done, 1)
                        if 2 <= k < L + 2:
                            q = k - 2
                            pe.wait_ge(hid_ready, L * i + (CR + q + 1))
                            pe.wait_ge(ht_ready, L * i + q + 1)
                            for m in range(KC):
                                last = nc.tensor.transpose(psum[:, 4 + q % 2, P * m:P * m + P],
                                                           hid[:, q % 2, P * m:P * m + P], ident)
                            last.then_inc(cc_done, 1)
                        if 3 <= k:
                            q = k - 3
                            pe.wait_ge(ht_ready, L * i + (CR + q + 1))
                            pe.wait_ge(y_ready, L * i + q + 1)
                            for m in range(KC):
                                last = nc.tensor.matmul(psum[:, 6 + q % 2, 0:C], hT[:, q % 2, P * m:P * m + P],
                                                        W3[:, bass.ds(ex[q], 1), m, :].squeeze(1), start=(m == 0),
                                                        stop=(m == KC - 1))
                            last.then_inc(d_done, 1)

            @block.scalar
            def _(act):
                nc.scalar.preload_act_table(ACT.Silu)
                act.sem_inc(xt_ready, CR)
                act.sem_inc(ht_ready, CR)
                with act.Fori(0, SLOT_TILES // L) as i:
                    for k in range(L + 2):
                        if k < L:
                            act.wait_ge(a_done, L * i + (L + k + 1))
                            act.wait_ge(b_done, L * i + k + 1)
                            nc.scalar.activation(xsT[:, k % 2, :], psum[:, k % 2, 0:P], ACT.Copy)\
                                .then_inc(xt_ready, 1)
                        if 1 <= k < L + 1:
                            q = k - 1
                            act.wait_ge(b_done, L * i + (CR + q + 1))
                            act.wait_ge(hid_ready, L * i + q + 1)
                            nc.scalar.activation(sil[:, q % 2, :], psum[:, 2 + q % 2, 0:HID], ACT.Silu)\
                                .then_inc(sil_ready, 1)
                        if 2 <= k:
                            q = k - 2
                            act.wait_ge(cc_done, L * i + (CR + q + 1))
                            act.wait_ge(d_done, L * i + q + 1)
                            nc.scalar.activation(hT[:, q % 2, :], psum[:, 4 + q % 2, 0:HID], ACT.Copy)\
                                .then_inc(ht_ready, 1)

            @block.vector
            def _(dve):
                dve.sem_inc(hid_ready, CR)
                dve.sem_inc(y_ready, CR)
                with dve.Fori(0, SLOT_TILES // L) as i:
                    for k in range(L + 2):
                        if k < L:
                            dve.wait_ge(sil_ready, L * i + k + 1)
                            dve.wait_ge(cc_done, L * i + k + 1)
                            nc.vector.tensor_tensor(hid[:, k % 2, :], psum[:, 2 + k % 2, HID:2 * HID],
                                                    sil[:, k % 2, :], ALU.mult).then_inc(hid_ready, 1)
                        if 2 <= k:
                            q = k - 2
                            dve.wait_ge(d_done, L * i + (CR + q + 1))
                            nc.vector.tensor_copy(yall[:, bass.ds(L * i + q, 1), :].squeeze(1),
                                                  psum[:, 6 + q % 2, 0:C]).then_inc(y_ready, 1)

        back = region(108, (2, T, C), F32)
        got = [sem(f"got{q}") for q in range(3)]
        comb = sem("p5_comb")
        with nc.Block() as block:
            @block.gpsimd
            def _(pool):
                for t in range(T):
                    for k in range(2):
                        nc.gpsimd.indirect_dma_start(
                            back[:, k, t, :], None, slots_out,
                            bass.IndirectOffsetOnAxis(ap=pos[:, k, t:t + 1].bitcast(U32), axis=0))\
                            .then_inc(got[t // 4], 16)

            @block.vector
            def _(dve):
                for t in range(T):
                    dve.wait_ge(got[t // 4], 16 * 8)
                    nc.vector.scalar_tensor_tensor(xr[:, t, :], back[:, 0, t, :], wts[:, 0, t:t + 1], xr[:, t, :],
                                                   ALU.mult, ALU.add).then_inc(comb, 1)
                    dve.wait_ge(comb, 2 * t + 1)
                    nc.vector.scalar_tensor_tensor(xr[:, t, :], back[:, 1, t, :], wts[:, 1, t:t + 1], xr[:, t, :],
                                                   ALU.mult, ALU.add).then_inc(comb, 1)
        def preload_attention2():
            for dst, src in ((uW_sb[:], uW), (uas_sb[:], uas), (uad_sb[:], uad)):
                nc.sync.dma_start(dst, src).then_inc(u_in, 16)

        layernorm(nc, sem, ln_mem, "ln3", sync=preload_attention2)

        V = (region(108, (T, CW), BF16), region(135.25, (T, CW), BF16))
        X1 = region(117, (T, 2 * VS), BF16)
        v1 = region(135.25, (T, V1), F32)
        r1 = region(141.5, (T, V1), F32)
        U1 = region(144.25, (2, T, CW), BF16)
        num1 = region(162.25, (T, V1), F32)
        G1 = (xT, mT)
        Wall = region(0, (E, 4 * HID + 4), F32)
        fsB = region(64.5, (N,), F32)
        early1 = bump(148, 160)
        uas_rep, uad_rep = early1([P, P], F32), early1([P, P], F32)
        gmax, tAC, fdg = early1([P, 4], F32), early1([P, 3, T], F32), early1([P, T], F32)
        q_w, q_hT, q_hTs, q_fs, q_fd, q_fc, q_hr, q_hsum, q_c, q_fac, q_hrs, q_fss, q_t, q_v, q_sa, q_sd, q_ones, \
            q_fcs, q_hs = (sem(f"p6_{n}") for n in ("w", "hT", "hTs", "fs", "fd", "fc", "hr", "hsum", "c", "fac",
                                               "hrs", "fss", "t", "v", "sa", "sd", "ones", "fcs", "hs"))
        with nc.Block() as block:
            @block.sync
            def _(sp):
                sp.dma_start(Wall, WrT).then_inc(wall_in, 16)

            @block.gpsimd
            def _(pool):
                pool.wait_ge(u_in, 48)
                nc.gpsimd.tensor_scalar(uas_rep, onesf[:], uas_sb[:], None, ALU.mult).then_inc(q_w, 1)
                nc.gpsimd.tensor_scalar(uad_rep, onesf[:], uad_sb[:], None, ALU.mult).then_inc(q_w, 1)
                nc.gpsimd.memset(X1[:, :, VS - 1:VS], 1.0).then_inc(q_ones, 1)
                nc.gpsimd.memset(X1[:, :, 2 * VS - 1:2 * VS], 1.0).then_inc(q_ones, 1)
                pool.wait_ge(q_ones, 2)

            @block.tensor
            def _(pe):
                pe.wait_ge(u_in, 48)
                for q in range(3):
                    nc.tensor.matmul(psum[:, q, :], uW_sb[:], xT[:, 512 * q:512 * q + 512], start=True,
                                     stop=True).then_inc(q_hT, 1)
                pe.wait_ge(q_w, 2)
                for q in range(3):
                    pe.wait_ge(q_hTs, q + 1)
                    nc.tensor.matmul(psum[:, 3 + q, :], uad_rep, mT[:, 512 * q:512 * q + 512], start=True,
                                     stop=True).then_inc(q_fd, 1)
                for t in range(T):
                    for k, col in enumerate((uas_sb, uad_sb)):
                        last = nc.tensor.matmul(psum[:, 0, 2 * t + k:2 * t + k + 1], mT[:, P * t:P * t + P],
                                                col[:], start=(t == 0 and k == 0), stop=True,
                                                skip_group_check=True)
                last.then_inc(q_fc, 1)
                for t in range(T):
                    last = nc.tensor.transpose(psum[:, (6, 7, 1)[t // 4], P * (t % 4):P * (t % 4) + P],
                                               mT[:, P * t:P * t + P], ident)
                    if t % 4 == 3:
                        last.then_inc(q_hr, 1)
                for q in range(3):
                    if q > 0:
                        pe.wait_ge(q_c, q + 1)
                    nc.tensor.matmul(psum[:, (2, 3, 4)[q], :], uas_rep, mT[:, 512 * q:512 * q + 512],
                                     start=True, stop=True).then_inc(q_fs, 1)
                pe.wait_ge(q_hrs, 3)
                pe.wait_ge(q_c, 3)
                for t in range(T):
                    last = nc.tensor.matmul(psum[:, 5, 0:C], onesf[:], hrow[:, t, :], start=(t == 0),
                                            stop=(t == T - 1))
                last.then_inc(q_hsum, 1)

            @block.scalar
            def _(act):
                for q in range(3):
                    act.wait_ge(q_hT, q + 1)
                    nc.scalar.activation(mT[:, 512 * q:512 * q + 512], psum[:, q, :], ACT.Copy).then_inc(q_hTs, 1)
                for q in range(3):
                    act.wait_ge(q_hr, q + 1)
                    nc.scalar.activation(hrow[:, 4 * q:4 * q + 4, :].rearrange("p t c -> p (t c)"),
                                         psum[:, (6, 7, 1)[q], :], ACT.Copy).then_inc(q_hrs, 1)
                act.wait_ge(q_t, 1)
                nc.scalar.activation(f1[:, 3, :], fdg, ACT.Exp, scale=SLOPE).then_inc(q_fac, 1)
                nc.scalar.activation(f1[:, 1, :], fdg, ACT.Exp).then_inc(q_fac, 1)
                act.wait_ge(q_t, 3)
                nc.scalar.activation(f1[:, 0, :], tAC[:, 0, :], ACT.Exp).then_inc(q_fac, 1)
                nc.scalar.activation(f1[:, 2, :], tAC[:, 1, :], ACT.Exp).then_inc(q_fac, 1)
                for k, at in enumerate((VS, 0)):
                    act.wait_ge(q_v, 2 * (k + 1))
                    nc.scalar.activation(X1[:, :, at:at + V1], v1, ACT.Copy).then_inc(q_sa, 1)
                    if k == 0:
                        for q in range(3):
                            act.wait_ge(q_fs, q + 1)
                            nc.scalar.activation(fsB[:, 512 * q:512 * q + 512], psum[:, (2, 3, 4)[q], :],
                                                 ACT.Copy).then_inc(q_fss, 1)
                    act.wait_ge(q_sd, 2 * k + 1)
                    nc.scalar.activation(X1[:, :, at + V1:at + 2 * V1], r1, ACT.Copy).then_inc(q_sa, 1)
                act.wait_ge(q_hsum, 1)
                nc.scalar.activation(hsum[:], psum[:, 5, 0:C], ACT.Copy).then_inc(q_hs, 1)

            @block.vector
            def _(dve):
                for q in range(3):
                    dve.wait_ge(q_fd, q + 1)
                    nc.vector.tensor_reduce(gmax[:, q:q + 1], psum[:, 3 + q, :], AX, ALU.max).then_inc(q_c, 1)
                dve.wait_ge(q_c, 3)
                nc.vector.tensor_reduce(gmax[:, 3:4], gmax[:, 0:3], AX, ALU.max).then_inc(q_c, 1)
                dve.wait_ge(q_c, 4)
                dve.wait_ge(q_fc, 1)
                fc = psum[:, 0, 0:2 * T].rearrange("p (t k) -> p t k", k=2)
                nc.vector.tensor_scalar(fdg, fc[:, :, 1], gmax[:, 3:4], None, ALU.subtract).then_inc(q_t, 1)
                nc.vector.tensor_scalar(nfd[:], fc[:, :, 1], -1.0, None, ALU.mult).then_inc(q_fcs, 1)
                nc.vector.tensor_scalar(tAC[:, 2, :], fc[:, :, 0], gmax[:, 3:4], None, ALU.add).then_inc(q_fcs, 1)
                dve.wait_ge(q_fcs, 2)
                nc.vector.tensor_scalar(tAC[:, 0, :], tAC[:, 2, :], 1.0 - SLOPE, 0.0, ALU.mult,
                                        ALU.min).then_inc(q_t, 1)
                nc.vector.tensor_scalar(tAC[:, 1, :], tAC[:, 2, :], SLOPE - 1.0, 0.0, ALU.mult,
                                        ALU.min).then_inc(q_t, 1)
                dve.wait_ge(q_hrs, 3)
                for k, (f, at) in enumerate(((f1[:, 3, :], VS), (f1[:, 1, :], 0))):
                    dve.wait_ge(q_fac, k + 1)
                    if k == 1:
                        dve.wait_ge(q_sd, 1)
                        dve.wait_ge(q_sa, 1)
                    nc.vector.tensor_tensor(v1[:, :, 0:C], hrow[:], f.unsqueeze(2).to_broadcast([P, T, C]),
                                            ALU.mult).then_inc(q_v, 1)
                    nc.vector.tensor_copy(v1[:, :, C], f).then_inc(q_v, 1)
                    dve.wait_ge(q_v, 2 * (k + 1))
                    dve.wait_ge(q_sa, 2 * k + 1)
                    if k == 1:
                        dve.wait_ge(q_sd, 2)
                    nc.vector.tensor_tensor(r1, v1, X1[:, :, at:at + V1], ALU.subtract).then_inc(q_sd, 1)
                    dve.wait_ge(q_sa, 2 * k + 2)
                    dve.wait_ge(q_sd, 2 * k + 1)
                    nc.vector.tensor_tensor(X1[:, :, at + 2 * V1:at + 3 * V1], r1, X1[:, :, at + V1:at + 2 * V1],
                                            ALU.subtract).then_inc(q_sd, 1)

        z_t, z_u, z_v, z_used, z_full, z_g, z_gfree = (sem(f"z_{n}") for n in (
            "t", "u", "v", "used", "full", "g", "gfree"))
        CT = CW // P
        with nc.Block() as block:
            @block.vector
            def _(dve):
                dve.sem_inc(z_gfree, 2)

                def sums(n, hh, k):
                    dve.wait_ge(z_g, n + (CT + 1))
                    nc.vector.tensor_reduce(num1[:, bass.ds(n, 1), :].squeeze(1),
                                            G1[k][:, 0:2 * PARTS * V1].rearrange("p (k c) -> p c k", c=V1), AX,
                                            ALU.add).then_inc(z_gfree, 1)

                with dve.Fori(0, 2) as i:
                    for hh in range(2):
                        cols_ = bass.ds(2 * CW * i + CW * hh, CW)
                        dve.wait_ge(z_used, 2 * i + hh + 1)
                        for t in range(T):
                            nc.vector.tensor_scalar(U1[:, hh, t, :], fsB[:, cols_], nfd[:, t:t + 1], None,
                                                    ALU.is_gt).then_inc(z_t, 1)
                        for h in range(2):
                            ts = slice(6 * h, 6 * h + 6)
                            dve.wait_ge(z_t, 2 * T * i + (T * hh + 6 * h + 6))
                            nc.vector.tensor_tensor(U1[:, hh, ts, :], U1[:, hh, ts, :], M2[:, ts, cols_],
                                                    ALU.mult).then_inc(z_u, 1)
                            dve.wait_ge(z_u, 4 * i + (2 * hh + h + 1))
                            nc.vector.tensor_tensor(V[hh][:, ts, :], M2[:, ts, cols_], U1[:, hh, ts, :],
                                                    ALU.subtract).then_inc(z_v, 1)
                        if hh == 1:
                            for k in range(CT):
                                sums(2 * CT * i + k, 0, k % 2)
                    for k in range(CT):
                        sums(2 * CT * i + (CT + k), 1, (CT + k) % 2)

            @block.tensor
            def _(pe):
                pe.sem_inc(z_used, 2)
                with pe.Fori(0, 2) as i:
                    for hh in range(2):
                        for k in range(CT):
                            pe.wait_ge(z_g, 2 * CT * i + (CT * hh + k + 1))
                            for t in range(T):
                                if k == 0 and t % 6 == 0:
                                    pe.wait_ge(z_v, 4 * i + (2 * hh + t // 6 + 1))
                                nc.tensor.matmul(psum[:, 2 * k, 0:VS], U1[:, hh, t, P * k:P * k + P],
                                                 X1[:, t, 0:VS], start=(t == 0), stop=(t == T - 1),
                                                 skip_group_check=True)
                                last = nc.tensor.matmul(psum[:, 2 * k + 1, 0:VS], V[hh][:, t, P * k:P * k + P],
                                                        X1[:, t, VS:2 * VS], start=(t == 0), stop=(t == T - 1),
                                                        skip_group_check=True)
                            last.then_inc(z_full, 1)
                        nc.tensor.matmul(psum[:, 7, 0:2], onesb[:], onesb[:, 0:2], start=True,
                                         stop=True).then_inc(z_used, 1)

            @block.scalar
            def _(act):
                act.sem_inc(z_g, CT)
                with act.Fori(0, 2) as i:
                    for hh in range(2):
                        for k in range(CT):
                            n = 2 * CT * i + (CT * hh + k)
                            col = bass.ds(n, 1)
                            g = G1[(CT * hh + k) % 2]
                            act.wait_ge(z_full, n + 1)
                            act.wait_ge(z_gfree, n + 1)
                            nc.scalar.activation(dg[:, 0, col], psum[:, 2 * k, VS - 1:VS], ACT.Copy)
                            nc.scalar.activation(dg[:, 1, col], psum[:, 2 * k + 1, VS - 1:VS], ACT.Copy)
                            nc.scalar.activation(g[:, 0:VS - 1], psum[:, 2 * k, 0:VS - 1], ACT.Copy,
                                                 scale=f1[:, 0, col])
                            nc.scalar.activation(g[:, VS - 1:2 * VS - 2], psum[:, 2 * k + 1, 0:VS - 1], ACT.Copy,
                                                 scale=f1[:, 2, col]).then_inc(z_g, 1)

        w_c, w_n, w_e = sem("p6_wc"), sem("p6_wn"), sem("p6_we")
        agg = xT[:, :].rearrange("p (t c) -> p t c", t=T)
        expo = mT[:, :].rearrange("p (t c) -> p t c", t=T)
        with nc.Block() as block:
            @block.vector
            def _(dve):
                n = [0]

                def link(ins):
                    n[0] += 1
                    ins.then_inc(w_c, 1)
                    dve.wait_ge(w_c, n[0])

                link(nc.vector.tensor_tensor(emp[:], dg[:, 0, :], dg[:, 1, :], ALU.add))
                link(nc.vector.tensor_scalar(emp[:], emp[:], 0.0, None, ALU.is_equal))
                link(nc.vector.scalar_tensor_tensor(deg[:], emp[:], float(N), num1[:, :, C], ALU.mult, ALU.add))
                link(nc.vector.reciprocal(deg[:], deg[:]))
                for t in range(T):
                    last = nc.vector.scalar_tensor_tensor(agg[:, t, :], hsum[:], emp[:, t:t + 1],
                                                          num1[:, t, 0:C], ALU.mult, ALU.add)
                link(last)
                link(nc.vector.tensor_tensor(agg, agg, deg[:].unsqueeze(2).to_broadcast([P, T, C]), ALU.mult))
                nc.vector.tensor_scalar(expo, agg, 0.0, None, ALU.min).then_inc(w_n, 1)
                link(nc.vector.tensor_scalar(agg, agg, 0.0, -1.0, ALU.max, ALU.add))
                link(nc.vector.tensor_tensor(xr[:], xr[:], agg, ALU.add))
                dve.wait_ge(w_e, 1)
                link(nc.vector.tensor_tensor(xr[:], xr[:], hrow[:], ALU.add))

            @block.scalar
            def _(act):
                act.wait_ge(w_n, 1)
                nc.scalar.activation(hrow[:], expo, ACT.Exp).then_inc(w_e, 1)

        xs4 = region(72, (FT * TS,), F32)
        h2s = region(85, (KC, FT * TS), F32)
        h2 = region(110, (KC, N), F32)
        ring = region(123, (2, 4 * HID + 4), F32)
        h0r = region(131.5, (2, KC, TS), F32)
        h1r = region(133.5, (2, KC, TS), F32)
        late = bump(136, 150)
        WsI = late([P, 4 * HID + 4], F32)
        Wi_sb, Wo_sb, bi_sb, boB = (late(k, F32) for k in ([P, HID], [P, KC, C], [P, KC], [P, C]))

        def preload_last():
            for dst, src in ((WsI, WsT), (Wi_sb, WiT), (Wo_sb, WoT), (bi_sb, bi),
                             (boB, bo.squeeze(0).partition_broadcast(P))):
                nc.sync.dma_start(dst, src).then_inc(l_in, 16)

        def clear_slots():
            nc.gpsimd.memset(xs4, 0.0).then_inc(cleared, 1)

        layernorm(nc, sem, ln_mem, "ln4", sync=preload_last, pool=clear_slots)

        m_h0p, m_h0, m_h1p, m_h1, m_h2p, m_ring, m_wsi, m_out, m_bo, m_perm_d, m_perm_a, \
            m_rows, m_done, m_h2w = (sem(f"m_{n}") for n in (
                "h0p", "h0", "h1p", "h1", "h2p", "ring", "wsi", "out", "bo", "perm_d",
                "perm_a", "rows", "done", "h2w"))
        GB = 8

        def group_starts(eng, b):
            return nc.values_load_multi_w_load_instructions(
                gpos_i[0:1, GB * b:GB * b + GB], engines=[eng], min_val=0, max_val=(FT - 1) * TS + TS - GT,
                skip_runtime_bounds_check_because="below the slots' end as made")[1]

        with nc.Block() as block:
            @block.vector
            def _(dve):
                dve.wait_ge(l_in, 80)
                for l in range(2):
                    for k in range(KC):
                        at = l * KC * HID + k * HID + k * P
                        nc.vector.tensor_tensor(WsI[:, at:at + P], WsI[:, at:at + P], ident,
                                                ALU.add).then_inc(m_wsi, 1)
                for b in range(0, GROUPS // GB, 2):
                    g = group_starts(mybir.EngineType.DVE, b)
                    for j in range(GB):
                        nc.vector.tensor_copy(xs4[:, bass.ds(g[j], GT)],
                                              xT[:, GT * (GB * b + j):GT * (GB * b + j) + GT]).then_inc(m_perm_d, 1)
                dve.wait_ge(m_perm_d, GROUPS // 2)
                dve.wait_ge(m_wsi, 2 * KC)

            @block.scalar
            def _(act):
                for b in range(1, GROUPS // GB, 2):
                    g = group_starts(mybir.EngineType.Activation, b)
                    for j in range(GB):
                        nc.scalar.activation(xs4[:, bass.ds(g[j], GT)],
                                             xT[:, GT * (GB * b + j):GT * (GB * b + j) + GT],
                                             ACT.Copy).then_inc(m_perm_a, 1)
                act.wait_ge(m_perm_a, GROUPS // 2)

            @block.gpsimd
            def _(pool):
                pool.wait_ge(l_in, 80)
                nc.gpsimd.tensor_tensor(xr[:], xr[:], boB.unsqueeze(1).to_broadcast([P, T, C]),
                                        ALU.add).then_inc(m_bo, 1)
                pool.wait_ge(m_bo, 1)

        with nc.Block() as block:
            @block.vector
            def _(dve):
                dve.sem_inc(m_h0, 2)
                with dve.Fori(0, FT // 2) as i:
                    e_of = nc.values_load_multi_w_load_instructions(
                        ge[0:1, bass.ds(i * 2, 2)], engines=[mybir.EngineType.DVE], min_val=0, max_val=E - 1,
                        skip_runtime_bounds_check_because="clamped when made")[1]
                    for k in range(2):
                        dve.wait_ge(m_h2w, 2 * i + k + 1)
                        nc.vector.tensor_tensor(ring[:, k, :], Wall[:, bass.ds(e_of[k], 1), :].squeeze(1), WsI,
                                                ALU.add).then_inc(m_ring, 1)
                        dve.wait_ge(m_h0p, 2 * i + k + 1)
                        dve.wait_ge(m_h1p, 2 * i + k + 1)
                        for m in range(KC):
                            last = nc.vector.tensor_scalar(h0r[:, k, m, :], psum[:, k, TS * m:TS * m + TS],
                                                           bi_sb[:, m:m + 1], 0.0, ALU.add, ALU.max)
                            if m == KC - 1:
                                last.then_inc(m_h0, 1)

            @block.tensor
            def _(pe):
                pe.sem_inc(m_h1p, 2)

                def layer(l, k, src, bank):
                    for o in range(KC):
                        for m in range(KC):
                            at = l * KC * HID + m * HID + o * P
                            last = nc.tensor.matmul(psum[:, bank, TS * o:TS * o + TS], ring[:, k, at:at + P],
                                                    src[:, k, m, :], start=(m == 0), stop=(m == KC - 1),
                                                    skip_group_check=True)
                    return last

                with pe.Fori(0, FT // 2) as i:
                    for k in range(2):
                        pe.wait_ge(m_h0, 2 * i + k + 1)
                        for m in range(KC):
                            last = nc.tensor.matmul(psum[:, k, TS * m:TS * m + TS], Wi_sb[:, P * m:P * m + P],
                                                    xs4[:, bass.ds((2 * i + k) * TS, TS)], start=True, stop=True,
                                                    skip_group_check=True)
                        last.then_inc(m_h0p, 1)
                    for k in range(2):
                        pe.wait_ge(m_h0, 2 * i + (2 + k + 1))
                        pe.wait_ge(m_ring, 2 * i + k + 1)
                        pe.wait_ge(m_h1, 2 * i + k + 1)
                        layer(0, k, h0r, 2 + k).then_inc(m_h1p, 1)
                    for k in range(2):
                        pe.wait_ge(m_h1, 2 * i + (2 + k + 1))
                        pe.wait_ge(m_h2w, 2 * i + k + 1)
                        layer(1, k, h1r, 4 + k).then_inc(m_h2p, 1)

            @block.scalar
            def _(act):
                act.sem_inc(m_h1, 2)
                act.sem_inc(m_h2w, 2)
                with act.Fori(0, FT // 2) as i:
                    for k in range(2):
                        act.wait_ge(m_h1p, 2 * i + (2 + k + 1))
                        for o in range(KC):
                            last = nc.scalar.activation(h1r[:, k, o, :], psum[:, 2 + k, TS * o:TS * o + TS],
                                                        ACT.Relu, bias=ring[:, k, 4 * HID + o:4 * HID + o + 1])
                        last.then_inc(m_h1, 1)
                    for k in range(2):
                        act.wait_ge(m_h2p, 2 * i + k + 1)
                        for o in range(KC):
                            last = nc.scalar.activation(
                                h2s[:, o, bass.ds((2 * i + k) * TS, TS)], psum[:, 4 + k, TS * o:TS * o + TS],
                                ACT.Relu, bias=ring[:, k, 4 * HID + KC + o:4 * HID + KC + o + 1])
                        last.then_inc(m_h2w, 1)

        with nc.Block() as block:
            @block.vector
            def _(dve):
                for b in range(0, GROUPS // GB, 2):
                    g = group_starts(mybir.EngineType.DVE, b)
                    for j in range(GB):
                        nc.vector.tensor_copy(h2[:, :, GT * (GB * b + j):GT * (GB * b + j) + GT],
                                              h2s[:, :, bass.ds(g[j], GT)]).then_inc(m_perm_d, 1)
                for q in range(3):
                    dve.wait_ge(m_out, q + 1)
                    nc.vector.tensor_tensor(xr[:, 4 * q:4 * q + 4, :], xr[:, 4 * q:4 * q + 4, :],
                                            psum[:, q, :].rearrange("p (t c) -> p t c", c=C),
                                            ALU.add).then_inc(m_rows, 1)

            @block.scalar
            def _(act):
                for b in range(1, GROUPS // GB, 2):
                    g = group_starts(mybir.EngineType.Activation, b)
                    for j in range(GB):
                        nc.scalar.activation(h2[:, :, GT * (GB * b + j):GT * (GB * b + j) + GT],
                                             h2s[:, :, bass.ds(g[j], GT)], ACT.Copy).then_inc(m_perm_a, 1)

            @block.tensor
            def _(pe):
                for t in range(T):
                    if t % 3 == 0:
                        pe.wait_ge(m_perm_d, GROUPS // 2 + GB * (t // 3 + 1))
                        pe.wait_ge(m_perm_a, GROUPS // 2 + GB * (t // 3 + 1))
                    for m in range(KC):
                        last = nc.tensor.matmul(psum[:, t // 4, P * (t % 4):P * (t % 4) + P],
                                                h2[:, m, P * t:P * t + P], Wo_sb[:, m, :], start=(m == 0),
                                                stop=(m == KC - 1), skip_group_check=True)
                    if t % 4 == 3:
                        last.then_inc(m_out, 1)

            @block.sync
            def _(sp):
                out_v = out.rearrange("(t p) c -> p t c", p=P)
                for q in range(3):
                    sp.wait_ge(m_rows, q + 1)
                    sp.dma_start(out_v[:, 4 * q:4 * q + 4, :], xr[:, 4 * q:4 * q + 4, :]).then_inc(m_done, 16)
                sp.wait_ge(m_done, 48)


def constants():
    import numpy as np
    c = np.zeros((P, K_END), np.float32)
    c[:, K_ID:K_ID + P] = np.eye(P)
    c[:, K_TRI:K_TRI + P] = np.triu(np.ones((P, P)), 1)
    c[:, K_HM:K_HM + H] = np.arange(P)[:, None] // D == np.arange(H)[None, :]
    c[:, K_IOTA:K_IOTA + E] = np.arange(E)
    c[:, K_SLOT:K_SLOT + SLOT_TILES] = np.arange(SLOT_TILES) * P
    c[:, K_FT:K_FT + FT] = np.arange(FT) * TS
    return c


def kernel(**inputs):
    import numpy as np
    import concourse.bacc as bacc
    from concourse.bass_utils import run_bass_kernel_spmd

    a = {k: np.asarray(v) for k, v in inputs.items()}
    turned = lambda v, *axes: np.ascontiguousarray(np.transpose(v, axes))
    arrays = {
        "x": a["x"], "adjT": turned(a["adj"], 1, 0),
        "gW": turned(a["L0_gnn_W"], 1, 0), "gb": a["L0_gnn_bW"].reshape(C, 1),
        "ga1": np.tile(a["L0_gnn_a1"], H).reshape(C, 1), "ga2": np.tile(a["L0_gnn_a2"], H).reshape(C, 1),
        "gab": a["L0_gnn_ab"].reshape(1), "gate_w": a["L0_ffn_gate_w"],
        "gate_b": a["L0_ffn_gate_b"].reshape(1, E),
        "w1": turned(a["L0_ffn_w1"], 1, 0, 2), "w2": turned(a["L0_ffn_w2"], 1, 0, 2),
        "w3": turned(a["L0_ffn_w3"].reshape(E, KC, P, C), 2, 0, 1, 3),
        "uW": a["L1_gnn_W"], "uas": a["L1_gnn_a_src"], "uad": a["L1_gnn_a_dst"],
        "route": a["L1_ffn_route_id"].reshape(GROUPS, 1),
        "WiT": turned(a["L1_ffn_Wi"], 1, 0), "bi": turned(a["L1_ffn_bi"].reshape(KC, P), 1, 0),
        "WrT": np.concatenate([
            turned(a["L1_ffn_Wr"].reshape(2, E, HID, KC, P), 4, 1, 0, 3, 2).reshape(P, E, 4 * HID),
            turned(a["L1_ffn_br"].reshape(2, E, KC, P), 3, 1, 0, 2).reshape(P, E, 4)], axis=2),
        "WsT": np.concatenate([
            turned(a["L1_ffn_Ws"].reshape(2, HID, KC, P), 3, 0, 2, 1).reshape(P, 4 * HID),
            turned(a["L1_ffn_bs"].reshape(2, KC, P), 2, 0, 1).reshape(P, 4)], axis=1),
        "WoT": turned(a["L1_ffn_Wo"].reshape(C, KC, P), 2, 1, 0), "bo": a["L1_ffn_bo"].reshape(1, C),
        "consts": constants(),
    }
    nc = bacc.Bacc("TRN2", target_bir_lowering=False, num_devices=1)
    maps, args = {}, {}
    for name, v in arrays.items():
        v = np.ascontiguousarray(v)
        maps[f"in_{name}"] = v
        args[name] = nc.dram_tensor(f"in_{name}", v.shape, mybir.dt.from_np(v.dtype), kind="ExternalInput").ap()
    args["out"] = nc.dram_tensor("out_rows", (N, C), F32, kind="ExternalOutput").ap()
    build(nc, **args)
    r = run_bass_kernel_spmd(nc, [maps], core_ids=[0])
    return r.results[0]["out_rows"]
```

```python
from contextlib import ExitStack

import concourse.bass as bass
from concourse import mybir

F32 = mybir.dt.float32
BF16 = mybir.dt.bfloat16
I32 = mybir.dt.int32
U32 = mybir.dt.uint32
ALU = mybir.AluOpType
ACT = mybir.ActivationFunctionType
AX = mybir.AxisListType.X

P = 128
N = 1536
T = N // P
C = 128
H = 8
D = C // H
D1 = D + 1
E = 16
HID = 256
KC = HID // P
PARTS = 3
SLOT_TILES = 40
GROUPS = 64
GT = N // GROUPS
GPT = P // GT
TS = GPT * GT
FT = 26
BIG = 2.0 ** 100
EPS = 1e-5
SLOPE = 0.2

K_ID, K_TRI, K_HM, K_IOTA, K_SLOT, K_FT = 0, 128, 256, 264, 280, 320
K_END = K_FT + FT

HS = 104
X_B, X_D, X_ONE = 0, PARTS * D1, 2 * PARTS * D1
R2 = 2 * D1
V1 = C + 1
VS = PARTS * V1 + 1
ST = 5
RING = 4
CW = 3 * P


def layernorm(nc, s, mem, name, sync=None, pool=None, gap=None, end=None, stats_made=False):
    xr, xn, xT, ident, st, mv, rstd, half, psum = mem
    scale, normed, turned = (s(f"{name}_{x}") for x in ("scale", "normed", "turned"))
    if not stats_made:
        stats, var = s(f"{name}_stats"), s(f"{name}_var")
    clear = pool
    with nc.Block() as block:
        if sync is not None:
            @block.sync
            def _(sp):
                sync(sp)

        @block.vector
        def _(dve):
            for t in range(0 if stats_made else T):
                nc.vector.bn_stats(st[:, t, :], xr[:, t, :]).then_inc(stats, 1)
            for t in range(0 if stats_made else T):
                dve.wait_ge(stats, t + 1)
                nc.vector.bn_aggr(mv[:, t, :], st[:, t, :]).then_inc(var, 1)
            if gap is not None:
                gap(dve)
            dve.wait_ge(scale, 3)
            for t in range(T):
                nc.vector.tensor_scalar(xn[:, t, :], xr[:, t, :], mv[:, t, 0:1], rstd[:, t:t + 1],
                                        ALU.subtract, ALU.mult).then_inc(normed, 1)
            for q in range(T // 4):
                if q % 2 == 1:
                    dve.wait_ge(turned, q + 1)
                    nc.vector.tensor_copy(xT[:, 512 * q:512 * q + 512], psum[:, q, :])
            if end is not None:
                end(dve)

        @block.gpsimd
        def _(pool):
            nc.gpsimd.memset(half[:], -0.5).then_inc(scale, 1)
            if not stats_made:
                pool.wait_ge(var, T)
            nc.gpsimd.tensor_scalar(rstd[:], mv[:, :, 1], EPS, None, ALU.add).then_inc(scale, 1)
            pool.wait_ge(scale, 2)
            nc.gpsimd.tensor_tensor(rstd[:], rstd[:], half[:], ALU.pow).then_inc(scale, 1)
            if clear is not None:
                clear(pool)

        @block.tensor
        def _(pe):
            for t in range(T):
                pe.wait_ge(normed, t + 1)
                last = nc.tensor.transpose(psum[:, t // 4, P * (t % 4):P * (t % 4) + P], xn[:, t, :], ident)
                if t % 4 == 3:
                    last.then_inc(turned, 1)

        @block.scalar
        def _(act):
            for q in range(0, T // 4, 2):
                act.wait_ge(turned, q + 1)
                nc.scalar.activation(xT[:, 512 * q:512 * q + 512], psum[:, q, :], ACT.Copy)


def build(nc, x, adjT, gW, gb, ga1, ga2, gab, gate_w, gate_b, w1, w2, w3, uW, uas, uad,
          route, WiT, bi, WrT, WsT, WoT, bo, consts, out):
    with ExitStack() as ctx:
        def sb(name, shape, dt):
            return ctx.enter_context(nc.sbuf_tensor(name, shape, dt))

        def sem(name):
            return ctx.enter_context(nc.semaphore(name))

        arena = sb("arena", [P, 169 * 256], F32)

        def region(kb, shape, dt):
            n = 1
            for k in shape:
                n *= k
            words = n * (2 if dt == BF16 else 4) // 4
            a = arena[:, int(kb * 256):int(kb * 256) + words]
            if dt != F32:
                a = a.bitcast(dt)
            if len(shape) == 2:
                a = a.rearrange("p (a b) -> p a b", a=shape[0])
            if len(shape) == 3:
                a = a.rearrange("p (a b c) -> p a b c", a=shape[0], b=shape[1])
            return a

        def bump(kb, end):
            at = [kb * 1024]

            def small(shape, dt):
                t = region(at[0] / 1024, tuple(shape[1:]), dt)
                n = 2 if dt == BF16 else 4
                for k in shape[1:]:
                    n *= k
                at[0] += (n + 63) // 64 * 64
                assert at[0] <= end * 1024
                return t[0:shape[0]]
            return small

        psum = ctx.enter_context(nc.psum_tensor("psum", [P, 8, 512], F32))

        cst = sb("cst", [P, K_END], F32)
        xr = sb("xr", [P, T, C], F32)
        xn = sb("xn", [P, T, C], F32)
        xT = sb("xT", [P, N], F32)
        mT = sb("mT", [P, N], F32)
        hrow = sb("hrow", [P, T, C], F32)
        st = sb("st", [P, T, 6], F32)
        mv = sb("mv", [P, T, 2], F32)
        rstd = sb("rstd", [P, T], F32)
        half = sb("half", [P, T], F32)
        onesb = sb("onesb", [P, P], BF16)
        onesf = sb("onesf", [P, P], F32)
        trib = sb("trib", [P, P], BF16)
        ident = cst[:, K_ID:K_ID + P]
        ln_mem = (xr, xn, xT, ident, st, mv, rstd, half, psum)

        s_bcast = nc.dram_tensor("si_rows", (H, N), F32, kind="Internal").ap()
        slots_in = nc.dram_tensor("slots_in", (SLOT_TILES * P, C), F32, kind="Internal").ap()
        slots_out = nc.dram_tensor("slots_out", (SLOT_TILES * P, C), F32, kind="Internal").ap()

        uW_sb = sb("uW_sb", [P, C], F32)
        ua_sb = sb("ua_sb", [P, 2], F32)
        f1 = sb("f1", [P, 4, T], F32)
        fdc = sb("fdc", [P, T], F32)
        dg = sb("dg", [P, 2, T], F32)
        u_in, wall_in, l_in, cleared = sem("u_in"), sem("wall_in"), sem("l_in"), sem("cleared")
        zeroed, zero_set = sem("zeroed"), sem("zero_set")
        zero = sb("zero", [P, C], F32)
        x_in, weights_in, adj_in = sem("x_in"), sem("weights_in"), [sem(f"adj_in{k}") for k in range(ST)]

        M = region(0, (T, N), BF16)
        MB = region(36, (T, N), BF16)
        siB = region(72, (2, N), F32)
        S = [region(84 + 3 * k, (N,), BF16) for k in range(4)]
        for whole in (mT[:, :], hrow[:, :, :].rearrange("p t c -> p (t c)"), xT[:, :]):
            S += [whole.bitcast(BF16)[:, N * k:N * k + N] for k in range(2)]
        SR = len(S)
        U = region(99, (4, N), BF16)
        stage = region(84, (ST, N), I32)
        X = region(117, (T, H, HS), BF16)
        vr = ((region(136.5, (T * H, D1), F32), region(143, (T * H, D1), F32)),
              (region(152, (T * H, D1), F32), region(162.5, (T * H, D1), F32)))
        S34 = region(149.5, (T * H, R2), F32)
        YD = region(162.5, (T * H, D1), F32)

        early = bump(149.5, 152)
        gW_sb = early([P, C], F32)
        cols = sb("cols", [P, 8], F32)
        a16 = sb("a16", [P, 2 * H], F32)
        sc = sb("sc", [P, T, 2 * H], F32)
        gB = sb("gB", [P, 2 * H], F32)
        gcol = sb("gcol", [2 * H, 1], F32)
        gdiag = sb("gdiag", [2 * H, 2 * H], F32)
        srow = region(162.5, (N,), F32)
        sjg = early([P, T, H], F32)
        nsj = sb("nsj", [P, T, H], F32)
        tA = early([P, T, H], F32)
        tC = early([P, T, H], F32)
        fB = sb("fB", [P, T * H], F32)
        fD = early([P, T * H], F32)
        fA = sb("fA", [P, T * H], F32)
        fC = sb("fC", [P, T * H], F32)
        deg = sb("deg", [P, T], F32)
        emp = sb("emp", [P, T], F32)
        hsum = sb("hsum", [P, C], F32)

        si_in = [sem("si_in0"), sem("si_in1")]
        mb_made, m_dve, m_act, m_pool, dch = sem("mb_made"), sem("m_dve"), sem("m_act"), sem("m_pool"), sem("p1_dch")

        def load_adjacency(sp, a, b):
            for t in range(a, b):
                if t >= ST:
                    sp.wait_ge(mb_made, t - ST + 1)
                sp.dma_start(stage[:, t % ST, :], adjT[P * t:P * t + P, :]).then_inc(adj_in[t % ST], 16)

        LATE = 8

        def masks(dve, a, b):
            for t in range(a, b):
                dve.wait_ge(adj_in[t % ST], 16 * (t // ST + 1))
                nc.vector.tensor_scalar(MB[:, t, :], stage[:, t % ST, :], 0.0, BIG, ALU.is_equal,
                                        ALU.mult).then_inc(mb_made, 1)

        with nc.Block() as block:
            @block.sync
            def _(sp):
                sp.dma_start(xr[:], x.rearrange("(t p) c -> p t c", p=P)).then_inc(x_in, 16)
                sp.dma_start(cst[:], consts).then_inc(x_in, 16)
                load_adjacency(sp, 0, 2)
                for dst, src in ((gW_sb[:], gW), (cols[:, 0:1], gb), (cols[:, 1:2], ga1), (cols[:, 2:3], ga2),
                                 (cols[:, 3:4], gab.partition_broadcast(P))):
                    sp.dma_start(dst, src).then_inc(weights_in, 16)
                load_adjacency(sp, 2, ST)
                sp.wait_ge(x_in, 32)

            @block.gpsimd
            def _(pool):
                nc.gpsimd.memset(zero[:], 0.0).then_inc(zero_set, 1)

        layernorm(nc, sem, ln_mem, "ln1", sync=lambda sp: load_adjacency(sp, ST, ST + 4),
                  gap=lambda dve: masks(dve, 0, 2), end=lambda dve: masks(dve, 2, 4))

        a16_ready, hT_ps, hT_sb, hr_ps, sc_ps, sr_ps, g_ready, gB_ps, hsum_ps, sr_sb, sjg_ready, f_ready, hr_sb, \
            v_ready, split_a, split_d, si_out, hs_ready, sc_ready, ones_ready = (sem(f"p1_{n}") for n in (
                "a16", "hT_ps", "hT_sb", "hr_ps", "sc_ps", "sr_ps", "g", "gB_ps", "hsum_ps", "sr_sb", "sjg", "f",
                "hr_sb", "v", "split_a", "split_d", "si_out", "hs", "sc", "ones"))
        Xg = X.rearrange("p t h c -> p (t h) c")
        with nc.Block() as block:
            @block.sync
            def _(sp):
                load_adjacency(sp, ST + 4, T)
                sp.wait_ge(sr_sb, 3)
                sp.dma_start(s_bcast, srow[0:H, :]).then_inc(si_out, 16)
                sp.wait_ge(si_out, 16)
                for hh in range(2):
                    sp.dma_start(siB[:, hh, :], s_bcast[hh, :].partition_broadcast(P)).then_inc(si_in[hh], 16)
                sp.wait_ge(zero_set, 1)
                sp.dma_start(slots_in.rearrange("(s p) c -> p s c", p=P),
                             zero[:].unsqueeze(1).to_broadcast([P, SLOT_TILES, C])).then_inc(zeroed, 16)
                sp.wait_ge(zeroed, 16)

            @block.gpsimd
            def _(pool):
                nc.gpsimd.memset(onesf[:], 1.0).then_inc(ones_ready, 1)
                nc.gpsimd.memset(onesb[:], 1.0).then_inc(ones_ready, 1)
                nc.gpsimd.memset(X[:, :, :, X_ONE:HS], 1.0).then_inc(ones_ready, 1)
                nc.gpsimd.tensor_copy(trib[:], cst[:, K_TRI:K_TRI + P]).then_inc(ones_ready, 1)
                for t in (0, 3, 6):
                    pool.wait_ge(mb_made, t + 1)
                    nc.gpsimd.tensor_scalar(M[:, t, :], MB[:, t, :], -1.0 / BIG, 1.0, ALU.mult,
                                            ALU.add).then_inc(m_pool, 1)

            @block.tensor
            def _(pe):
                pe.wait_ge(weights_in, 80)
                for q in range(3):
                    nc.tensor.matmul(psum[:, q, :], gW_sb[:], xT[:, 512 * q:512 * q + 512], start=True,
                                     stop=True).then_inc(hT_ps, 1)
                pe.wait_ge(hT_sb, 3)
                pe.wait_ge(a16_ready, 2)
                for q in range(3):
                    nc.tensor.matmul(psum[0:2 * H, 3 + q, :], a16[:], mT[:, 512 * q:512 * q + 512], start=True,
                                     stop=True).then_inc(sr_ps, 1)
                for t in range(T):
                    last = nc.tensor.matmul(psum[:, 6, 2 * H * t:2 * H * t + 2 * H], mT[:, P * t:P * t + P],
                                            a16[:], start=(t == 0), stop=True, skip_group_check=True)
                last.then_inc(sc_ps, 1)
                for t in range(T):
                    last = nc.tensor.transpose(psum[:, t // 4, P * (t % 4):P * (t % 4) + P],
                                               mT[:, P * t:P * t + P], ident)
                    if t % 4 == 3:
                        last.then_inc(hr_ps, 1)
                pe.wait_ge(g_ready, 1)
                pe.wait_ge(ones_ready, 1)
                nc.tensor.matmul(psum[:, 7, 0:2 * H], onesf[0:2 * H, :], gdiag[:], start=True,
                                 stop=True).then_inc(gB_ps, 1)
                pe.wait_ge(hr_sb, 3)
                pe.wait_ge(sc_ready, 1)
                for t in range(T):
                    last = nc.tensor.matmul(psum[:, 6, 0:C], onesf[:], hrow[:, t, :], start=(t == 0),
                                            stop=(t == T - 1))
                last.then_inc(hsum_ps, 1)

            @block.scalar
            def _(act):
                def adjacent(*ts):
                    for t in ts:
                        act.wait_ge(mb_made, t + 1)
                        nc.scalar.activation(M[:, t, :], MB[:, t, :], ACT.Identity, scale=-1.0 / BIG,
                                             bias=onesf[:, 0:1]).then_inc(m_act, 1)

                for q in range(3):
                    act.wait_ge(hT_ps, q + 1)
                    nc.scalar.activation(mT[:, 512 * q:512 * q + 512], psum[:, q, :], ACT.Identity,
                                         bias=cols[:, 0:1]).then_inc(hT_sb, 1)
                for q in range(3):
                    act.wait_ge(sr_ps, q + 1)
                    nc.scalar.activation(srow[0:2 * H, 512 * q:512 * q + 512], psum[0:2 * H, 3 + q, :],
                                         ACT.Identity, bias=cols[0:2 * H, 3:4]).then_inc(sr_sb, 1)
                act.wait_ge(ones_ready, 1)
                adjacent(1)
                for q in range(3):
                    act.wait_ge(hr_ps, q + 1)
                    nc.scalar.activation(hrow[:, 4 * q:4 * q + 4, :].rearrange("p t c -> p (t c)"), psum[:, q, :],
                                         ACT.Copy).then_inc(hr_sb, 1)
                adjacent(2)
                act.wait_ge(sjg_ready, 3)
                flat = lambda a: a[:, :, :].rearrange("p t h -> p (t h)")
                nc.scalar.activation(fD[:], flat(sjg), ACT.Exp, scale=SLOPE).then_inc(f_ready, 1)
                nc.scalar.activation(fB[:], flat(sjg), ACT.Exp).then_inc(f_ready, 1)
                nc.scalar.activation(fA[:], flat(tA), ACT.Exp).then_inc(f_ready, 1)
                nc.scalar.activation(fC[:], flat(tC), ACT.Exp).then_inc(f_ready, 1)
                for k, at in enumerate((X_D, X_B)):
                    act.wait_ge(v_ready, 2 * (k + 1))
                    nc.scalar.activation(Xg[:, :, at:at + D1], vr[k][0], ACT.Copy).then_inc(split_a, 1)
                for k, at in enumerate((X_D, X_B)):
                    act.wait_ge(split_d, k + 1)
                    nc.scalar.activation(Xg[:, :, at + D1:at + 2 * D1], vr[k][1], ACT.Copy).then_inc(split_a, 1)
                adjacent(4, 5, 7)
                act.wait_ge(hsum_ps, 1)
                nc.scalar.activation(hsum[:], psum[:, 6, 0:C], ACT.Copy).then_inc(hs_ready, 1)

            @block.vector
            def _(dve):
                dve.wait_ge(weights_in, 80)
                for k in range(2):
                    nc.vector.tensor_scalar(a16[:, H * k:H * k + H], cst[:, K_HM:K_HM + H], cols[:, 1 + k:2 + k],
                                            None, ALU.mult).then_inc(a16_ready, 1)
                masks(dve, 4, 8)
                dve.wait_ge(sr_sb, 3)
                nc.vector.tensor_reduce(gcol[:], srow[0:2 * H, :], AX, ALU.max).then_inc(dch, 1)
                dve.wait_ge(dch, 1)
                nc.vector.tensor_scalar(gdiag[:], cst[0:2 * H, K_ID:K_ID + 2 * H], gcol[:], None,
                                        ALU.mult).then_inc(g_ready, 1)
                dve.wait_ge(sc_ps, 1)
                nc.vector.tensor_copy(sc[:, :, :].rearrange("p t h -> p (t h)"),
                                      psum[:, 6, 0:T * 2 * H]).then_inc(sc_ready, 1)
                dve.wait_ge(gB_ps, 1)
                nc.vector.tensor_copy(gB[:], psum[:, 7, 0:2 * H]).then_inc(dch, 1)
                dve.wait_ge(dch, 2)
                dve.wait_ge(sc_ready, 1)
                g3 = gB[:, H:2 * H].unsqueeze(1).to_broadcast([P, T, H])
                nc.vector.tensor_tensor(sjg[:], sc[:, :, H:2 * H], g3, ALU.subtract).then_inc(dch, 1)
                nc.vector.tensor_tensor(tA[:], sc[:, :, 0:H], g3, ALU.add).then_inc(dch, 1)
                nc.vector.tensor_scalar(nsj[:], sc[:, :, H:2 * H], -1.0, None, ALU.mult).then_inc(dch, 1)
                dve.wait_ge(dch, 5)
                nc.vector.tensor_scalar(sjg[:], sjg[:], cols[:, 3:4], None, ALU.add).then_inc(sjg_ready, 1)
                nc.vector.tensor_scalar(tC[:], tA[:], SLOPE - 1.0, 0.0, ALU.mult, ALU.min).then_inc(sjg_ready, 1)
                dve.wait_ge(sjg_ready, 2)
                nc.vector.tensor_scalar(tA[:], tA[:], 1.0 - SLOPE, 0.0, ALU.mult, ALU.min).then_inc(sjg_ready, 1)
                masks(dve, 8, 9)
                dve.wait_ge(hr_sb, 3)
                halves = tuple(zip(vr, (fD, fB), (X_D, X_B)))
                for k, ((v, r), f, at) in enumerate(halves):
                    dve.wait_ge(f_ready, k + 1)
                    nc.vector.tensor_tensor(v[:, :, 0:D], hrow[:, :, :].rearrange("p t (h d) -> p (t h) d", h=H),
                                            f[:].unsqueeze(2).to_broadcast([P, T * H, D]),
                                            ALU.mult).then_inc(v_ready, 1)
                    nc.vector.tensor_copy(v[:, :, D], f[:]).then_inc(v_ready, 1)
                dve.wait_ge(si_out, 16)
                for k, ((v, r), f, at) in enumerate(halves):
                    dve.wait_ge(v_ready, 2 * (k + 1))
                    dve.wait_ge(split_a, k + 1)
                    nc.vector.tensor_tensor(r, v, Xg[:, :, at:at + D1], ALU.subtract).then_inc(split_d, 1)
                for k, ((v, r), f, at) in enumerate(halves):
                    dve.wait_ge(split_d, k + 1)
                    dve.wait_ge(split_a, k + 3)
                    nc.vector.tensor_tensor(Xg[:, :, at + 2 * D1:at + 3 * D1], r, Xg[:, :, at + D1:at + 2 * D1],
                                            ALU.subtract).then_inc(split_d, 1)
                masks(dve, 9, T)

        ACT_TILES = [1, 2, 3, 4, 5, 7, 8, 9, 10, 11]
        NA = len(ACT_TILES)
        s_ready, u_ready, u_free, acc_full, acc_free, y_full, y_free = (sem(f"at_{n}") for n in (
            "s_ready", "u_ready", "u_free", "acc_full", "acc_free", "y_full", "y_free"))
        Sv = S34.rearrange("p (t h) c -> p t h c", h=H)
        YDv = YD.rearrange("p (t h) c -> p t h c", h=H)
        x1_ready = sem("at_x1_ready")
        alike = region(143, (T, C), F32)
        U0 = 2 * T
        PAIRS = H // 2 - 1
        YT = (0, 5)
        with nc.Block() as block:
            @block.sync
            def _(sp):
                with sp.Fori(0, PAIRS) as i:
                    for hh in range(2):
                        sp.wait_ge(u_ready, 2 * T * i + (U0 + T * (hh + 1)))
                        sp.dma_start(siB[:, hh, :], s_bcast[bass.ds(2 * i + (hh + 2), 1), :].squeeze(0)
                                     .partition_broadcast(P)).then_inc(si_in[hh], 16)

            @block.gpsimd
            def _(pool):
                nc.gpsimd.tensor_scalar(xr[:], xr[:], -1.0, None, ALU.add).then_inc(x1_ready, 1)
                pool.wait_ge(y_free, T + 1)
                nc.gpsimd.tensor_scalar(emp[:], deg[:], 0.0, 1.0 / N, ALU.is_equal, ALU.mult).then_inc(x1_ready, 1)
                pool.wait_ge(x1_ready, 2)
                nc.gpsimd.tensor_tensor(alike, hsum[:].unsqueeze(1).to_broadcast([P, T, C]),
                                        emp[:].unsqueeze(2).to_broadcast([P, T, C]), ALU.mult).then_inc(x1_ready, 1)
                pool.wait_ge(x1_ready, 3)
                nc.gpsimd.tensor_tensor(xn[:], xn[:], alike, ALU.add).then_inc(x1_ready, 1)
                pool.wait_ge(x1_ready, 4)

            @block.scalar
            def _(act):
                nc.scalar.preload_act_table(ACT.Exp)

                def head(h, hh, trip):
                    act.wait_ge(si_in[hh], 16 * trip + 16)
                    for k, t in enumerate(ACT_TILES):
                        back = ACT_TILES[k - SR] + 1 if k >= SR else ACT_TILES[k - SR + NA] + 1 - T
                        act.wait_ge(u_ready, T * h + (U0 + back))
                        nc.scalar.activation(S[k % SR], siB[:, hh, :], ACT.Identity,
                                             bias=sc[:, t, bass.ds(h + H, 1)]).then_inc(s_ready, 1)

                head(0, 0, 0)
                with act.Fori(0, PAIRS) as i:
                    head(2 * i + 1, 1, i)
                    head(2 * i + 2, 0, i + 1)
                head(H - 1, 1, H // 2 - 1)

            @block.vector
            def _(dve):
                dve.sem_inc(u_ready, U0)
                dve.sem_inc(acc_free, 2)
                dve.sem_inc(y_free, 1)

                def take_y(m):
                    dve.wait_ge(y_full, m + 1)
                    yb = psum[:, 6, 0:H * 52].rearrange("p (h c) -> p h c", h=H)
                    nc.vector.tensor_reduce(
                        YDv[:, bass.ds(m, 1), :, :].squeeze(1),
                        yb[:, :, 0:PARTS * D1].rearrange("p h (k c) -> p h c k", k=PARTS), AX,
                        ALU.add)
                    nc.vector.tensor_copy(deg[:, bass.ds(m, 1)], yb[:, 0, 51:52]).then_inc(y_free, 1)

                def take_head(h, hh):
                    dve.wait_ge(acc_full, h + 1)
                    for b in range(3):
                        out_ = Sv[:, 4 * b:4 * b + 4, bass.ds(h, 1), :].squeeze(2)\
                            .rearrange("p t (f c) -> p t f c", f=2)
                        acc = psum[:, 3 * hh + b, :].rearrange("p (t c) -> p t c", t=4)
                        for f, at in enumerate((X_B, X_D)):
                            last = nc.vector.tensor_reduce(
                                out_[:, :, f, :], acc[:, :, at:at + PARTS * D1]
                                .rearrange("p t (k c) -> p t c k", k=PARTS), AX, ALU.add)
                    last.then_inc(acc_free, 1)

                def head(h, hh, trip, before, ys):
                    dve.wait_ge(si_in[hh], 16 * trip + 16)
                    for t in range(T):
                        if before is None and t >= LATE:
                            nc.vector.tensor_scalar(M[:, t, :], MB[:, t, :], 0.0, None, ALU.is_equal).then_inc(m_dve, 1)
                        dve.wait_ge(u_free, T * h + (t + 1))
                        if t in ACT_TILES:
                            k = ACT_TILES.index(t)
                            dve.wait_ge(s_ready, NA * h + (k + 1))
                            nc.vector.tensor_tensor(U[:, t % 4, :], S[k % SR], MB[:, t, :],
                                                    ALU.is_gt).then_inc(u_ready, 1)
                        else:
                            nc.vector.scalar_tensor_tensor(
                                U[:, t % 4, :], siB[:, hh, :], nsj[:, t, bass.ds(h, 1)], M[:, t, :],
                                ALU.is_gt, ALU.mult).then_inc(u_ready, 1)
                        if ys and t - 5 in YT:
                            take_y(ys[YT.index(t - 5)])
                        if before is not None and t == 4:
                            take_head(before, 1 - hh)

                head(0, 0, 0, None, None)
                with dve.Fori(0, PAIRS) as i:
                    head(2 * i + 1, 1, i, 2 * i, (4 * i, 4 * i + 1))
                    head(2 * i + 2, 0, i + 1, 2 * i + 1, (4 * i + 2, 4 * i + 3))
                head(H - 1, 1, H // 2 - 1, H - 2, None)
                take_head(H - 1, 1)

            @block.tensor
            def _(pe):
                pe.sem_inc(u_free, 4)

                def masked(m):
                    pe.wait_ge(y_free, m + 1)
                    for j in range(T):
                        y = nc.tensor.matmul(psum[:, 6, 0:H * 52], M[:, j, bass.ds(m * P, P)],
                                             X[:, j, :, X_D:X_D + 52], start=(j == 0), stop=(j == T - 1))
                    y.then_inc(y_full, 1)

                def head(h, hh, ys):
                    pe.wait_ge(acc_free, h + 1)
                    for t in range(T):
                        pe.wait_ge(u_ready, T * h + (U0 + t + 1))
                        for b in range(T):
                            last = nc.tensor.matmul(
                                psum[:, 3 * hh + b // 4, P * (b % 4):P * (b % 4) + 2 * PARTS * D1],
                                U[:, t % 4, P * b:P * b + P],
                                X[:, t, bass.ds(h, 1), 0:2 * PARTS * D1].squeeze(1),
                                start=(t == 0 and b % 4 == 0), stop=(t == T - 1), skip_group_check=True)
                        last.then_inc(u_free, 1)
                        if ys and t in YT:
                            masked(ys[YT.index(t)])
                    nc.tensor.matmul(psum[:, 7, 0:2], onesb[:], onesb[:, 0:2], start=True,
                                     stop=True).then_inc(acc_full, 1)

                head(0, 0, None)
                pe.wait_ge(m_dve, T - LATE)
                with pe.Fori(0, PAIRS) as i:
                    head(2 * i + 1, 1, (4 * i, 4 * i + 1))
                    head(2 * i + 2, 0, (4 * i + 2, 4 * i + 3))
                head(H - 1, 1, None)

        M2 = region(72, (T, N), BF16)
        stage2 = [region(kb, (N,), I32) for kb in (48, 54, 60, 66, 132, 138, 144, 150, 156, 162)]
        S2 = len(stage2)
        m2_made, adj2_in = sem("m2_made"), [sem(f"adj2_in{k}") for k in range(T // 2)]
        gw_in, w_in = sem("gw_in"), sem("w_in")
        gates_w, gates_b = sb("gates_w", [P, E], F32), sb("gates_b", [P, E], F32)
        route_i = sb("route_i", [GROUPS, 1], I32)
        Wexp = region(0, (E, 3 * HID), F32)

        def load_adjacency2(sp, a, b):
            for t in range(a, b):
                if t >= S2:
                    sp.wait_ge(m2_made, t - S2 + 1)
                sp.dma_start(stage2[t % S2], adjT[P * t:P * t + P, :]).then_inc(adj2_in[t // 2], 16)

        c2, elu_e = sem("p2_chain"), sem("p2_elu")
        dD, dA = region(126, (T * H,), F32), region(127, (T * H,), F32)
        G, mins = T * H // 3, [0]
        Q = 3
        num = region(108, (T * H, D), F32)
        tmp = region(114, (T * H, D), F32)
        e1 = region(120, (T * H, D), F32)
        with nc.Block() as block:
            @block.vector
            def _(dve):
                n = [0]

                def link(ins):
                    n[0] += 1
                    ins.then_inc(c2, 1)
                    dve.wait_ge(c2, n[0])

                link(nc.vector.tensor_tensor(dD, YD[:, :, D], S34[:, :, R2 - 1], ALU.subtract))
                link(nc.vector.tensor_tensor(dD, dD, fC[:], ALU.mult))
                link(nc.vector.tensor_tensor(dA, S34[:, :, D], fA[:], ALU.mult))
                link(nc.vector.tensor_tensor(dD, dD, dA, ALU.add))
                link(nc.vector.scalar_tensor_tensor(
                    dA.rearrange("p (t h) -> p t h", h=H), emp[:].unsqueeze(2).to_broadcast([P, T, H]),
                    float(N), dD.rearrange("p (t h) -> p t h", h=H), ALU.mult, ALU.add))
                link(nc.vector.reciprocal(dD, dA))
                link(nc.vector.tensor_tensor(fA[:], fA[:], dD, ALU.mult))
                link(nc.vector.tensor_tensor(fC[:], fC[:], dD, ALU.mult))

                base = n[0]
                steps = [0]

                def each(op):
                    for q in range(Q):
                        if steps[0]:
                            dve.wait_ge(c2, base + Q * (steps[0] - 1) + q + 1)
                        op(slice(G * q, G * q + G)).then_inc(c2, 1)
                    steps[0] += 1

                wide = lambda f, g: f[:, g].unsqueeze(2).to_broadcast([P, G, D])
                rows = lambda a: a[:, :, :].rearrange("p t (h d) -> p (t h) d", d=D)
                each(lambda g: nc.vector.tensor_tensor(num[:, g], YD[:, g, 0:D], S34[:, g, D1:R2 - 1], ALU.subtract))
                each(lambda g: nc.vector.tensor_tensor(num[:, g], num[:, g], wide(fC, g), ALU.mult))
                each(lambda g: nc.vector.tensor_tensor(tmp[:, g], S34[:, g, 0:D], wide(fA, g), ALU.mult))
                each(lambda g: nc.vector.tensor_tensor(num[:, g], num[:, g], tmp[:, g], ALU.add))
                each(lambda g: nc.vector.tensor_tensor(num[:, g], num[:, g], rows(xn)[:, g], ALU.add))
                each(lambda g: nc.vector.tensor_scalar(tmp[:, g], num[:, g], 0.0, None, ALU.min))
                last_min = base + Q * steps[0]
                each(lambda g: nc.vector.scalar_tensor_tensor(rows(xr)[:, g], num[:, g], 0.0, rows(xr)[:, g],
                                                              ALU.max, ALU.add))
                mins[0] = last_min
                for q in range(Q):
                    g = slice(G * q, G * q + G)
                    dve.wait_ge(elu_e, q + 1)
                    dve.wait_ge(c2, base + Q * (steps[0] - 1) + q + 1)
                    nc.vector.tensor_tensor(rows(xr)[:, g], rows(xr)[:, g], e1[:, g], ALU.add).then_inc(c2, 1)

            @block.sync
            def _(sp):
                for dst, src in ((gates_w[:], gate_w), (gates_b[:], gate_b.squeeze(0).partition_broadcast(P)),
                                 (route_i[:], route)):
                    sp.dma_start(dst, src).then_inc(gw_in, 16)
                for k, w in enumerate((w1, w2, w3)):
                    sp.dma_start(Wexp[:, :, HID * k:HID * k + HID], w).then_inc(w_in, 16)
                load_adjacency2(sp, 0, 6)

            @block.scalar
            def _(act):
                for q in range(Q):
                    act.wait_ge(c2, mins[0] - Q + q + 1)
                    nc.scalar.activation(e1[:, G * q:G * q + G], tmp[:, G * q:G * q + G], ACT.Exp)\
                        .then_inc(elu_e, 1)
        layernorm(nc, sem, ln_mem, "ln2", sync=lambda sp: load_adjacency2(sp, 6, S2))

        yall = region(144, (SLOT_TILES, C), F32)
        small = bump(120, 132)
        lg = small([P, T, E], F32)
        mx = small([P, T, 8], F32)
        ix = small([P, T, 8], U32)
        ixf = small([P, T, 2], F32)
        OH = small([P, 2, T, E], BF16)
        OHs = small([P, T, E], BF16)
        cnt = small([P, E], F32)
        over = small([P, E, T + 1], F32)
        padded = small([P, E], F32)
        ends = small([P, E], F32)
        rk = small([P, T, E], F32)
        rk2 = small([P, 2, T, E], F32)
        posf = small([P, 2, T], F32)
        pos = sb("pos", [P, 2, T], I32)
        wts = sb("wts", [P, 2, T], F32)
        e2 = small([P, T], F32)
        se = small([1, SLOT_TILES, E], F32)
        ef = small([1, SLOT_TILES], F32)
        eslot = sb("eslot", [1, SLOT_TILES], I32)
        route_f = small([GROUPS, 1], F32)
        OHg = small([GROUPS, E], BF16)
        gcnt = small([GROUPS, E], F32)
        gover = small([GROUPS, E, GROUPS // GPT + 1], F32)
        gpad = small([GROUPS, E], F32)
        gend = small([GROUPS, E], F32)
        grk = small([GROUPS, E], F32)
        gpos = small([GROUPS, 1], F32)
        gpos_i = sb("gpos_i", [1, GROUPS], I32)
        gef = small([1, FT], F32)
        ge = sb("ge", [1, FT], I32)
        scattered, c3 = sem("scattered"), sem("p3_c")
        lg_ps, oh_ready, rk_ps, pos_ready, d_e2, e2_ready, g_oh, g_ps, g_col, g_row = (sem(f"p3_{n}") for n in (
            "lg_ps", "oh", "rk_ps", "pos", "d", "e2", "g_oh", "g_ps", "g_col", "g_row"))
        with nc.Block() as block:
            @block.sync
            def _(sp):
                load_adjacency2(sp, S2, T)

            @block.tensor
            def _(pe):
                pe.wait_ge(gw_in, 48)
                for t in range(T):
                    last = nc.tensor.matmul(psum[:, 0, E * t:E * t + E], xT[:, P * t:P * t + P], gates_w[:],
                                            start=(t == 0), stop=True, skip_group_check=True)
                last.then_inc(lg_ps, 1)
                pe.wait_ge(g_oh, 1)
                nc.tensor.matmul(psum[0:GROUPS, 3, 0:E], trib[0:GROUPS, 0:GROUPS], OHg[:], start=True, stop=True)
                nc.tensor.matmul(psum[0:GROUPS, 4, 0:E], onesb[0:GROUPS, 0:GROUPS], OHg[:], start=True,
                                 stop=True).then_inc(g_ps, 1)
                pe.wait_ge(oh_ready, 1)
                nc.tensor.matmul(psum[:, 1, 0:T * E], trib[:], OHs[:, :, :].rearrange("p t e -> p (t e)"),
                                 start=True, stop=False, skip_group_check=True)
                for d in range(1, T):
                    nc.tensor.matmul(psum[:, 1, d * E:T * E], onesb[:],
                                     OHs[:, 0:T - d, :].rearrange("p t e -> p (t e)"), start=False,
                                     stop=(d == T - 1), skip_group_check=True)
                for t in range(T):
                    last = nc.tensor.matmul(psum[:, 2, 0:E], onesb[:], OHs[:, t, :], start=(t == 0),
                                            stop=(t == T - 1))
                last.then_inc(rk_ps, 1)
                pe.wait_ge(g_col, 1)
                nc.tensor.matmul(psum[0:1, 5, 0:GROUPS], gpos[:], cst[0:GROUPS, K_ID:K_ID + GROUPS], start=True,
                                 stop=True).then_inc(g_row, 1)

            @block.scalar
            def _(act):
                act.wait_ge(d_e2, 1)
                nc.scalar.activation(e2[:], e2[:], ACT.Exp).then_inc(e2_ready, 1)

            @block.vector
            def _(dve):
                n = [0]

                def link(ins):
                    n[0] += 1
                    ins.then_inc(c3, 1)
                    dve.wait_ge(c3, n[0])

                dve.wait_ge(gw_in, 48)
                link(nc.vector.tensor_copy(route_f[:], route_i[:]))
                nc.vector.tensor_scalar(OHg[:], cst[0:GROUPS, K_IOTA:K_IOTA + E], route_f[:], None,
                                        ALU.is_equal).then_inc(g_oh, 1)
                dve.wait_ge(lg_ps, 1)
                link(nc.vector.tensor_tensor(lg[:], psum[:, 0, 0:T * E].rearrange("p (t e) -> p t e", t=T),
                                             gates_b[:].unsqueeze(1).to_broadcast([P, T, E]), ALU.add))
                for t in range(T):
                    last = nc.vector.max(mx[:, t, :], lg[:, t, :])
                link(last)
                for t in range(T):
                    last = nc.vector.max_index(ix[:, t, :], mx[:, t, :], lg[:, t, :])
                link(last)
                link(nc.vector.tensor_copy(ixf[:], ix[:, :, 0:2]))
                iota = cst[:, K_IOTA:K_IOTA + E].unsqueeze(1).to_broadcast([P, T, E])
                for k in range(2):
                    link(nc.vector.tensor_tensor(OH[:, k, :, :], iota,
                                                 ixf[:, :, k:k + 1].to_broadcast([P, T, E]), ALU.is_equal))
                nc.vector.tensor_tensor(OHs[:], OH[:, 0, :, :], OH[:, 1, :, :], ALU.add).then_inc(oh_ready, 1)
                nc.vector.tensor_tensor(e2[:], mx[:, :, 1], mx[:, :, 0], ALU.subtract).then_inc(d_e2, 1)
                dve.wait_ge(rk_ps, 1)
                link(nc.vector.tensor_copy(cnt[:], psum[:, 2, 0:E]))
                link(nc.vector.tensor_tensor(over[:], cnt[:].unsqueeze(2).to_broadcast([P, E, T + 1]),
                                             cst[:, K_SLOT:K_SLOT + T + 1].unsqueeze(1)
                                             .to_broadcast([P, E, T + 1]), ALU.is_gt))
                link(nc.vector.tensor_reduce(padded[:], over[:], AX, ALU.add))
                link(nc.vector.tensor_scalar(padded[:], padded[:], float(P), None, ALU.mult))
                link(nc.vector.tensor_tensor_scan(ends[:], onesf[:, 0:E], padded[:], 0.0, ALU.mult, ALU.add))
                link(nc.vector.tensor_tensor(padded[:], ends[:], padded[:], ALU.subtract))
                link(nc.vector.tensor_tensor(rk[:], psum[:, 1, 0:T * E].rearrange("p (t e) -> p t e", t=T),
                                             padded[:].unsqueeze(1).to_broadcast([P, T, E]), ALU.add))
                for k in range(2):
                    link(nc.vector.tensor_tensor(rk2[:, k, :, :], OH[:, k, :, :], rk[:], ALU.mult))
                link(nc.vector.tensor_reduce(posf[:, :, :].rearrange("p k t -> p (k t)"),
                                             rk2[:, :, :, :].rearrange("p k t e -> p (k t) e"), AX, ALU.add))
                nc.vector.tensor_copy(pos[:], posf[:]).then_inc(pos_ready, 1)
                link(nc.vector.tensor_tensor(se[:], ends[0:1, :].unsqueeze(1).to_broadcast([1, SLOT_TILES, E]),
                                             cst[0:1, K_SLOT:K_SLOT + SLOT_TILES].unsqueeze(2)
                                             .to_broadcast([1, SLOT_TILES, E]), ALU.is_le))
                link(nc.vector.tensor_reduce(ef[:], se[:], AX, ALU.add))
                link(nc.vector.tensor_scalar(eslot[:], ef[:], float(E - 1), None, ALU.min))
                dve.wait_ge(e2_ready, 1)
                link(nc.vector.tensor_scalar(wts[:, 0, :], e2[:], 1.0, None, ALU.add))
                link(nc.vector.reciprocal(wts[:, 0, :], wts[:, 0, :]))
                link(nc.vector.tensor_tensor(wts[:, 1, :], wts[:, 0, :], e2[:], ALU.mult))
                dve.wait_ge(g_ps, 1)
                link(nc.vector.tensor_scalar(gcnt[:], psum[0:GROUPS, 4, 0:E], float(GT), None, ALU.mult))
                nk = GROUPS // GPT + 1
                link(nc.vector.tensor_tensor(gover[:], gcnt[:].unsqueeze(2).to_broadcast([GROUPS, E, nk]),
                                             cst[0:GROUPS, K_FT:K_FT + nk].unsqueeze(1)
                                             .to_broadcast([GROUPS, E, nk]), ALU.is_gt))
                link(nc.vector.tensor_reduce(gpad[:], gover[:], AX, ALU.add))
                link(nc.vector.tensor_scalar(gpad[:], gpad[:], float(TS), None, ALU.mult))
                link(nc.vector.tensor_tensor_scan(gend[:], onesf[0:GROUPS, 0:E], gpad[:], 0.0, ALU.mult, ALU.add))
                link(nc.vector.tensor_tensor(gpad[:], gend[:], gpad[:], ALU.subtract))
                link(nc.vector.scalar_tensor_tensor(grk[:], psum[0:GROUPS, 3, 0:E], float(GT), gpad[:], ALU.mult,
                                                    ALU.add))
                link(nc.vector.tensor_tensor(grk[:], grk[:], OHg[:], ALU.mult))
                nc.vector.tensor_reduce(gpos[:], grk[:], AX, ALU.add).then_inc(g_col, 1)
                link(nc.vector.tensor_tensor(se[:, 0:FT, :], gend[0:1, :].unsqueeze(1).to_broadcast([1, FT, E]),
                                             cst[0:1, K_FT:K_FT + FT].unsqueeze(2).to_broadcast([1, FT, E]),
                                             ALU.is_le))
                link(nc.vector.tensor_reduce(gef[:], se[:, 0:FT, :], AX, ALU.add))
                link(nc.vector.tensor_scalar(ge[:], gef[:], float(E - 1), None, ALU.min))
                dve.wait_ge(g_row, 1)
                link(nc.vector.tensor_copy(gpos_i[:], psum[0:1, 5, 0:GROUPS]))
                for t in range(T):
                    dve.wait_ge(adj2_in[t // 2], 32)
                    nc.vector.tensor_scalar(M2[:, t, :], stage2[t % S2], 0.0, None, ALU.is_gt).then_inc(m2_made, 1)

            @block.gpsimd
            def _(pool):
                pool.wait_ge(pos_ready, 1)
                for t in range(T):
                    for k in range(2):
                        nc.gpsimd.indirect_dma_start(
                            slots_in, bass.IndirectOffsetOnAxis(ap=pos[:, k, t:t + 1].bitcast(U32), axis=0),
                            xn[:, t, :], None).then_inc(scattered, 16)
                pool.wait_ge(scattered, 16 * 2 * T)

        xs = region(60, (RING, P), F32)
        xsT = region(62, (2, P), F32)
        sil = region(63, (2, HID), F32)
        hid = region(65, (2, HID), F32)
        wring = region(108, (RING, 3 * HID), F32)
        xs_in = [sem(f"xs_in{k}") for k in range(RING)]
        turned, multiplied, y_made, xt_ready, sil_ready, hid_ready, y_ready, w_ready, y_out = (
            sem(f"p4_{n}") for n in ("turned", "multiplied", "y_made", "xt", "sil", "hid", "y", "w", "y_out"))
        PASSES = (SLOT_TILES - 4) // RING
        slots_v = slots_in.rearrange("(s p) c -> p s c", p=P)
        out_v = slots_out.rearrange("(s p) c -> p s c", p=P)
        with nc.Block() as block:
            @block.sync
            def _(sp):
                for k in range(RING):
                    sp.dma_start(xs[:, k, :], slots_v[:, k, :]).then_inc(xs_in[k], 16)
                with sp.Fori(0, SLOT_TILES // RING - 1) as i:
                    for k in range(RING):
                        sp.wait_ge(turned, RING * i + k + 1)
                        sp.dma_start(xs[:, k, :], slots_v[:, bass.ds(RING * i + (RING + k), 1), :].squeeze(1))\
                            .then_inc(xs_in[k], 16)

            @block.tensor
            def _(pe):
                pe.sem_inc(multiplied, 2)
                pe.sem_inc(y_made, RING)
                pe.wait_ge(w_in, 48)

                def turn(n, k, trip):
                    pe.wait_ge(xs_in[k], 16 * trip + 16)
                    pe.wait_ge(xt_ready, n + 1)
                    nc.tensor.transpose(psum[:, k % 2, 0:P], xs[:, k, :], ident).then_inc(turned, 1)

                def hidden(n, k):
                    pe.wait_ge(xt_ready, n + (2 + 1))
                    pe.wait_ge(w_ready, n + 1)
                    pe.wait_ge(hid_ready, n + 1)
                    for m in range(4):
                        last = nc.tensor.matmul(psum[:, 2 + k % 2, P * m:P * m + P], wring[:, k, P * m:P * m + P],
                                                xsT[:, k % 2, :], start=True, stop=True, skip_group_check=True)
                    last.then_inc(multiplied, 1)

                def outputs(n, k):
                    pe.wait_ge(hid_ready, n + (2 + 1))
                    pe.wait_ge(y_ready, n + 1)
                    for m in range(KC):
                        last = nc.tensor.matmul(psum[:, 4 + k % 2, 0:C], hid[:, k % 2, P * m:P * m + P],
                                                wring[:, k, 2 * HID + C * m:2 * HID + C * m + C],
                                                start=(m == 0), stop=(m == KC - 1))
                    last.then_inc(y_made, 1)

                turn(0, 0, 0)
                turn(1, 1, 0)
                hidden(0, 0)
                with pe.Fori(0, PASSES) as i:
                    for j in range(RING):
                        turn(RING * i + (2 + j), (2 + j) % RING, i + (2 + j) // RING)
                        hidden(RING * i + (1 + j), (1 + j) % RING)
                        outputs(RING * i + j, j)
                for n in range(SLOT_TILES - 2, SLOT_TILES + 2):
                    if n < SLOT_TILES:
                        turn(n, n % RING, n // RING)
                    if n - 1 < SLOT_TILES:
                        hidden(n - 1, (n - 1) % RING)
                    outputs(n - 2, (n - 2) % RING)

            @block.scalar
            def _(act):
                nc.scalar.preload_act_table(ACT.Silu)
                act.sem_inc(xt_ready, 2)
                act.sem_inc(y_ready, 2)

                def turn(n, k):
                    act.wait_ge(turned, n + 1)
                    act.wait_ge(multiplied, n + 1)
                    nc.scalar.activation(xsT[:, k % 2, :], psum[:, k % 2, 0:P], ACT.Copy).then_inc(xt_ready, 1)

                def hidden(n, k):
                    act.wait_ge(multiplied, n + (2 + 1))
                    act.wait_ge(hid_ready, n + 1)
                    nc.scalar.activation(sil[:, k % 2, :], psum[:, 2 + k % 2, 0:HID], ACT.Silu)\
                        .then_inc(sil_ready, 1)

                def outputs(n, k):
                    act.wait_ge(y_made, n + (RING + 1))
                    nc.scalar.activation(yall[:, bass.ds(n, 1), :].squeeze(1), psum[:, 4 + k % 2, 0:C],
                                         ACT.Copy).then_inc(y_ready, 1)
                    if k == RING - 1:
                        act.wait_ge(y_ready, n + (2 + 1))
                        act.dma_start(out_v[:, bass.ds(n - (RING - 1), RING), :],
                                      yall[:, bass.ds(n - (RING - 1), RING), :]).then_inc(y_out, 16)

                turn(0, 0)
                turn(1, 1)
                hidden(0, 0)
                with act.Fori(0, PASSES) as i:
                    for j in range(RING):
                        turn(RING * i + (2 + j), (2 + j) % RING)
                        hidden(RING * i + (1 + j), (1 + j) % RING)
                        outputs(RING * i + j, j)
                for n in range(SLOT_TILES - 2, SLOT_TILES + 2):
                    if n < SLOT_TILES:
                        turn(n, n % RING)
                    if n - 1 < SLOT_TILES:
                        hidden(n - 1, (n - 1) % RING)
                    outputs(n - 2, (n - 2) % RING)
                act.wait_ge(y_out, 16 * SLOT_TILES // RING)

            @block.vector
            def _(dve):
                dve.sem_inc(hid_ready, 2)
                dve.wait_ge(w_in, 48)

                def experts(first, count):
                    return nc.values_load_multi_w_load_instructions(
                        eslot[0:1, bass.ds(first, count)], engines=[mybir.EngineType.DVE], min_val=0,
                        max_val=E - 1, skip_runtime_bounds_check_because="clamped when made")[1]

                def weights(n, k, e):
                    dve.wait_ge(y_made, n + 1)
                    nc.vector.tensor_copy(wring[:, k, :], Wexp[:, bass.ds(e, 1), :].squeeze(1)).then_inc(w_ready, 1)

                def hidden(n, k):
                    dve.wait_ge(sil_ready, n + 1)
                    dve.wait_ge(y_made, n + (RING - 2 + 1))
                    nc.vector.tensor_tensor(hid[:, k % 2, :], psum[:, 2 + k % 2, HID:2 * HID],
                                            sil[:, k % 2, :], ALU.mult).then_inc(hid_ready, 1)

                e = experts(0, 2)
                weights(0, 0, e[0])
                weights(1, 1, e[1])
                hidden(0, 0)
                with dve.Fori(0, PASSES) as i:
                    e = experts(i * RING + 2, RING)
                    for j in range(RING):
                        weights(RING * i + (2 + j), (2 + j) % RING, e[j])
                        hidden(RING * i + (1 + j), (1 + j) % RING)
                e = experts(SLOT_TILES - 2, 2)
                for n in range(SLOT_TILES - 2, SLOT_TILES + 1):
                    if n < SLOT_TILES:
                        weights(n, n % RING, e[n - SLOT_TILES + 2])
                    hidden(n - 1, (n - 1) % RING)

        back = region(108, (2, T, C), F32)
        got = [sem(f"got{q}") for q in range(3)]
        comb, comb2, row_stats = sem("p5_comb"), sem("p5_var"), sem("p5_stats")
        with nc.Block() as block:
            @block.gpsimd
            def _(pool):
                for t in range(T):
                    for k in range(2):
                        nc.gpsimd.indirect_dma_start(
                            back[:, k, t, :], None, slots_out,
                            bass.IndirectOffsetOnAxis(ap=pos[:, k, t:t + 1].bitcast(U32), axis=0))\
                            .then_inc(got[t // 4], 16)

            @block.vector
            def _(dve):
                for t in range(T):
                    dve.wait_ge(got[t // 4], 16 * 8)
                    nc.vector.scalar_tensor_tensor(xr[:, t, :], back[:, 0, t, :], wts[:, 0, t:t + 1], xr[:, t, :],
                                                   ALU.mult, ALU.add).then_inc(comb, 1)
                    dve.wait_ge(comb, 2 * t + 1)
                    nc.vector.scalar_tensor_tensor(xr[:, t, :], back[:, 1, t, :], wts[:, 1, t:t + 1], xr[:, t, :],
                                                   ALU.mult, ALU.add).then_inc(comb, 1)
                    dve.wait_ge(comb, 2 * t + 2)
                    nc.vector.bn_stats(st[:, t, :], xr[:, t, :]).then_inc(row_stats, 1)
                    dve.wait_ge(row_stats, t + 1)
                    nc.vector.bn_aggr(mv[:, t, :], st[:, t, :]).then_inc(comb2, 1)

        def preload_attention2(sp):
            for dst, src in ((uW_sb[:], uW), (ua_sb[:, 0:1], uas), (ua_sb[:, 1:2], uad)):
                nc.sync.dma_start(dst, src).then_inc(u_in, 16)

        layernorm(nc, sem, ln_mem, "ln3", sync=preload_attention2, stats_made=True)

        V = (region(108, (T, CW), BF16), region(135.25, (T, CW), BF16))
        X1 = region(117, (T, 2 * VS), BF16)
        vr1 = ((region(135.25, (T, V1), F32), region(141.5, (T, V1), F32)),
               (region(108, (T, V1), F32), region(162.25, (T, V1), F32)))
        U1 = region(144.25, (2, T, CW), BF16)
        num1 = region(162.25, (T, V1), F32)
        G1 = (xT, mT)
        Wall = region(0, (E, 4 * HID + 4), F32)
        fsB = region(64.5, (N,), F32)
        early1 = bump(148, 160)
        uas_rep, uad_rep = early1([P, P], F32), early1([P, P], F32)
        gmax, tAC, fdg = early1([P, 4], F32), early1([P, 3, T], F32), early1([P, T], F32)
        q_w, q_hT, q_hTs, q_fs, q_fd, q_fc, q_hr, q_hsum, q_c, q_fac, q_hrs, q_fss, q_t, q_v, q_sa, q_sd, q_ones, \
            q_fcs, q_hs = (sem(f"p6_{n}") for n in ("w", "hT", "hTs", "fs", "fd", "fc", "hr", "hsum", "c", "fac",
                                               "hrs", "fss", "t", "v", "sa", "sd", "ones", "fcs", "hs"))
        with nc.Block() as block:
            @block.sync
            def _(sp):
                sp.dma_start(Wall, WrT).then_inc(wall_in, 16)

            @block.gpsimd
            def _(pool):
                pool.wait_ge(u_in, 48)
                nc.gpsimd.tensor_scalar(uas_rep, onesf[:], ua_sb[:, 0:1], None, ALU.mult).then_inc(q_w, 1)
                nc.gpsimd.tensor_scalar(uad_rep, onesf[:], ua_sb[:, 1:2], None, ALU.mult).then_inc(q_w, 1)
                nc.gpsimd.memset(X1[:, :, VS - 1:VS], 1.0).then_inc(q_ones, 1)
                nc.gpsimd.memset(X1[:, :, 2 * VS - 1:2 * VS], 1.0).then_inc(q_ones, 1)
                pool.wait_ge(q_ones, 2)

            @block.tensor
            def _(pe):
                pe.wait_ge(u_in, 48)
                for q in range(3):
                    nc.tensor.matmul(psum[:, q, :], uW_sb[:], xT[:, 512 * q:512 * q + 512], start=True,
                                     stop=True).then_inc(q_hT, 1)
                pe.wait_ge(q_w, 2)
                for q in range(3):
                    pe.wait_ge(q_hTs, q + 1)
                    nc.tensor.matmul(psum[:, 3 + q, :], uad_rep, mT[:, 512 * q:512 * q + 512], start=True,
                                     stop=True).then_inc(q_fd, 1)
                for t in range(T):
                    last = nc.tensor.matmul(psum[:, 0, 2 * t:2 * t + 2], mT[:, P * t:P * t + P], ua_sb[:],
                                            start=(t == 0), stop=True, skip_group_check=True)
                last.then_inc(q_fc, 1)
                for t in range(T):
                    last = nc.tensor.transpose(psum[:, (6, 7, 1)[t // 4], P * (t % 4):P * (t % 4) + P],
                                               mT[:, P * t:P * t + P], ident)
                    if t % 4 == 3:
                        last.then_inc(q_hr, 1)
                for q in range(3):
                    if q > 0:
                        pe.wait_ge(q_c, q + 1)
                    nc.tensor.matmul(psum[:, (2, 3, 4)[q], :], uas_rep, mT[:, 512 * q:512 * q + 512],
                                     start=True, stop=True).then_inc(q_fs, 1)
                pe.wait_ge(q_hrs, 3)
                pe.wait_ge(q_c, 3)
                for t in range(T):
                    last = nc.tensor.matmul(psum[:, 5, 0:C], onesf[:], hrow[:, t, :], start=(t == 0),
                                            stop=(t == T - 1))
                last.then_inc(q_hsum, 1)

            @block.scalar
            def _(act):
                nc.scalar.preload_act_table(ACT.Exp)
                for q in range(3):
                    act.wait_ge(q_hT, q + 1)
                    nc.scalar.activation(mT[:, 512 * q:512 * q + 512], psum[:, q, :], ACT.Copy).then_inc(q_hTs, 1)
                for q in range(3):
                    act.wait_ge(q_hr, q + 1)
                    nc.scalar.activation(hrow[:, 4 * q:4 * q + 4, :].rearrange("p t c -> p (t c)"),
                                         psum[:, (6, 7, 1)[q], :], ACT.Copy).then_inc(q_hrs, 1)
                act.wait_ge(q_t, 1)
                nc.scalar.activation(f1[:, 3, :], fdg, ACT.Exp, scale=SLOPE).then_inc(q_fac, 1)
                nc.scalar.activation(f1[:, 1, :], fdg, ACT.Exp).then_inc(q_fac, 1)
                act.wait_ge(q_t, 3)
                nc.scalar.activation(f1[:, 0, :], tAC[:, 0, :], ACT.Exp).then_inc(q_fac, 1)
                nc.scalar.activation(f1[:, 2, :], tAC[:, 1, :], ACT.Exp).then_inc(q_fac, 1)
                for k, at in enumerate((VS, 0)):
                    act.wait_ge(q_v, 2 * (k + 1))
                    nc.scalar.activation(X1[:, :, at:at + V1], vr1[k][0], ACT.Copy).then_inc(q_sa, 1)
                for k, at in enumerate((VS, 0)):
                    act.wait_ge(q_sd, k + 1)
                    nc.scalar.activation(X1[:, :, at + V1:at + 2 * V1], vr1[k][1], ACT.Copy).then_inc(q_sa, 1)
                for q in range(3):
                    act.wait_ge(q_fs, q + 1)
                    nc.scalar.activation(fsB[:, 512 * q:512 * q + 512], psum[:, (2, 3, 4)[q], :],
                                         ACT.Copy).then_inc(q_fss, 1)
                act.wait_ge(q_hsum, 1)
                nc.scalar.activation(hsum[:], psum[:, 5, 0:C], ACT.Copy).then_inc(q_hs, 1)

            @block.vector
            def _(dve):
                for q in range(3):
                    dve.wait_ge(q_fd, q + 1)
                    nc.vector.tensor_reduce(gmax[:, q:q + 1], psum[:, 3 + q, :], AX, ALU.max).then_inc(q_c, 1)
                dve.wait_ge(q_c, 3)
                nc.vector.tensor_reduce(gmax[:, 3:4], gmax[:, 0:3], AX, ALU.max).then_inc(q_c, 1)
                dve.wait_ge(q_c, 4)
                dve.wait_ge(q_fc, 1)
                fc = psum[:, 0, 0:2 * T].rearrange("p (t k) -> p t k", k=2)
                nc.vector.tensor_scalar(fdg, fc[:, :, 1], gmax[:, 3:4], None, ALU.subtract).then_inc(q_t, 1)
                nc.vector.tensor_copy(fdc[:], fc[:, :, 1]).then_inc(q_fcs, 1)
                nc.vector.tensor_scalar(tAC[:, 2, :], fc[:, :, 0], gmax[:, 3:4], None, ALU.add).then_inc(q_fcs, 1)
                dve.wait_ge(q_fcs, 2)
                nc.vector.tensor_scalar(tAC[:, 0, :], tAC[:, 2, :], 1.0 - SLOPE, 0.0, ALU.mult,
                                        ALU.min).then_inc(q_t, 1)
                nc.vector.tensor_scalar(tAC[:, 1, :], tAC[:, 2, :], SLOPE - 1.0, 0.0, ALU.mult,
                                        ALU.min).then_inc(q_t, 1)
                dve.wait_ge(q_hrs, 3)
                halves = tuple(zip(vr1, (f1[:, 3, :], f1[:, 1, :]), (VS, 0)))
                for k, ((v1, r1), f, at) in enumerate(halves):
                    dve.wait_ge(q_fac, k + 1)
                    nc.vector.tensor_tensor(v1[:, :, 0:C], hrow[:], f.unsqueeze(2).to_broadcast([P, T, C]),
                                            ALU.mult).then_inc(q_v, 1)
                    nc.vector.tensor_copy(v1[:, :, C], f).then_inc(q_v, 1)
                for k, ((v1, r1), f, at) in enumerate(halves):
                    dve.wait_ge(q_v, 2 * (k + 1))
                    dve.wait_ge(q_sa, k + 1)
                    nc.vector.tensor_tensor(r1, v1, X1[:, :, at:at + V1], ALU.subtract).then_inc(q_sd, 1)
                for k, ((v1, r1), f, at) in enumerate(halves):
                    dve.wait_ge(q_sd, k + 1)
                    dve.wait_ge(q_sa, k + 3)
                    nc.vector.tensor_tensor(X1[:, :, at + 2 * V1:at + 3 * V1], r1, X1[:, :, at + V1:at + 2 * V1],
                                            ALU.subtract).then_inc(q_sd, 1)

        z_m = sem("z_m")
        z_t, z_u, z_v, z_used, z_full, z_g, z_gfree = (sem(f"z_{n}") for n in (
            "t", "u", "v", "used", "full", "g", "gfree"))
        CT = CW // P
        w_c, w_n, w_e = sem("p6_wc"), sem("p6_wn"), sem("p6_we")
        with nc.Block() as block:
            @block.vector
            def _(dve):
                dve.sem_inc(z_gfree, 2)

                def sums(n):
                    dve.wait_ge(z_g, n + (CT + 1))
                    nc.vector.tensor_reduce(num1[:, n, :],
                                            G1[n % 2][:, 0:2 * PARTS * V1].rearrange("p (k c) -> p c k", c=V1), AX,
                                            ALU.add).then_inc(z_gfree, 1)

                links = [0]

                def link(ins):
                    links[0] += 1
                    ins.then_inc(w_c, 1)
                    dve.wait_ge(w_c, links[0])

                def rows(c):
                    ts = slice(CT * c, CT * c + CT)
                    for k in range(CT):
                        sums(CT * c + k)
                    dve.wait_ge(z_gfree, 2 + CT * (c + 1))
                    link(nc.vector.tensor_tensor(emp[:, ts], dg[:, 0, ts], dg[:, 1, ts], ALU.add))
                    link(nc.vector.tensor_scalar(emp[:, ts], emp[:, ts], 0.0, None, ALU.is_equal))
                    link(nc.vector.scalar_tensor_tensor(deg[:, ts], emp[:, ts], float(N), num1[:, ts, C], ALU.mult,
                                                        ALU.add))
                    link(nc.vector.reciprocal(deg[:, ts], deg[:, ts]))
                    for t in range(CT * c, CT * c + CT):
                        last = nc.vector.scalar_tensor_tensor(hrow[:, t, :], hsum[:], emp[:, t:t + 1],
                                                              num1[:, t, 0:C], ALU.mult, ALU.add)
                    link(last)
                    link(nc.vector.tensor_tensor(hrow[:, ts, :], hrow[:, ts, :],
                                                 deg[:, ts].unsqueeze(2).to_broadcast([P, CT, C]), ALU.mult))
                    nc.vector.tensor_scalar(xn[:, ts, :], hrow[:, ts, :], 0.0, None, ALU.min).then_inc(w_n, 1)
                    link(nc.vector.scalar_tensor_tensor(xr[:, ts, :], hrow[:, ts, :], 0.0, xr[:, ts, :], ALU.max,
                                                        ALU.add))

                def finish(c):
                    ts = slice(CT * c, CT * c + CT)
                    dve.wait_ge(w_e, c + 1)
                    link(nc.vector.scalar_tensor_tensor(xr[:, ts, :], xn[:, ts, :], -1.0, xr[:, ts, :], ALU.add,
                                                        ALU.add))
                    for t in range(CT * c, CT * c + CT):
                        last = nc.vector.bn_stats(st[:, t, :], xr[:, t, :])
                    link(last)
                    for t in range(CT * c, CT * c + CT):
                        last = nc.vector.bn_aggr(mv[:, t, :], st[:, t, :])
                    link(last)

                for c in range(N // CW):
                    hh, cols_ = c % 2, slice(CW * c, CW * c + CW)
                    for h in range(2):
                        ts = slice(6 * h, 6 * h + 6)
                        dve.wait_ge(z_t, T * c + 6 * h + 6)
                        nc.vector.tensor_scalar(U1[:, hh, ts, :], U1[:, hh, ts, :], 0.0, None,
                                                ALU.is_gt).then_inc(z_m, 1)
                        dve.wait_ge(z_m, 2 * c + h + 1)
                        nc.vector.tensor_tensor(U1[:, hh, ts, :], U1[:, hh, ts, :], M2[:, ts, cols_],
                                                ALU.mult).then_inc(z_u, 1)
                        dve.wait_ge(z_u, 2 * c + h + 1)
                        nc.vector.tensor_tensor(V[hh][:, ts, :], M2[:, ts, cols_], U1[:, hh, ts, :],
                                                ALU.subtract).then_inc(z_v, 1)
                    if c > 0:
                        rows(c - 1)
                    if c > 1:
                        finish(c - 2)
                rows(N // CW - 1)
                finish(N // CW - 2)
                finish(N // CW - 1)

            @block.tensor
            def _(pe):
                pe.sem_inc(z_used, 2)
                with pe.Fori(0, 2) as i:
                    for hh in range(2):
                        for k in range(CT):
                            pe.wait_ge(z_g, 2 * CT * i + (CT * hh + k + 1))
                            for t in range(T):
                                if k == 0 and t % 6 == 0:
                                    pe.wait_ge(z_v, 4 * i + (2 * hh + t // 6 + 1))
                                nc.tensor.matmul(psum[:, 2 * k, 0:VS], U1[:, hh, t, P * k:P * k + P],
                                                 X1[:, t, 0:VS], start=(t == 0), stop=(t == T - 1),
                                                 skip_group_check=True)
                                last = nc.tensor.matmul(psum[:, 2 * k + 1, 0:VS], V[hh][:, t, P * k:P * k + P],
                                                        X1[:, t, VS:2 * VS], start=(t == 0), stop=(t == T - 1),
                                                        skip_group_check=True)
                            last.then_inc(z_full, 1)
                        nc.tensor.matmul(psum[:, 7, 0:2], onesb[:], onesb[:, 0:2], start=True,
                                         stop=True).then_inc(z_used, 1)

            @block.scalar
            def _(act):
                act.sem_inc(z_g, CT)

                def scores(c):
                    act.wait_ge(z_used, c + 1)
                    for t in range(T):
                        nc.scalar.activation(U1[:, c % 2, t, :], fsB[:, CW * c:CW * c + CW], ACT.Identity,
                                             bias=fdc[:, t:t + 1]).then_inc(z_t, 1)

                def exps(c):
                    ts = slice(CT * c, CT * c + CT)
                    act.wait_ge(w_n, c + 1)
                    nc.scalar.activation(xn[:, ts, :], xn[:, ts, :], ACT.Exp).then_inc(w_e, 1)

                scores(0)
                scores(1)
                for c in range(N // CW):
                    for k in range(CT):
                        n = CT * c + k
                        g = G1[n % 2]
                        act.wait_ge(z_full, n + 1)
                        act.wait_ge(z_gfree, n + 1)
                        for m in range(2):
                            nc.scalar.activation(dg[:, m, n:n + 1], psum[:, 2 * k + m, VS - 1:VS], ACT.Copy)
                        nc.scalar.activation(g[:, 0:VS - 1], psum[:, 2 * k, 0:VS - 1], ACT.Copy,
                                             scale=f1[:, 0, n:n + 1])
                        nc.scalar.activation(g[:, VS - 1:2 * VS - 2], psum[:, 2 * k + 1, 0:VS - 1], ACT.Copy,
                                             scale=f1[:, 2, n:n + 1]).then_inc(z_g, 1)
                    if c > 0:
                        exps(c - 1)
                    if c + 2 < N // CW:
                        scores(c + 2)
                exps(N // CW - 1)

        xs4 = region(72, (FT * TS,), F32)
        h2s = region(85, (KC, FT * TS), F32)
        h2 = region(110, (KC, N), F32)
        ring = region(123, (RING, 4 * HID + 4), F32)
        h0r = region(139.25, (2, KC, TS), F32)
        h1r = region(141.25, (2, KC, TS), F32)
        late = bump(143.25, 152)
        WsI = late([P, 4 * HID + 4], F32)
        Wi_sb, Wo_sb, bi_sb, boB = (late(k, F32) for k in ([P, HID], [P, KC, C], [P, KC], [P, C]))

        def preload_last(sp):
            for dst, src in ((WsI, WsT), (Wi_sb, WiT), (Wo_sb, WoT), (bi_sb, bi),
                             (boB, bo.squeeze(0).partition_broadcast(P))):
                nc.sync.dma_start(dst, src).then_inc(l_in, 16)

        def clear_slots(pool):
            nc.gpsimd.memset(xs4, 0.0).then_inc(cleared, 1)

        layernorm(nc, sem, ln_mem, "ln4", sync=preload_last, pool=clear_slots, stats_made=True)

        m_h0p, m_h0, m_h1p, m_h1, m_h2p, m_ring, m_wsi, m_out, m_bo, m_perm_d, m_perm_a, \
            m_rows, m_done, m_h2w = (sem(f"m_{n}") for n in (
                "h0p", "h0", "h1p", "h1", "h2p", "ring", "wsi", "out", "bo", "perm_d",
                "perm_a", "rows", "done", "h2w"))
        GB = 8

        def group_starts(eng, b):
            return nc.values_load_multi_w_load_instructions(
                gpos_i[0:1, GB * b:GB * b + GB], engines=[eng], min_val=0, max_val=(FT - 1) * TS + TS - GT,
                skip_runtime_bounds_check_because="below the slots' end as made")[1]

        with nc.Block() as block:
            @block.vector
            def _(dve):
                dve.wait_ge(l_in, 80)
                for l in range(2):
                    for k in range(KC):
                        at = l * KC * HID + k * HID + k * P
                        nc.vector.tensor_tensor(WsI[:, at:at + P], WsI[:, at:at + P], ident,
                                                ALU.add).then_inc(m_wsi, 1)
                for b in range(0, GROUPS // GB, 2):
                    g = group_starts(mybir.EngineType.DVE, b)
                    for j in range(GB):
                        nc.vector.tensor_copy(xs4[:, bass.ds(g[j], GT)],
                                              xT[:, GT * (GB * b + j):GT * (GB * b + j) + GT]).then_inc(m_perm_d, 1)
                dve.wait_ge(m_perm_d, GROUPS // 2)
                dve.wait_ge(m_wsi, 2 * KC)

            @block.scalar
            def _(act):
                for b in range(1, GROUPS // GB, 2):
                    g = group_starts(mybir.EngineType.Activation, b)
                    for j in range(GB):
                        nc.scalar.activation(xs4[:, bass.ds(g[j], GT)],
                                             xT[:, GT * (GB * b + j):GT * (GB * b + j) + GT],
                                             ACT.Copy).then_inc(m_perm_a, 1)
                act.wait_ge(m_perm_a, GROUPS // 2)

            @block.gpsimd
            def _(pool):
                pool.wait_ge(l_in, 80)
                nc.gpsimd.tensor_tensor(xr[:], xr[:], boB.unsqueeze(1).to_broadcast([P, T, C]),
                                        ALU.add).then_inc(m_bo, 1)
                pool.wait_ge(m_bo, 1)

        with nc.Block() as block:
            @block.vector
            def _(dve):
                dve.sem_inc(m_h0, 2)

                def weights(n, k, e):
                    dve.wait_ge(m_h2w, n + 1)
                    nc.vector.tensor_tensor(ring[:, k, :], Wall[:, bass.ds(e, 1), :].squeeze(1), WsI,
                                            ALU.add).then_inc(m_ring, 1)

                def step(n, k):
                    dve.wait_ge(m_h0p, n + 1)
                    dve.wait_ge(m_h1p, n + 1)
                    for m in range(KC):
                        last = nc.vector.tensor_scalar(h0r[:, k % 2, m, :], psum[:, k % 2, TS * m:TS * m + TS],
                                                       bi_sb[:, m:m + 1], 0.0, ALU.add, ALU.max)
                    last.then_inc(m_h0, 1)

                def experts(first, count):
                    return nc.values_load_multi_w_load_instructions(
                        ge[0:1, bass.ds(first, count)], engines=[mybir.EngineType.DVE], min_val=0,
                        max_val=E - 1, skip_runtime_bounds_check_because="clamped when made")[1]

                e = experts(0, 2)
                for n in range(2):
                    weights(n, n, e[n])
                    step(n, n)
                with dve.Fori(0, (FT - 2) // RING) as i:
                    e = experts(i * RING + 2, RING)
                    for j in range(RING):
                        weights(RING * i + (2 + j), (2 + j) % RING, e[j])
                        step(RING * i + (2 + j), (2 + j) % RING)

            @block.tensor
            def _(pe):
                pe.sem_inc(m_h1p, 2)

                def layer(l, k, src, bank):
                    for o in range(KC):
                        for m in range(KC):
                            at = l * KC * HID + m * HID + o * P
                            last = nc.tensor.matmul(psum[:, bank, TS * o:TS * o + TS], ring[:, k, at:at + P],
                                                    src[:, k % 2, m, :], start=(m == 0), stop=(m == KC - 1),
                                                    skip_group_check=True)
                    return last

                def first(n, k):
                    pe.wait_ge(m_h0, n + 1)
                    for m in range(KC):
                        last = nc.tensor.matmul(psum[:, k % 2, TS * m:TS * m + TS], Wi_sb[:, P * m:P * m + P],
                                                xs4[:, bass.ds(n * TS, TS)], start=True, stop=True,
                                                skip_group_check=True)
                    last.then_inc(m_h0p, 1)

                def second(n, k):
                    pe.wait_ge(m_h0, n + (2 + 1))
                    pe.wait_ge(m_ring, n + 1)
                    pe.wait_ge(m_h1, n + 1)
                    layer(0, k, h0r, 2 + k % 2).then_inc(m_h1p, 1)

                def third(n, k):
                    pe.wait_ge(m_h1, n + (2 + 1))
                    pe.wait_ge(m_h2w, n + (RING - 2 + 1))
                    layer(1, k, h1r, 4 + k % 2).then_inc(m_h2p, 1)

                first(0, 0)
                first(1, 1)
                second(0, 0)
                with pe.Fori(0, (FT - 2) // RING) as i:
                    for j in range(RING):
                        n = RING * i + (2 + j)
                        first(n, (2 + j) % RING)
                        second(RING * i + (1 + j), (1 + j) % RING)
                        third(RING * i + j, j % RING)
                second(FT - 1, (FT - 1) % RING)
                third(FT - 2, (FT - 2) % RING)
                third(FT - 1, (FT - 1) % RING)

            @block.scalar
            def _(act):
                act.sem_inc(m_h1, 2)
                act.sem_inc(m_h2w, RING)

                def second(n, k):
                    act.wait_ge(m_h1p, n + (2 + 1))
                    for o in range(KC):
                        last = nc.scalar.activation(h1r[:, k % 2, o, :], psum[:, 2 + k % 2, TS * o:TS * o + TS],
                                                    ACT.Relu, bias=ring[:, k, 4 * HID + o:4 * HID + o + 1])
                    last.then_inc(m_h1, 1)

                def third(n, k):
                    act.wait_ge(m_h2p, n + 1)
                    for o in range(KC):
                        last = nc.scalar.activation(
                            h2s[:, o, bass.ds(n * TS, TS)], psum[:, 4 + k % 2, TS * o:TS * o + TS],
                            ACT.Relu, bias=ring[:, k, 4 * HID + KC + o:4 * HID + KC + o + 1])
                    last.then_inc(m_h2w, 1)

                second(0, 0)
                with act.Fori(0, (FT - 2) // RING) as i:
                    for j in range(RING):
                        second(RING * i + (1 + j), (1 + j) % RING)
                        third(RING * i + j, j % RING)
                second(FT - 1, (FT - 1) % RING)
                third(FT - 2, (FT - 2) % RING)
                third(FT - 1, (FT - 1) % RING)

        with nc.Block() as block:
            @block.vector
            def _(dve):
                for b in range(0, GROUPS // GB, 2):
                    g = group_starts(mybir.EngineType.DVE, b)
                    for j in range(GB):
                        nc.vector.tensor_copy(h2[:, :, GT * (GB * b + j):GT * (GB * b + j) + GT],
                                              h2s[:, :, bass.ds(g[j], GT)]).then_inc(m_perm_d, 1)
                for q in range(3):
                    dve.wait_ge(m_out, q + 1)
                    nc.vector.tensor_tensor(xr[:, 4 * q:4 * q + 4, :], xr[:, 4 * q:4 * q + 4, :],
                                            psum[:, q, :].rearrange("p (t c) -> p t c", c=C),
                                            ALU.add).then_inc(m_rows, 1)

            @block.scalar
            def _(act):
                for b in range(1, GROUPS // GB, 2):
                    g = group_starts(mybir.EngineType.Activation, b)
                    for j in range(GB):
                        nc.scalar.activation(h2[:, :, GT * (GB * b + j):GT * (GB * b + j) + GT],
                                             h2s[:, :, bass.ds(g[j], GT)], ACT.Copy).then_inc(m_perm_a, 1)

            @block.tensor
            def _(pe):
                for t in range(T):
                    if t % 3 == 0:
                        pe.wait_ge(m_perm_d, GROUPS // 2 + GB * (t // 3 + 1))
                        pe.wait_ge(m_perm_a, GROUPS // 2 + GB * (t // 3 + 1))
                    for m in range(KC):
                        last = nc.tensor.matmul(psum[:, t // 4, P * (t % 4):P * (t % 4) + P],
                                                h2[:, m, P * t:P * t + P], Wo_sb[:, m, :], start=(m == 0),
                                                stop=(m == KC - 1), skip_group_check=True)
                    if t % 4 == 3:
                        last.then_inc(m_out, 1)

            @block.sync
            def _(sp):
                out_v = out.rearrange("(t p) c -> p t c", p=P)
                for q in range(3):
                    sp.wait_ge(m_rows, q + 1)
                    sp.dma_start(out_v[:, 4 * q:4 * q + 4, :], xr[:, 4 * q:4 * q + 4, :]).then_inc(m_done, 16)
                sp.wait_ge(m_done, 48)


def constants():
    import numpy as np
    c = np.zeros((P, K_END), np.float32)
    c[:, K_ID:K_ID + P] = np.eye(P)
    c[:, K_TRI:K_TRI + P] = np.triu(np.ones((P, P)), 1)
    c[:, K_HM:K_HM + H] = np.arange(P)[:, None] // D == np.arange(H)[None, :]
    c[:, K_IOTA:K_IOTA + E] = np.arange(E)
    c[:, K_SLOT:K_SLOT + SLOT_TILES] = np.arange(SLOT_TILES) * P
    c[:, K_FT:K_FT + FT] = np.arange(FT) * TS
    return c


def kernel(**inputs):
    import numpy as np
    import concourse.bacc as bacc
    from concourse.bass_utils import run_bass_kernel_spmd

    a = {k: np.asarray(v) for k, v in inputs.items()}
    turned = lambda v, *axes: np.ascontiguousarray(np.transpose(v, axes))
    arrays = {
        "x": a["x"], "adjT": turned(a["adj"], 1, 0),
        "gW": turned(a["L0_gnn_W"], 1, 0), "gb": a["L0_gnn_bW"].reshape(C, 1),
        "ga1": np.tile(a["L0_gnn_a1"], H).reshape(C, 1), "ga2": np.tile(a["L0_gnn_a2"], H).reshape(C, 1),
        "gab": a["L0_gnn_ab"].reshape(1), "gate_w": a["L0_ffn_gate_w"],
        "gate_b": a["L0_ffn_gate_b"].reshape(1, E),
        "w1": turned(a["L0_ffn_w1"], 1, 0, 2), "w2": turned(a["L0_ffn_w2"], 1, 0, 2),
        "w3": turned(a["L0_ffn_w3"].reshape(E, KC, P, C), 2, 0, 1, 3).reshape(P, E, HID),
        "uW": a["L1_gnn_W"], "uas": a["L1_gnn_a_src"], "uad": a["L1_gnn_a_dst"],
        "route": a["L1_ffn_route_id"].reshape(GROUPS, 1),
        "WiT": turned(a["L1_ffn_Wi"], 1, 0), "bi": turned(a["L1_ffn_bi"].reshape(KC, P), 1, 0),
        "WrT": np.concatenate([
            turned(a["L1_ffn_Wr"].reshape(2, E, HID, KC, P), 4, 1, 0, 3, 2).reshape(P, E, 4 * HID),
            turned(a["L1_ffn_br"].reshape(2, E, KC, P), 3, 1, 0, 2).reshape(P, E, 4)], axis=2),
        "WsT": np.concatenate([
            turned(a["L1_ffn_Ws"].reshape(2, HID, KC, P), 3, 0, 2, 1).reshape(P, 4 * HID),
            turned(a["L1_ffn_bs"].reshape(2, KC, P), 2, 0, 1).reshape(P, 4)], axis=1),
        "WoT": turned(a["L1_ffn_Wo"].reshape(C, KC, P), 2, 1, 0), "bo": a["L1_ffn_bo"].reshape(1, C),
        "consts": constants(),
    }
    nc = bacc.Bacc("TRN2", target_bir_lowering=False, num_devices=1)
    maps, args = {}, {}
    for name, v in arrays.items():
        v = np.ascontiguousarray(v)
        maps[f"in_{name}"] = v
        args[name] = nc.dram_tensor(f"in_{name}", v.shape, mybir.dt.from_np(v.dtype), kind="ExternalInput").ap()
    args["out"] = nc.dram_tensor("out_rows", (N, C), F32, kind="ExternalOutput").ap()
    build(nc, **args)
    r = run_bass_kernel_spmd(nc, [maps], core_ids=[0])
    return r.results[0]["out_rows"]
```

```python
from contextlib import ExitStack

import concourse.bass as bass
from concourse import mybir

F32 = mybir.dt.float32
BF16 = mybir.dt.bfloat16
I32 = mybir.dt.int32
U32 = mybir.dt.uint32
ALU = mybir.AluOpType
ACT = mybir.ActivationFunctionType
AX = mybir.AxisListType.X

P = 128
N = 1536
T = N // P
C = 128
H = 8
D = C // H
D1 = D + 1
E = 16
HID = 256
KC = HID // P
PARTS = 3
SLOT_TILES = 40
GROUPS = 64
GT = N // GROUPS
GPT = P // GT
TS = GPT * GT
FT = 26
BIG = 2.0 ** 100
EPS = 1e-5
SLOPE = 0.2

K_ID, K_TRI, K_HM, K_IOTA, K_SLOT, K_FT = 0, 128, 256, 264, 280, 320
K_END = K_FT + FT

HS = 104
X_B, X_D, X_ONE = 0, PARTS * D1, 2 * PARTS * D1
R2 = 2 * D1
V1 = C + 1
VS = PARTS * V1 + 1
ST = 5
RING = 4
CW = 3 * P
LN_TILES = 3
LN_PARTS = T // LN_TILES


def layernorm(nc, signals, mem, n, variance, sync=None, pool_start=None, pool_end=None, dve_start=None,
              gap=None, dve_end=None, act_start=None, act_end=None, pe_start=None, product=None, pe_end=None,
              loaded=None, ident_in=None):
    xr, xn, xT, ident, st, mv, rstd, half, psum = mem
    scale, normed, turned, taken_a, taken_d, stats, var = signals
    scales = 1 + 2 * LN_PARTS

    def third_taken(eng, q):
        if q == 1:
            eng.wait_ge(taken_d, n + 1)
        else:
            eng.wait_ge(taken_a, 2 * n + q // 2 + 1)

    with nc.Block() as block:
        if sync is not None:
            @block.sync
            def _(sp):
                sync(sp)

        @block.vector

        def _(dve):
            if dve_start is not None:
                dve_start(dve)
            if loaded is not None:
                for q in range(3):
                    dve.wait_ge(loaded[q], 16)
                    for t in range(4 * q, 4 * q + 4):
                        nc.vector.bn_stats(st[:, t, :], xr[:, t, :]).then_inc(stats, 1)
                    for t in range(4 * q, 4 * q + 4):
                        dve.wait_ge(stats, t + 1)
                        nc.vector.bn_aggr(mv[:, t, :], st[:, t, :]).then_inc(var, 1)
            if gap is not None:
                gap(dve)
            for t in range(T):
                if t % LN_TILES == 0:
                    dve.wait_ge(scale, scales * n + (1 + 2 * (t // LN_TILES + 1)))
                nc.vector.tensor_scalar(xn[:, t, :], xr[:, t, :], mv[:, t, 0:1], rstd[:, t:t + 1],
                                        ALU.subtract, ALU.mult).then_inc(normed, 1)
            dve.wait_ge(turned, 3 * n + 2)
            nc.vector.tensor_copy(xT[:, 512:1024], psum[:, 1, :]).then_inc(taken_d, 1)
            if dve_end is not None:
                dve_end(dve)

        @block.gpsimd

        def _(pool):
            if pool_start is not None:
                pool_start(pool)
            nc.gpsimd.memset(half[:], -0.5).then_inc(scale, 1)
            for p in range(LN_PARTS):
                part = slice(LN_TILES * p, LN_TILES * p + LN_TILES)
                variance(pool, p)
                nc.gpsimd.tensor_scalar(rstd[:, part], mv[:, part, 1], EPS, None, ALU.add).then_inc(scale, 1)
                pool.wait_ge(scale, scales * n + (2 + 2 * p))
                nc.gpsimd.tensor_tensor(rstd[:, part], rstd[:, part], half[:, part], ALU.pow).then_inc(scale, 1)
            if pool_end is not None:
                pool_end(pool)

        @block.tensor

        def _(pe):
            if pe_start is not None:
                pe_start(pe)
            if ident_in is not None:
                pe.wait_ge(ident_in, 16)
            for t in range(T):
                pe.wait_ge(normed, T * n + t + 1)
                last = nc.tensor.transpose(psum[:, t // 4, P * (t % 4):P * (t % 4) + P], xn[:, t, :], ident)
                if t % 4 == 3:
                    last.then_inc(turned, 1)
            if product is not None:
                for q in range(3):
                    third_taken(pe, q)
                    product(pe, q)
            if pe_end is not None:
                pe_end(pe)

        @block.scalar

        def _(act):
            if act_start is not None:
                act_start(act)
            for q in range(0, T // 4, 2):
                act.wait_ge(turned, 3 * n + q + 1)
                nc.scalar.activation(xT[:, 512 * q:512 * q + 512], psum[:, q, :], ACT.Copy).then_inc(taken_a, 1)
            if act_end is not None:
                act_end(act)


def build(nc, x, adjT, gW, gb, ga1, ga2, gab, gate_w, gate_b, w1, w2, w3, uW, uas, uad,
          route, WiT, bi, WrT, WsT, WoT, bo, consts, out):
    with ExitStack() as ctx:
        def sb(name, shape, dt):
            return ctx.enter_context(nc.sbuf_tensor(name, shape, dt))

        def sem(name):
            return ctx.enter_context(nc.semaphore(name))

        arena = sb("arena", [P, 169 * 256], F32)

        def region(kb, shape, dt):
            n = 1
            for k in shape:
                n *= k
            words = n * (2 if dt == BF16 else 4) // 4
            a = arena[:, int(kb * 256):int(kb * 256) + words]
            if dt != F32:
                a = a.bitcast(dt)
            if len(shape) == 2:
                a = a.rearrange("p (a b) -> p a b", a=shape[0])
            if len(shape) == 3:
                a = a.rearrange("p (a b c) -> p a b c", a=shape[0], b=shape[1])
            return a

        def bump(kb, end):
            at = [kb * 1024]

            def small(shape, dt):
                t = region(at[0] / 1024, tuple(shape[1:]), dt)
                n = 2 if dt == BF16 else 4
                for k in shape[1:]:
                    n *= k
                at[0] += (n + 63) // 64 * 64
                assert at[0] <= end * 1024
                return t[0:shape[0]]
            return small

        psum = ctx.enter_context(nc.psum_tensor("psum", [P, 8, 512], F32))

        cst = sb("cst", [P, K_END], F32)
        xr = sb("xr", [P, T, C], F32)
        xn = sb("xn", [P, T, C], F32)
        xT = sb("xT", [P, N], F32)
        mT = sb("mT", [P, N], F32)
        hrow = sb("hrow", [P, T, C], F32)
        st = sb("st", [P, T, 6], F32)
        mv = sb("mv", [P, T, 2], F32)
        rstd = sb("rstd", [P, T], F32)
        half = sb("half", [P, T], F32)
        onesb = sb("onesb", [P, P], BF16)
        onesf = sb("onesf", [P, P], F32)
        trib = sb("trib", [P, P], BF16)
        ident = cst[:, K_ID:K_ID + P]

        def keep_busy(pe, n, bank):
            with pe.Fori(0, n // 8) as _:
                for k in range(8):
                    nc.tensor.matmul(psum[:, bank, 0:P], onesb[:], onesb[:], start=True, stop=True,
                                     skip_group_check=True)

        ln_signals = [sem(f"ln_{x}") for x in (
            "scale", "normed", "turned", "taken_a", "taken_d", "stats", "var")]
        ln_mem = (xr, xn, xT, ident, st, mv, rstd, half, psum)

        s_bcast = nc.dram_tensor("si_rows", (H, N), F32, kind="Internal").ap()
        slots_in = nc.dram_tensor("slots_in", (SLOT_TILES * P, C), F32, kind="Internal").ap()
        slots_out = nc.dram_tensor("slots_out", (SLOT_TILES * P, C), F32, kind="Internal").ap()

        uW_sb = sb("uW_sb", [P, C], F32)
        ua_sb = sb("ua_sb", [P, 2], F32)
        f1 = sb("f1", [P, 4, T], F32)
        fdc = sb("fdc", [P, T], F32)
        dg = sb("dg", [P, 2, T], F32)
        u_in, wall_in, l_in = sem("u_in"), sem("wall_in"), sem("l_in")
        cleared = sem("cleared")
        zeroed, zero_set = sem("zeroed"), sem("zero_set")
        zero = sb("zero", [P, C], F32)
        x_in, consts_in, weights_in = [sem(f"x_in{q}") for q in range(3)], sem("consts_in"), sem("weights_in")
        adj_in = [sem(f"adj_in{k}") for k in range(ST)]

        M = region(0, (T, N), BF16)
        MB = region(36, (T, N), BF16)
        siB = region(72, (2, N), F32)
        S = [region(84 + 3 * k, (N,), BF16) for k in range(4)]
        for whole in (mT[:, :], hrow[:, :, :].rearrange("p t c -> p (t c)"), xT[:, :]):
            S += [whole.bitcast(BF16)[:, N * k:N * k + N] for k in range(2)]
        SR = len(S)
        U = region(99, (4, N), BF16)
        stage = region(84, (ST, N), I32)
        X = region(117, (T, H, HS), BF16)
        vr = ((region(136.5, (T * H, D1), F32), region(143, (T * H, D1), F32)),
              (region(152, (T * H, D1), F32), region(162.5, (T * H, D1), F32)))
        S34 = region(149.5, (T * H, R2), F32)
        YD = region(162.5, (T * H, D1), F32)

        early = bump(149.5, 152)
        gW_sb = early([P, C], F32)
        cols = sb("cols", [P, 8], F32)
        a16 = sb("a16", [P, 2 * H], F32)
        sc = sb("sc", [P, T, 2 * H], F32)
        gB = sb("gB", [P, 2 * H], F32)
        gcol = sb("gcol", [2 * H, 1], F32)
        gdiag = sb("gdiag", [2 * H, 2 * H], F32)
        srow = region(162.5, (N,), F32)
        sjg = early([P, T, H], F32)
        nsj = sb("nsj", [P, T, H], F32)
        tA = early([P, T, H], F32)
        tC = early([P, T, H], F32)
        fB = sb("fB", [P, T * H], F32)
        fD = early([P, T * H], F32)
        fA = sb("fA", [P, T * H], F32)
        fC = sb("fC", [P, T * H], F32)
        deg = sb("deg", [P, T], F32)
        emp = sb("emp", [P, T], F32)
        hsum = sb("hsum", [P, C], F32)

        si_in = [sem("si_in0"), sem("si_in1")]
        mb_made, dch = sem("mb_made"), sem("p1_dch")
        m_dve, m_act, m_pool = sem("m_dve"), sem("m_act"), sem("m_pool")

        def load_adjacency(sp, a, b):
            for t in range(a, b):
                if t >= ST:
                    sp.wait_ge(mb_made, t - ST + 1)
                sp.dma_start(stage[:, t % ST, :], adjT[P * t:P * t + P, :]).then_inc(adj_in[t % ST], 16)

        LATE = 8

        def masks(dve, a, b):
            for t in range(a, b):
                dve.wait_ge(adj_in[t % ST], 16 * (t // ST + 1))
                nc.vector.tensor_scalar(MB[:, t, :], stage[:, t % ST, :], 0.0, BIG, ALU.is_equal,
                                        ALU.mult).then_inc(mb_made, 1)

        ones_made = sem("ones_made")

        def load_first(sp):
            for q in range(3):
                sp.dma_start(xr[:, 4 * q:4 * q + 4, :],
                             x.rearrange("(t p) c -> p t c", p=P)[:, 4 * q:4 * q + 4, :]).then_inc(x_in[q], 16)
            sp.dma_start(cst[:], consts).then_inc(consts_in, 16)
            load_adjacency(sp, 0, 2)
            for dst, src in ((gW_sb[:], gW), (cols[:, 0:1], gb), (cols[:, 1:2], ga1), (cols[:, 2:3], ga2),
                             (cols[:, 3:4], gab.partition_broadcast(P))):
                sp.dma_start(dst, src).then_inc(weights_in, 16)
            load_adjacency(sp, 2, ST + 4)

        def make_ones(pool):
            nc.gpsimd.memset(onesb[:], 1.0).then_inc(ones_made, 1)
            nc.gpsimd.memset(onesf[:], 1.0).then_inc(ones_made, 1)

        def start_busy(pe):
            pe.wait_ge(ones_made, 1)
            keep_busy(pe, 48, 7)

        def clear_zero(pool):
            nc.gpsimd.memset(zero[:], 0.0).then_inc(zero_set, 1)

        def project1(pe, q):
            if q == 0:
                pe.wait_ge(weights_in, 80)
            nc.tensor.matmul(psum[:, 3 + q, :], gW_sb[:], xT[:, 512 * q:512 * q + 512], start=True, stop=True)\
                .then_inc(hT_ps, 1)

        hT_ps = sem("p1_hT_ps")
        a16_ready, hT_sb, hr_ps, sc_ps, sr_ps, g_ready, gB_ps, hsum_ps, sr_sb, sjg_ready, f_ready, hr_sb, \
            v_ready, split_a, split_d, si_out, hs_ready, sc_ready, ones_ready = (sem(f"p1_{n}") for n in (
                "a16", "hT_sb", "hr_ps", "sc_ps", "sr_ps", "g", "gB_ps", "hsum_ps", "sr_sb", "sjg", "f",
                "hr_sb", "v", "split_a", "split_d", "si_out", "hs", "sc", "ones"))
        Xg = X.rearrange("p t h c -> p (t h) c")

        def first_sync(sp):
            load_first(sp)
            load_adjacency(sp, ST + 4, T - 2)
            sp.wait_ge(sr_sb, 3)
            sp.dma_start(s_bcast, srow[0:H, :]).then_inc(si_out, 16)
            load_adjacency(sp, T - 2, T)
            sp.wait_ge(si_out, 16)
            for hh in range(2):
                sp.dma_start(siB[:, hh, :], s_bcast[hh, :].partition_broadcast(P)).then_inc(si_in[hh], 16)

        def first_pool(pool):
            clear_zero(pool)
            nc.gpsimd.memset(X[:, :, :, X_ONE:HS], 1.0).then_inc(ones_ready, 1)
            pool.wait_ge(consts_in, 16)
            nc.gpsimd.tensor_copy(trib[:], cst[:, K_TRI:K_TRI + P]).then_inc(ones_ready, 1)
            for t in (0, 3, 6):
                pool.wait_ge(mb_made, t + 1)
                nc.gpsimd.tensor_scalar(M[:, t, :], MB[:, t, :], -1.0 / BIG, 1.0, ALU.mult,
                                        ALU.add).then_inc(m_pool, 1)

        def first_pe(pe):
            pe.wait_ge(ones_made, 2)
            pe.wait_ge(weights_in, 80)
            pe.wait_ge(hT_sb, 3)
            pe.wait_ge(a16_ready, 2)
            for q in range(3):
                nc.tensor.matmul(psum[0:2 * H, q, :], a16[:], mT[:, 512 * q:512 * q + 512], start=True,
                                 stop=True).then_inc(sr_ps, 1)
            for t in range(T):
                last = nc.tensor.matmul(psum[:, 6, 2 * H * t:2 * H * t + 2 * H], mT[:, P * t:P * t + P],
                                        a16[:], start=(t == 0), stop=True, skip_group_check=True)
            last.then_inc(sc_ps, 1)
            for t in range(T):
                last = nc.tensor.transpose(psum[:, 3 + t // 4, P * (t % 4):P * (t % 4) + P],
                                           mT[:, P * t:P * t + P], ident)
                if t % 4 == 3:
                    last.then_inc(hr_ps, 1)
            pe.wait_ge(g_ready, 1)
            nc.tensor.matmul(psum[:, 7, 0:2 * H], onesf[0:2 * H, :], gdiag[:], start=True,
                             stop=True).then_inc(gB_ps, 1)
            pe.wait_ge(hr_sb, 3)
            pe.wait_ge(sc_ready, 1)
            for t in range(T):
                last = nc.tensor.matmul(psum[:, 6, 0:C], onesf[:], hrow[:, t, :], start=(t == 0),
                                        stop=(t == T - 1))
            last.then_inc(hsum_ps, 1)

        def first_act(act):
            act.wait_ge(weights_in, 80)
            act.wait_ge(ones_made, 2)

            def adjacent(*ts):
                for t in ts:
                    act.wait_ge(mb_made, t + 1)
                    nc.scalar.activation(M[:, t, :], MB[:, t, :], ACT.Identity, scale=-1.0 / BIG,
                                         bias=onesf[:, 0:1]).then_inc(m_act, 1)

            for q in range(3):
                act.wait_ge(hT_ps, q + 1)
                nc.scalar.activation(mT[:, 512 * q:512 * q + 512], psum[:, 3 + q, :], ACT.Identity,
                                     bias=cols[:, 0:1]).then_inc(hT_sb, 1)
            for q in range(3):
                act.wait_ge(sr_ps, q + 1)
                nc.scalar.activation(srow[0:2 * H, 512 * q:512 * q + 512], psum[0:2 * H, q, :],
                                     ACT.Identity, bias=cols[0:2 * H, 3:4]).then_inc(sr_sb, 1)
            adjacent(1)
            for q in range(3):
                act.wait_ge(hr_ps, q + 1)
                nc.scalar.activation(hrow[:, 4 * q:4 * q + 4, :].rearrange("p t c -> p (t c)"),
                                     psum[:, 3 + q, :], ACT.Copy).then_inc(hr_sb, 1)
            adjacent(2)
            act.wait_ge(sjg_ready, 3)
            flat = lambda a: a[:, :, :].rearrange("p t h -> p (t h)")
            nc.scalar.activation(fD[:], flat(sjg), ACT.Exp, scale=SLOPE).then_inc(f_ready, 1)
            nc.scalar.activation(fB[:], flat(sjg), ACT.Exp).then_inc(f_ready, 1)
            nc.scalar.activation(fA[:], flat(tA), ACT.Exp).then_inc(f_ready, 1)
            nc.scalar.activation(fC[:], flat(tC), ACT.Exp).then_inc(f_ready, 1)
            for k, at in enumerate((X_D, X_B)):
                act.wait_ge(v_ready, 2 * (k + 1))
                nc.scalar.activation(Xg[:, :, at:at + D1], vr[k][0], ACT.Copy).then_inc(split_a, 1)
            for k, at in enumerate((X_D, X_B)):
                act.wait_ge(split_d, k + 1)
                nc.scalar.activation(Xg[:, :, at + D1:at + 2 * D1], vr[k][1], ACT.Copy).then_inc(split_a, 1)
            adjacent(4, 5, 7)
            act.wait_ge(hsum_ps, 1)
            nc.scalar.activation(hsum[:], psum[:, 6, 0:C], ACT.Copy).then_inc(hs_ready, 1)

        def first_dve(dve):
            dve.wait_ge(weights_in, 80)
            dve.wait_ge(consts_in, 16)
            for k in range(2):
                nc.vector.tensor_scalar(a16[:, H * k:H * k + H], cst[:, K_HM:K_HM + H], cols[:, 1 + k:2 + k],
                                        None, ALU.mult).then_inc(a16_ready, 1)
            masks(dve, 0, 4)
            dve.wait_ge(sr_sb, 3)
            nc.vector.tensor_reduce(gcol[:], srow[0:2 * H, :], AX, ALU.max).then_inc(dch, 1)
            dve.wait_ge(dch, 1)
            nc.vector.tensor_scalar(gdiag[:], cst[0:2 * H, K_ID:K_ID + 2 * H], gcol[:], None,
                                    ALU.mult).then_inc(g_ready, 1)
            masks(dve, 4, 5)
            dve.wait_ge(sc_ps, 1)
            nc.vector.tensor_copy(sc[:, :, :].rearrange("p t h -> p (t h)"),
                                  psum[:, 6, 0:T * 2 * H]).then_inc(sc_ready, 1)
            dve.wait_ge(gB_ps, 1)
            nc.vector.tensor_copy(gB[:], psum[:, 7, 0:2 * H]).then_inc(dch, 1)
            dve.wait_ge(dch, 2)
            dve.wait_ge(sc_ready, 1)
            g3 = gB[:, H:2 * H].unsqueeze(1).to_broadcast([P, T, H])
            nc.vector.tensor_tensor(sjg[:], sc[:, :, H:2 * H], g3, ALU.subtract).then_inc(dch, 1)
            nc.vector.tensor_tensor(tA[:], sc[:, :, 0:H], g3, ALU.add).then_inc(dch, 1)
            nc.vector.tensor_scalar(nsj[:], sc[:, :, H:2 * H], -1.0, None, ALU.mult).then_inc(dch, 1)
            dve.wait_ge(dch, 5)
            nc.vector.tensor_scalar(sjg[:], sjg[:], cols[:, 3:4], None, ALU.add).then_inc(sjg_ready, 1)
            nc.vector.tensor_scalar(tC[:], tA[:], SLOPE - 1.0, 0.0, ALU.mult, ALU.min).then_inc(sjg_ready, 1)
            dve.wait_ge(sjg_ready, 2)
            nc.vector.tensor_scalar(tA[:], tA[:], 1.0 - SLOPE, 0.0, ALU.mult, ALU.min).then_inc(sjg_ready, 1)
            masks(dve, 5, 7)
            dve.wait_ge(hr_sb, 3)
            halves = tuple(zip(vr, (fD, fB), (X_D, X_B)))
            for k, ((v, r), f, at) in enumerate(halves):
                dve.wait_ge(f_ready, k + 1)
                nc.vector.tensor_tensor(v[:, :, 0:D], hrow[:, :, :].rearrange("p t (h d) -> p (t h) d", h=H),
                                        f[:].unsqueeze(2).to_broadcast([P, T * H, D]),
                                        ALU.mult).then_inc(v_ready, 1)
                nc.vector.tensor_copy(v[:, :, D], f[:]).then_inc(v_ready, 1)
            masks(dve, 7, 9)
            dve.wait_ge(si_out, 16)
            for k, ((v, r), f, at) in enumerate(halves):
                dve.wait_ge(v_ready, 2 * (k + 1))
                dve.wait_ge(split_a, k + 1)
                nc.vector.tensor_tensor(r, v, Xg[:, :, at:at + D1], ALU.subtract).then_inc(split_d, 1)
            for k, ((v, r), f, at) in enumerate(halves):
                dve.wait_ge(split_d, k + 1)
                dve.wait_ge(split_a, k + 3)
                nc.vector.tensor_tensor(Xg[:, :, at + 2 * D1:at + 3 * D1], r, Xg[:, :, at + D1:at + 2 * D1],
                                        ALU.subtract).then_inc(split_d, 1)
            masks(dve, 9, T)

        layernorm(nc, ln_signals, ln_mem, 0,
                  lambda pool, p: pool.wait_ge(ln_signals[-1], LN_TILES * (p + 1)),
                  sync=first_sync, pool_start=make_ones, pool_end=first_pool, dve_end=first_dve,
                  act_end=first_act, pe_start=start_busy, product=project1, pe_end=first_pe,
                  loaded=x_in, ident_in=consts_in)

        ACT_TILES = [1, 2, 3, 4, 5, 7, 8, 9, 10, 11]
        NA = len(ACT_TILES)
        s_ready, u_ready, u_free, acc_full, acc_free, y_full, y_free = (sem(f"at_{n}") for n in (
            "s_ready", "u_ready", "u_free", "acc_full", "acc_free", "y_full", "y_free"))
        Sv = S34.rearrange("p (t h) c -> p t h c", h=H)
        YDv = YD.rearrange("p (t h) c -> p t h c", h=H)
        x1_ready = sem("at_x1_ready")
        alike = region(143, (T, C), F32)
        U0 = 2 * T
        PAIRS = H // 2 - 1
        YT = (0, 5)
        with nc.Block() as block:
            @block.sync
            def _(sp):
                sp.wait_ge(zero_set, 1)
                sp.dma_start(slots_in.rearrange("(s p) c -> p s c", p=P),
                             zero[:].unsqueeze(1).to_broadcast([P, SLOT_TILES, C])).then_inc(zeroed, 16)
                with sp.Fori(0, PAIRS) as i:
                    for hh in range(2):
                        sp.wait_ge(u_ready, 2 * T * i + (U0 + T * (hh + 1)))
                        sp.dma_start(siB[:, hh, :], s_bcast[bass.ds(2 * i + (hh + 2), 1), :].squeeze(0)
                                     .partition_broadcast(P)).then_inc(si_in[hh], 16)
                sp.wait_ge(zeroed, 16)

            @block.gpsimd
            def _(pool):
                nc.gpsimd.tensor_scalar(xr[:], xr[:], -1.0, None, ALU.add).then_inc(x1_ready, 1)
                pool.wait_ge(y_free, T + 1)
                nc.gpsimd.tensor_scalar(emp[:], deg[:], 0.0, 1.0 / N, ALU.is_equal, ALU.mult)\
                    .then_inc(x1_ready, 1)
                pool.wait_ge(x1_ready, 2)
                nc.gpsimd.tensor_tensor(alike, hsum[:].unsqueeze(1).to_broadcast([P, T, C]),
                                        emp[:].unsqueeze(2).to_broadcast([P, T, C]), ALU.mult)\
                    .then_inc(x1_ready, 1)
                pool.wait_ge(x1_ready, 3)
                nc.gpsimd.tensor_tensor(xn[:], xn[:], alike, ALU.add).then_inc(x1_ready, 1)
                pool.wait_ge(x1_ready, 4)

            @block.scalar
            def _(act):
                def head(h, hh, trip):
                    act.wait_ge(si_in[hh], 16 * trip + 16)
                    for k, t in enumerate(ACT_TILES):
                        back = ACT_TILES[k - SR] + 1 if k >= SR else ACT_TILES[k - SR + NA] + 1 - T
                        act.wait_ge(u_ready, T * h + (U0 + back))
                        nc.scalar.activation(S[k % SR], siB[:, hh, :], ACT.Identity,
                                             bias=sc[:, t, bass.ds(h + H, 1)]).then_inc(s_ready, 1)

                head(0, 0, 0)
                with act.Fori(0, PAIRS) as i:
                    head(2 * i + 1, 1, i)
                    head(2 * i + 2, 0, i + 1)
                head(H - 1, 1, H // 2 - 1)

            @block.vector
            def _(dve):
                dve.sem_inc(u_ready, U0)
                dve.sem_inc(acc_free, 2)
                dve.sem_inc(y_free, 1)

                def take_y(m):
                    dve.wait_ge(y_full, m + 1)
                    yb = psum[:, 6, 0:H * 52].rearrange("p (h c) -> p h c", h=H)
                    nc.vector.tensor_reduce(
                        YDv[:, bass.ds(m, 1), :, :].squeeze(1),
                        yb[:, :, 0:PARTS * D1].rearrange("p h (k c) -> p h c k", k=PARTS), AX,
                        ALU.add)
                    nc.vector.tensor_copy(deg[:, bass.ds(m, 1)], yb[:, 0, 51:52]).then_inc(y_free, 1)

                def take_head(h, hh):
                    dve.wait_ge(acc_full, h + 1)
                    for b in range(3):
                        out_ = Sv[:, 4 * b:4 * b + 4, bass.ds(h, 1), :].squeeze(2)\
                            .rearrange("p t (f c) -> p t f c", f=2)
                        acc = psum[:, 3 * hh + b, :].rearrange("p (t c) -> p t c", t=4)
                        for f, at in enumerate((X_B, X_D)):
                            last = nc.vector.tensor_reduce(
                                out_[:, :, f, :], acc[:, :, at:at + PARTS * D1]
                                .rearrange("p t (k c) -> p t c k", k=PARTS), AX, ALU.add)
                    last.then_inc(acc_free, 1)

                def head(h, hh, trip, before, ys):
                    dve.wait_ge(si_in[hh], 16 * trip + 16)
                    for t in range(T):
                        if before is None and t >= LATE:
                            nc.vector.tensor_scalar(M[:, t, :], MB[:, t, :], 0.0, None, ALU.is_equal)\
                                .then_inc(m_dve, 1)
                        dve.wait_ge(u_free, T * h + (t + 1))
                        if t in ACT_TILES:
                            k = ACT_TILES.index(t)
                            dve.wait_ge(s_ready, NA * h + (k + 1))
                            nc.vector.tensor_tensor(U[:, t % 4, :], S[k % SR], MB[:, t, :],
                                                    ALU.is_gt).then_inc(u_ready, 1)
                        else:
                            nc.vector.scalar_tensor_tensor(
                                U[:, t % 4, :], siB[:, hh, :], nsj[:, t, bass.ds(h, 1)], M[:, t, :],
                                ALU.is_gt, ALU.mult).then_inc(u_ready, 1)
                        if ys and t - 5 in YT:
                            take_y(ys[YT.index(t - 5)])
                        if before is not None and t == 4:
                            take_head(before, 1 - hh)

                head(0, 0, 0, None, None)
                with dve.Fori(0, PAIRS) as i:
                    head(2 * i + 1, 1, i, 2 * i, (4 * i, 4 * i + 1))
                    head(2 * i + 2, 0, i + 1, 2 * i + 1, (4 * i + 2, 4 * i + 3))
                head(H - 1, 1, H // 2 - 1, H - 2, None)
                take_head(H - 1, 1)

            @block.tensor
            def _(pe):
                pe.sem_inc(u_free, 4)

                def masked(m):
                    pe.wait_ge(y_free, m + 1)
                    for j in range(T):
                        y = nc.tensor.matmul(psum[:, 6, 0:H * 52], M[:, j, bass.ds(m * P, P)],
                                             X[:, j, :, X_D:X_D + 52], start=(j == 0), stop=(j == T - 1))
                    y.then_inc(y_full, 1)

                def head(h, hh, ys):
                    pe.wait_ge(acc_free, h + 1)
                    for t in range(T):
                        pe.wait_ge(u_ready, T * h + (U0 + t + 1))
                        for b in range(T):
                            last = nc.tensor.matmul(
                                psum[:, 3 * hh + b // 4, P * (b % 4):P * (b % 4) + 2 * PARTS * D1],
                                U[:, t % 4, P * b:P * b + P],
                                X[:, t, bass.ds(h, 1), 0:2 * PARTS * D1].squeeze(1),
                                start=(t == 0 and b % 4 == 0), stop=(t == T - 1), skip_group_check=True)
                        last.then_inc(u_free, 1)
                        if ys and t in YT:
                            masked(ys[YT.index(t)])
                    nc.tensor.matmul(psum[:, 7, 0:2], onesb[:], onesb[:, 0:2], start=True,
                                     stop=True).then_inc(acc_full, 1)

                head(0, 0, None)
                pe.wait_ge(m_dve, T - LATE)
                with pe.Fori(0, PAIRS) as i:
                    head(2 * i + 1, 1, (4 * i, 4 * i + 1))
                    head(2 * i + 2, 0, (4 * i + 2, 4 * i + 3))
                head(H - 1, 1, None)

        M2 = region(72, (T, N), BF16)
        stage2 = [region(kb, (N,), I32) for kb in (48, 54, 60, 66, 132, 138, 144, 150, 156, 162)]
        S2 = len(stage2)
        m2_made, adj2_in = sem("m2_made"), [sem(f"adj2_in{k}") for k in range(T // 2)]
        gw_in, w_in = sem("gw_in"), sem("w_in")
        gates_w, gates_b = sb("gates_w", [P, E], F32), sb("gates_b", [P, E], F32)
        route_i = sb("route_i", [GROUPS, 1], I32)
        Wexp = region(0, (E, 3 * HID), F32)

        def load_adjacency2(sp, a, b):
            for t in range(a, b):
                if t >= S2:
                    sp.wait_ge(m2_made, t - S2 + 1)
                sp.dma_start(stage2[t % S2], adjT[P * t:P * t + P, :]).then_inc(adj2_in[t // 2], 16)

        c2, elu_e, scale2, turned2, taken2, lg_ps = (sem(f"p2_{x}") for x in (
            "chain", "elu", "scale", "turned", "taken", "lg_ps"))
        dD, dA = region(126, (T * H,), F32), region(127, (T * H,), F32)
        G, SMALL, STEPS, SKEW = T * H // 3, 8, 11, 3
        Q = 3
        order = [(q, w - SKEW * q) for w in range(STEPS + SKEW * (Q - 1)) for q in range(Q)
                 if 0 <= w - SKEW * q < STEPS]
        done = {qs: SMALL + k + 1 for k, qs in enumerate(order)}
        num = region(108, (T * H, D), F32)
        tmp = region(114, (T * H, D), F32)
        e1 = region(120, (T * H, D), F32)
        with nc.Block() as block:
            @block.vector
            def _(dve):
                n = [0]

                def link(ins):
                    n[0] += 1
                    ins.then_inc(c2, 1)
                    dve.wait_ge(c2, n[0])

                link(nc.vector.tensor_tensor(dD, YD[:, :, D], S34[:, :, R2 - 1], ALU.subtract))
                link(nc.vector.tensor_tensor(dD, dD, fC[:], ALU.mult))
                link(nc.vector.tensor_tensor(dA, S34[:, :, D], fA[:], ALU.mult))
                link(nc.vector.tensor_tensor(dD, dD, dA, ALU.add))
                link(nc.vector.scalar_tensor_tensor(
                    dA.rearrange("p (t h) -> p t h", h=H), emp[:].unsqueeze(2).to_broadcast([P, T, H]),
                    float(N), dD.rearrange("p (t h) -> p t h", h=H), ALU.mult, ALU.add))
                link(nc.vector.reciprocal(dD, dA))
                link(nc.vector.tensor_tensor(fA[:], fA[:], dD, ALU.mult))
                link(nc.vector.tensor_tensor(fC[:], fC[:], dD, ALU.mult))

                wide = lambda f, g: f[:, g].unsqueeze(2).to_broadcast([P, G, D])
                rows = lambda a: a[:, :, :].rearrange("p t (h d) -> p (t h) d", d=D)

                def step(q, s_):
                    g, ts = slice(G * q, G * q + G), range(4 * q, 4 * q + 4)
                    if s_ == 0:
                        return nc.vector.tensor_tensor(tmp[:, g], S34[:, g, 0:D], wide(fA, g), ALU.mult)
                    if s_ == 1:
                        return nc.vector.tensor_tensor(num[:, g], YD[:, g, 0:D], S34[:, g, D1:R2 - 1],
                                                       ALU.subtract)
                    if s_ == 2:
                        return nc.vector.tensor_tensor(num[:, g], num[:, g], wide(fC, g), ALU.mult)
                    if s_ == 3:
                        return nc.vector.tensor_tensor(num[:, g], num[:, g], tmp[:, g], ALU.add)
                    if s_ == 4:
                        return nc.vector.tensor_tensor(num[:, g], num[:, g], rows(xn)[:, g], ALU.add)
                    if s_ == 5:
                        return nc.vector.tensor_scalar(tmp[:, g], num[:, g], 0.0, None, ALU.min)
                    if s_ == 6:
                        return nc.vector.scalar_tensor_tensor(rows(xr)[:, g], num[:, g], 0.0, rows(xr)[:, g],
                                                              ALU.max, ALU.add)
                    if s_ == 7:
                        dve.wait_ge(elu_e, q + 1)
                        return nc.vector.tensor_tensor(rows(xr)[:, g], rows(xr)[:, g], e1[:, g], ALU.add)
                    if s_ == 8:
                        return [nc.vector.bn_stats(st[:, t, :], xr[:, t, :]) for t in ts][-1]
                    if s_ == 9:
                        return [nc.vector.bn_aggr(mv[:, t, :], st[:, t, :]) for t in ts][-1]
                    if s_ == 10:
                        dve.wait_ge(scale2, 2 * q + 2)
                        return [nc.vector.tensor_scalar(xn[:, t, :], xr[:, t, :], mv[:, t, 0:1], rstd[:, t:t + 1],
                                                        ALU.subtract, ALU.mult) for t in ts][-1]

                for w in range(STEPS + SKEW * (Q - 1)):
                    for q in range(Q):
                        if 0 <= w - SKEW * q < STEPS:
                            if w > SKEW * q:
                                dve.wait_ge(c2, done[q, w - SKEW * q - 1])
                            step(q, w - SKEW * q).then_inc(c2, 1)

            @block.sync
            def _(sp):
                for dst, src in ((gates_w[:], gate_w), (gates_b[:], gate_b.squeeze(0).partition_broadcast(P)),
                                 (route_i[:], route)):
                    sp.dma_start(dst, src).then_inc(gw_in, 16)
                for k, w in enumerate((w1, w2, w3)):
                    sp.dma_start(Wexp[:, :, HID * k:HID * k + HID], w).then_inc(w_in, 16)
                load_adjacency2(sp, 0, 6)
                sp.wait_ge(c2, done[Q - 1, 1])
                load_adjacency2(sp, 6, S2)

            @block.gpsimd
            def _(pool):
                for q in range(Q):
                    third = slice(4 * q, 4 * q + 4)
                    pool.wait_ge(c2, done[q, 9])
                    nc.gpsimd.tensor_scalar(rstd[:, third], mv[:, third, 1], EPS, None, ALU.add)\
                        .then_inc(scale2, 1)
                    pool.wait_ge(scale2, 2 * q + 1)
                    nc.gpsimd.tensor_tensor(rstd[:, third], rstd[:, third], half[:, third], ALU.pow)\
                        .then_inc(scale2, 1)

            @block.tensor
            def _(pe):
                def turn(q):
                    pe.wait_ge(c2, done[q, 10])
                    for t in range(4 * q, 4 * q + 4):
                        last = nc.tensor.transpose(psum[:, q, P * (t % 4):P * (t % 4) + P], xn[:, t, :], ident)
                    last.then_inc(turned2, 1)

                def gate(q):
                    pe.wait_ge(taken2, q + 1)
                    for t in range(4 * q, 4 * q + 4):
                        last = nc.tensor.matmul(psum[:, 3, E * t:E * t + E], xT[:, P * t:P * t + P], gates_w[:],
                                                start=(t == 0), stop=True, skip_group_check=True)
                    if q == 2:
                        last.then_inc(lg_ps, 1)

                pe.wait_ge(gw_in, 48)
                for q in range(Q):
                    turn(q)
                    gate(q)

            @block.scalar
            def _(act):
                for q in range(Q):
                    act.wait_ge(c2, done[q, 5])
                    nc.scalar.activation(e1[:, G * q:G * q + G], tmp[:, G * q:G * q + G], ACT.Exp)\
                        .then_inc(elu_e, 1)
                for q in range(Q):
                    act.wait_ge(turned2, q + 1)
                    nc.scalar.activation(xT[:, 512 * q:512 * q + 512], psum[:, q, :], ACT.Copy)\
                        .then_inc(taken2, 1)

        yall = region(144, (SLOT_TILES, C), F32)
        small = bump(120, 132)
        lg = small([P, T, E], F32)
        mx = small([P, T, 8], F32)
        ix = small([P, T, 8], U32)
        ixf = small([P, T, 2], F32)
        OH = small([P, 2, T, E], BF16)
        OHs = small([P, T, E], BF16)
        cnt = small([P, E], F32)
        over = small([P, E, T + 1], F32)
        padded = small([P, E], F32)
        ends = small([P, E], F32)
        rk = small([P, T, E], F32)
        rk2 = small([P, 2, T, E], F32)
        posf = small([P, 2, T], F32)
        pos = sb("pos", [P, 2, T], I32)
        wts = sb("wts", [P, 2, T], F32)
        e2 = small([P, T], F32)
        se = small([1, SLOT_TILES, E], F32)
        ef = small([1, SLOT_TILES], F32)
        eslot = sb("eslot", [1, SLOT_TILES], I32)
        route_f = small([GROUPS, 1], F32)
        OHg = small([GROUPS, E], BF16)
        gcnt = small([GROUPS, E], F32)
        gover = small([GROUPS, E, GROUPS // GPT + 1], F32)
        gpad = small([GROUPS, E], F32)
        gend = small([GROUPS, E], F32)
        grk = small([GROUPS, E], F32)
        gpos = small([GROUPS, 1], F32)
        gpos_i = sb("gpos_i", [1, GROUPS], I32)
        gef = small([1, FT], F32)
        ge = sb("ge", [1, FT], I32)
        scattered, c3 = [sem("scattered0"), sem("scattered1")], sem("p3_c")
        oh_ready, rk_ps, pos_ready, d_e2, e2_ready, g_oh, g_ps, g_col, g_row = (sem(f"p3_{n}") for n in (
            "oh", "rk_ps", "pos", "d", "e2", "g_oh", "g_ps", "g_col", "g_row"))
        with nc.Block() as block:
            @block.sync
            def _(sp):
                load_adjacency2(sp, S2, T)

            @block.tensor
            def _(pe):
                pe.wait_ge(g_oh, 1)
                nc.tensor.matmul(psum[0:GROUPS, 6, 0:E], trib[0:GROUPS, 0:GROUPS], OHg[:], start=True, stop=True)
                nc.tensor.matmul(psum[0:GROUPS, 7, 0:E], onesb[0:GROUPS, 0:GROUPS], OHg[:], start=True,
                                 stop=True).then_inc(g_ps, 1)
                pe.wait_ge(oh_ready, 1)
                nc.tensor.matmul(psum[:, 1, 0:T * E], trib[:], OHs[:, :, :].rearrange("p t e -> p (t e)"),
                                 start=True, stop=False, skip_group_check=True)
                for d in range(1, T):
                    nc.tensor.matmul(psum[:, 1, d * E:T * E], onesb[:],
                                     OHs[:, 0:T - d, :].rearrange("p t e -> p (t e)"), start=False,
                                     stop=(d == T - 1), skip_group_check=True)
                for t in range(T):
                    last = nc.tensor.matmul(psum[:, 2, 0:E], onesb[:], OHs[:, t, :], start=(t == 0),
                                            stop=(t == T - 1))
                last.then_inc(rk_ps, 1)
                pe.wait_ge(g_col, 1)
                nc.tensor.matmul(psum[0:1, 5, 0:GROUPS], gpos[:], cst[0:GROUPS, K_ID:K_ID + GROUPS], start=True,
                                 stop=True).then_inc(g_row, 1)
                pe.wait_ge(scattered[0], 16 * (2 * T - 6))
                keep_busy(pe, 56, 4)

            @block.scalar
            def _(act):
                act.wait_ge(d_e2, 1)
                nc.scalar.activation(e2[:], e2[:], ACT.Exp).then_inc(e2_ready, 1)
                nc.scalar.preload_act_table(ACT.Silu)

            @block.vector
            def _(dve):
                n = [0]

                def link(ins):
                    n[0] += 1
                    ins.then_inc(c3, 1)
                    dve.wait_ge(c3, n[0])

                dve.wait_ge(gw_in, 48)
                link(nc.vector.tensor_copy(route_f[:], route_i[:]))
                nc.vector.tensor_scalar(OHg[:], cst[0:GROUPS, K_IOTA:K_IOTA + E], route_f[:], None,
                                        ALU.is_equal).then_inc(g_oh, 1)
                dve.wait_ge(lg_ps, 1)
                link(nc.vector.tensor_tensor(lg[:], psum[:, 3, 0:T * E].rearrange("p (t e) -> p t e", t=T),
                                             gates_b[:].unsqueeze(1).to_broadcast([P, T, E]), ALU.add))
                for t in range(T):
                    last = nc.vector.max(mx[:, t, :], lg[:, t, :])
                link(last)
                for t in range(T):
                    last = nc.vector.max_index(ix[:, t, :], mx[:, t, :], lg[:, t, :])
                link(last)
                link(nc.vector.tensor_copy(ixf[:], ix[:, :, 0:2]))
                iota = cst[:, K_IOTA:K_IOTA + E].unsqueeze(1).to_broadcast([P, T, E])
                for k in range(2):
                    link(nc.vector.tensor_tensor(OH[:, k, :, :], iota,
                                                 ixf[:, :, k:k + 1].to_broadcast([P, T, E]), ALU.is_equal))
                nc.vector.tensor_tensor(OHs[:], OH[:, 0, :, :], OH[:, 1, :, :], ALU.add).then_inc(oh_ready, 1)
                nc.vector.tensor_tensor(e2[:], mx[:, :, 1], mx[:, :, 0], ALU.subtract).then_inc(d_e2, 1)
                dve.wait_ge(rk_ps, 1)
                link(nc.vector.tensor_copy(cnt[:], psum[:, 2, 0:E]))
                link(nc.vector.tensor_tensor(over[:], cnt[:].unsqueeze(2).to_broadcast([P, E, T + 1]),
                                             cst[:, K_SLOT:K_SLOT + T + 1].unsqueeze(1)
                                             .to_broadcast([P, E, T + 1]), ALU.is_gt))
                link(nc.vector.tensor_reduce(padded[:], over[:], AX, ALU.add))
                link(nc.vector.tensor_scalar(padded[:], padded[:], float(P), None, ALU.mult))
                link(nc.vector.tensor_tensor_scan(ends[:], onesf[:, 0:E], padded[:], 0.0, ALU.mult, ALU.add))
                link(nc.vector.tensor_tensor(padded[:], ends[:], padded[:], ALU.subtract))
                link(nc.vector.tensor_tensor(rk[:], psum[:, 1, 0:T * E].rearrange("p (t e) -> p t e", t=T),
                                             padded[:].unsqueeze(1).to_broadcast([P, T, E]), ALU.add))
                for k in range(2):
                    link(nc.vector.tensor_tensor(rk2[:, k, :, :], OH[:, k, :, :], rk[:], ALU.mult))
                link(nc.vector.tensor_reduce(posf[:, :, :].rearrange("p k t -> p (k t)"),
                                             rk2[:, :, :, :].rearrange("p k t e -> p (k t) e"), AX, ALU.add))
                nc.vector.tensor_copy(pos[:], posf[:]).then_inc(pos_ready, 1)
                link(nc.vector.tensor_tensor(se[:], ends[0:1, :].unsqueeze(1).to_broadcast([1, SLOT_TILES, E]),
                                             cst[0:1, K_SLOT:K_SLOT + SLOT_TILES].unsqueeze(2)
                                             .to_broadcast([1, SLOT_TILES, E]), ALU.is_le))
                link(nc.vector.tensor_reduce(ef[:], se[:], AX, ALU.add))
                link(nc.vector.tensor_scalar(eslot[:], ef[:], float(E - 1), None, ALU.min))
                dve.wait_ge(e2_ready, 1)
                link(nc.vector.tensor_scalar(wts[:, 0, :], e2[:], 1.0, None, ALU.add))
                link(nc.vector.reciprocal(wts[:, 0, :], wts[:, 0, :]))
                link(nc.vector.tensor_tensor(wts[:, 1, :], wts[:, 0, :], e2[:], ALU.mult))
                dve.wait_ge(g_ps, 1)
                link(nc.vector.tensor_scalar(gcnt[:], psum[0:GROUPS, 7, 0:E], float(GT), None, ALU.mult))
                nk = GROUPS // GPT + 1
                link(nc.vector.tensor_tensor(gover[:], gcnt[:].unsqueeze(2).to_broadcast([GROUPS, E, nk]),
                                             cst[0:GROUPS, K_FT:K_FT + nk].unsqueeze(1)
                                             .to_broadcast([GROUPS, E, nk]), ALU.is_gt))
                link(nc.vector.tensor_reduce(gpad[:], gover[:], AX, ALU.add))
                link(nc.vector.tensor_scalar(gpad[:], gpad[:], float(TS), None, ALU.mult))
                link(nc.vector.tensor_tensor_scan(gend[:], onesf[0:GROUPS, 0:E], gpad[:], 0.0, ALU.mult, ALU.add))
                link(nc.vector.tensor_tensor(gpad[:], gend[:], gpad[:], ALU.subtract))
                link(nc.vector.scalar_tensor_tensor(grk[:], psum[0:GROUPS, 6, 0:E], float(GT), gpad[:], ALU.mult,
                                                    ALU.add))
                link(nc.vector.tensor_tensor(grk[:], grk[:], OHg[:], ALU.mult))
                nc.vector.tensor_reduce(gpos[:], grk[:], AX, ALU.add).then_inc(g_col, 1)
                link(nc.vector.tensor_tensor(se[:, 0:FT, :], gend[0:1, :].unsqueeze(1).to_broadcast([1, FT, E]),
                                             cst[0:1, K_FT:K_FT + FT].unsqueeze(2).to_broadcast([1, FT, E]),
                                             ALU.is_le))
                link(nc.vector.tensor_reduce(gef[:], se[:, 0:FT, :], AX, ALU.add))
                link(nc.vector.tensor_scalar(ge[:], gef[:], float(E - 1), None, ALU.min))
                dve.wait_ge(g_row, 1)
                link(nc.vector.tensor_copy(gpos_i[:], psum[0:1, 5, 0:GROUPS]))
                for t in range(T):
                    dve.wait_ge(adj2_in[t // 2], 32)
                    nc.vector.tensor_scalar(M2[:, t, :], stage2[t % S2], 0.0, None, ALU.is_gt)\
                        .then_inc(m2_made, 1)

            @block.gpsimd
            def _(pool):
                pool.wait_ge(pos_ready, 1)
                for t in range(T):
                    for k in range(2):
                        nc.gpsimd.indirect_dma_start(
                            slots_in, bass.IndirectOffsetOnAxis(ap=pos[:, k, t:t + 1].bitcast(U32), axis=0),
                            xn[:, t, :], None).then_inc(scattered[t // (T - 3)], 16)
                pool.wait_ge(scattered[0], 16 * (2 * T - 6))
                pool.wait_ge(scattered[1], 16 * 6)

        xs = region(60, (RING, P), F32)
        xsT = region(62, (2, P), F32)
        sil = region(63, (2, HID), F32)
        hid = region(65, (2, HID), F32)
        wring = region(108, (RING, 3 * HID), F32)
        xs_in = [sem(f"xs_in{k}") for k in range(RING)]
        turned, multiplied, y_made, xt_ready, sil_ready, hid_ready, y_ready, w_ready, y_out = (
            sem(f"p4_{n}") for n in ("turned", "multiplied", "y_made", "xt", "sil", "hid", "y", "w", "y_out"))
        PASSES = (SLOT_TILES - 4) // RING
        slots_v = slots_in.rearrange("(s p) c -> p s c", p=P)
        out_v = slots_out.rearrange("(s p) c -> p s c", p=P)
        with nc.Block() as block:
            @block.sync
            def _(sp):
                for k in range(RING):
                    sp.dma_start(xs[:, k, :], slots_v[:, k, :]).then_inc(xs_in[k], 16)
                with sp.Fori(0, SLOT_TILES // RING - 1) as i:
                    for k in range(RING):
                        sp.wait_ge(turned, RING * i + k + 1)
                        sp.dma_start(xs[:, k, :], slots_v[:, bass.ds(RING * i + (RING + k), 1), :].squeeze(1))\
                            .then_inc(xs_in[k], 16)

            @block.tensor
            def _(pe):
                pe.sem_inc(multiplied, 2)
                pe.sem_inc(y_made, RING)
                pe.wait_ge(w_in, 48)

                def turn(n, k, trip):
                    pe.wait_ge(xs_in[k], 16 * trip + 16)
                    pe.wait_ge(xt_ready, n + 1)
                    nc.tensor.transpose(psum[:, k % 2, 0:P], xs[:, k, :], ident).then_inc(turned, 1)

                def hidden(n, k):
                    pe.wait_ge(xt_ready, n + (2 + 1))
                    pe.wait_ge(w_ready, n + 1)
                    pe.wait_ge(hid_ready, n + 1)
                    for m in range(4):
                        last = nc.tensor.matmul(psum[:, 2 + k % 2, P * m:P * m + P], wring[:, k, P * m:P * m + P],
                                                xsT[:, k % 2, :], start=True, stop=True, skip_group_check=True)
                    last.then_inc(multiplied, 1)

                def outputs(n, k):
                    pe.wait_ge(hid_ready, n + (2 + 1))
                    pe.wait_ge(y_ready, n + 1)
                    for m in range(KC):
                        last = nc.tensor.matmul(psum[:, 4 + k % 2, 0:C], hid[:, k % 2, P * m:P * m + P],
                                                wring[:, k, 2 * HID + C * m:2 * HID + C * m + C],
                                                start=(m == 0), stop=(m == KC - 1))
                    last.then_inc(y_made, 1)

                turn(0, 0, 0)
                turn(1, 1, 0)
                hidden(0, 0)
                with pe.Fori(0, PASSES) as i:
                    for j in range(RING):
                        turn(RING * i + (2 + j), (2 + j) % RING, i + (2 + j) // RING)
                        hidden(RING * i + (1 + j), (1 + j) % RING)
                        outputs(RING * i + j, j)
                for n in range(SLOT_TILES - 2, SLOT_TILES + 2):
                    if n < SLOT_TILES:
                        turn(n, n % RING, n // RING)
                    if n - 1 < SLOT_TILES:
                        hidden(n - 1, (n - 1) % RING)
                    outputs(n - 2, (n - 2) % RING)

            @block.scalar
            def _(act):
                nc.scalar.preload_act_table(ACT.Silu)
                act.sem_inc(xt_ready, 2)
                act.sem_inc(y_ready, 2)

                def turn(n, k):
                    act.wait_ge(turned, n + 1)
                    act.wait_ge(multiplied, n + 1)
                    nc.scalar.activation(xsT[:, k % 2, :], psum[:, k % 2, 0:P], ACT.Copy).then_inc(xt_ready, 1)

                def hidden(n, k):
                    act.wait_ge(multiplied, n + (2 + 1))
                    act.wait_ge(hid_ready, n + 1)
                    nc.scalar.activation(sil[:, k % 2, :], psum[:, 2 + k % 2, 0:HID], ACT.Silu)\
                        .then_inc(sil_ready, 1)

                def outputs(n, k):
                    act.wait_ge(y_made, n + (RING + 1))
                    nc.scalar.activation(yall[:, bass.ds(n, 1), :].squeeze(1), psum[:, 4 + k % 2, 0:C],
                                         ACT.Copy).then_inc(y_ready, 1)
                    if k == RING - 1:
                        act.wait_ge(y_ready, n + (2 + 1))
                        act.dma_start(out_v[:, bass.ds(n - (RING - 1), RING), :],
                                      yall[:, bass.ds(n - (RING - 1), RING), :]).then_inc(y_out, 16)

                turn(0, 0)
                turn(1, 1)
                hidden(0, 0)
                with act.Fori(0, PASSES) as i:
                    for j in range(RING):
                        turn(RING * i + (2 + j), (2 + j) % RING)
                        hidden(RING * i + (1 + j), (1 + j) % RING)
                        outputs(RING * i + j, j)
                for n in range(SLOT_TILES - 2, SLOT_TILES + 2):
                    if n < SLOT_TILES:
                        turn(n, n % RING)
                    if n - 1 < SLOT_TILES:
                        hidden(n - 1, (n - 1) % RING)
                    outputs(n - 2, (n - 2) % RING)
                act.wait_ge(y_out, 16 * SLOT_TILES // RING)

            @block.vector
            def _(dve):
                dve.sem_inc(hid_ready, 2)
                dve.wait_ge(w_in, 48)

                def experts(first, count):
                    return nc.values_load_multi_w_load_instructions(
                        eslot[0:1, bass.ds(first, count)], engines=[mybir.EngineType.DVE], min_val=0,
                        max_val=E - 1, skip_runtime_bounds_check_because="clamped when made")[1]

                def weights(n, k, e):
                    dve.wait_ge(y_made, n + 1)
                    nc.vector.tensor_copy(wring[:, k, :], Wexp[:, bass.ds(e, 1), :].squeeze(1))\
                        .then_inc(w_ready, 1)

                def hidden(n, k):
                    dve.wait_ge(sil_ready, n + 1)
                    dve.wait_ge(y_made, n + (RING - 2 + 1))
                    nc.vector.tensor_tensor(hid[:, k % 2, :], psum[:, 2 + k % 2, HID:2 * HID],
                                            sil[:, k % 2, :], ALU.mult).then_inc(hid_ready, 1)

                e = experts(0, 2)
                weights(0, 0, e[0])
                weights(1, 1, e[1])
                hidden(0, 0)
                with dve.Fori(0, PASSES) as i:
                    e = experts(i * RING + 2, RING)
                    for j in range(RING):
                        weights(RING * i + (2 + j), (2 + j) % RING, e[j])
                        hidden(RING * i + (1 + j), (1 + j) % RING)
                e = experts(SLOT_TILES - 2, 2)
                for n in range(SLOT_TILES - 2, SLOT_TILES + 1):
                    if n < SLOT_TILES:
                        weights(n, n % RING, e[n - SLOT_TILES + 2])
                    hidden(n - 1, (n - 1) % RING)

        def preload_attention2(sp):
            for dst, src in ((uW_sb[:], uW), (ua_sb[:, 0:1], uas), (ua_sb[:, 1:2], uad)):
                sp.dma_start(dst, src).then_inc(u_in, 16)

        back = region(108, (2, T, C), F32)
        got = [sem(f"got{q}") for q in range(T // 2)]
        comb, var3, row_stats = sem("p5_comb"), sem("p5_var"), sem("p5_stats")

        def gather(pool):
            for t in range(T):
                for k in range(2):
                    nc.gpsimd.indirect_dma_start(
                        back[:, k, t, :], None, slots_out,
                        bass.IndirectOffsetOnAxis(ap=pos[:, k, t:t + 1].bitcast(U32), axis=0))\
                        .then_inc(got[t // 2], 16)

        def gather_busy(pe):
            pe.wait_ge(var3, T - LN_TILES)
            keep_busy(pe, 56, 7)

        def combine(dve):
            for t in range(T):
                dve.wait_ge(got[t // 2], 16 * 4)
                nc.vector.scalar_tensor_tensor(xr[:, t, :], back[:, 0, t, :], wts[:, 0, t:t + 1], xr[:, t, :],
                                               ALU.mult, ALU.add).then_inc(comb, 1)
                dve.wait_ge(comb, 2 * t + 1)
                nc.vector.scalar_tensor_tensor(xr[:, t, :], back[:, 1, t, :], wts[:, 1, t:t + 1], xr[:, t, :],
                                               ALU.mult, ALU.add).then_inc(comb, 1)
                dve.wait_ge(comb, 2 * t + 2)
                nc.vector.bn_stats(st[:, t, :], xr[:, t, :]).then_inc(row_stats, 1)
                dve.wait_ge(row_stats, t + 1)
                nc.vector.bn_aggr(mv[:, t, :], st[:, t, :]).then_inc(var3, 1)

        q_hT = sem("p6_hT")
        z_m = sem("z_m")
        z_t, z_u, z_v, z_used, z_full, z_g, z_gfree = (sem(f"z_{n}") for n in (
            "t", "u", "v", "used", "full", "g", "gfree"))

        def scores(act, c, first=0, end=T):
            if c >= 2:
                act.wait_ge(z_used, c + 1)
            for t in range(first, end):
                nc.scalar.activation(U1[:, 1 - c % 2, t, :], fsB[:, CW * c:CW * c + CW], ACT.Identity,
                                     bias=fdc[:, t:t + 1]).then_inc(z_t, 1)

        V = (region(108, (T, CW), BF16), region(135.25, (T, CW), BF16))
        X1 = region(117, (T, 2 * VS), BF16)
        vr1 = ((region(135.25, (T, V1), F32), region(141.5, (T, V1), F32)),
               (region(108, (T, V1), F32), region(162.25, (T, V1), F32)))
        U1 = region(144.25, (2, T, CW), BF16)
        num1 = region(162.25, (T, V1), F32)
        G1 = (xT, mT)
        Wall = region(0, (E, 4 * HID + 4), F32)
        fsB = region(64.5, (N,), F32)
        early1 = bump(70.5, 72)
        uas_rep, uad_rep = early1([P, P], F32), early1([P, P], F32)
        gmax, tAC, fdg = early1([P, 4], F32), early1([P, 3, T], F32), early1([P, T], F32)
        q_w, q_hTs, q_fs, q_fd, q_fc, q_hr, q_hsum, q_c, q_fac, q_hrs, q_fss, q_t, q_v, q_sa, q_sd, q_ones, \
            q_fcs, q_hs = (sem(f"p6_{n}") for n in ("w", "hTs", "fs", "fd", "fc", "hr", "hsum", "c", "fac",
                                               "hrs", "fss", "t", "v", "sa", "sd", "ones", "fcs", "hs"))

        def project2(pe, q):
            if q == 0:
                pe.wait_ge(u_in, 48)
            nc.tensor.matmul(psum[:, 3 + q, :], uW_sb[:], xT[:, 512 * q:512 * q + 512], start=True, stop=True)\
                .then_inc(q_hT, 1)

        def spread(pool):
            pool.wait_ge(u_in, 48)
            nc.gpsimd.tensor_scalar(uas_rep, onesf[:], ua_sb[:, 0:1], None, ALU.mult).then_inc(q_w, 1)
            nc.gpsimd.tensor_scalar(uad_rep, onesf[:], ua_sb[:, 1:2], None, ALU.mult).then_inc(q_w, 1)
            nc.gpsimd.memset(X1[:, :, VS - 1:VS], 1.0).then_inc(q_ones, 1)
            nc.gpsimd.memset(X1[:, :, 2 * VS - 1:2 * VS], 1.0).then_inc(q_ones, 1)
            pool.wait_ge(q_w, 2)
            pool.wait_ge(q_ones, 2)

        def projected(act):
            for q in range(3):
                act.wait_ge(q_hT, q + 1)
                nc.scalar.activation(mT[:, 512 * q:512 * q + 512], psum[:, 3 + q, :], ACT.Copy).then_inc(q_hTs, 1)

        def project_sync(sp):
            preload_attention2(sp)
            sp.wait_ge(var3, T)
            sp.dma_start(Wall, WrT).then_inc(wall_in, 16)

        def project_pe(pe):
            pe.wait_ge(u_in, 48)
            pe.wait_ge(q_w, 2)
            for q in range(3):
                pe.wait_ge(q_hTs, q + 1)
                nc.tensor.matmul(psum[:, q, :], uad_rep, mT[:, 512 * q:512 * q + 512], start=True,
                                 stop=True).then_inc(q_fd, 1)
            for t in range(T):
                last = nc.tensor.matmul(psum[:, 3, 2 * t:2 * t + 2], mT[:, P * t:P * t + P], ua_sb[:],
                                        start=(t == 0), stop=True, skip_group_check=True)
            last.then_inc(q_fc, 1)
            for t in range(T):
                last = nc.tensor.transpose(psum[:, (6, 7, 4)[t // 4], P * (t % 4):P * (t % 4) + P],
                                           mT[:, P * t:P * t + P], ident)
                if t % 4 == 3:
                    last.then_inc(q_hr, 1)
            for q in range(3):
                if q > 0:
                    pe.wait_ge(q_c, q + 1)
                nc.tensor.matmul(psum[:, (5, 0, 1)[q], :], uas_rep, mT[:, 512 * q:512 * q + 512],
                                 start=True, stop=True).then_inc(q_fs, 1)
            pe.wait_ge(q_hrs, 3)
            pe.wait_ge(q_c, 3)
            for t in range(T):
                last = nc.tensor.matmul(psum[:, 2, 0:C], onesf[:], hrow[:, t, :], start=(t == 0),
                                        stop=(t == T - 1))
            last.then_inc(q_hsum, 1)

        def project_act(act):
            projected(act)
            for q in range(3):
                act.wait_ge(q_hr, q + 1)
                nc.scalar.activation(hrow[:, 4 * q:4 * q + 4, :].rearrange("p t c -> p (t c)"),
                                     psum[:, (6, 7, 4)[q], :], ACT.Copy).then_inc(q_hrs, 1)
            act.wait_ge(q_t, 1)
            nc.scalar.activation(f1[:, 3, :], fdg, ACT.Exp, scale=SLOPE).then_inc(q_fac, 1)
            nc.scalar.activation(f1[:, 1, :], fdg, ACT.Exp).then_inc(q_fac, 1)
            act.wait_ge(q_t, 3)
            nc.scalar.activation(f1[:, 0, :], tAC[:, 0, :], ACT.Exp).then_inc(q_fac, 1)
            nc.scalar.activation(f1[:, 2, :], tAC[:, 1, :], ACT.Exp).then_inc(q_fac, 1)
            for k, at in enumerate((VS, 0)):
                act.wait_ge(q_v, 2 * (k + 1))
                nc.scalar.activation(X1[:, :, at:at + V1], vr1[k][0], ACT.Copy).then_inc(q_sa, 1)
            for k, at in enumerate((VS, 0)):
                act.wait_ge(q_sd, k + 1)
                nc.scalar.activation(X1[:, :, at + V1:at + 2 * V1], vr1[k][1], ACT.Copy).then_inc(q_sa, 1)
            for q in range(3):
                act.wait_ge(q_fs, q + 1)
                nc.scalar.activation(fsB[:, 512 * q:512 * q + 512], psum[:, (5, 0, 1)[q], :],
                                     ACT.Copy).then_inc(q_fss, 1)
            act.wait_ge(q_fss, 1)
            act.wait_ge(q_fcs, 2)
            scores(act, 0, 0, T // 2)
            act.wait_ge(q_hsum, 1)
            nc.scalar.activation(hsum[:], psum[:, 2, 0:C], ACT.Copy).then_inc(q_hs, 1)

        def project_dve(dve):
            for q in range(3):
                dve.wait_ge(q_fd, q + 1)
                nc.vector.tensor_reduce(gmax[:, q:q + 1], psum[:, q, :], AX, ALU.max).then_inc(q_c, 1)
            dve.wait_ge(q_c, 3)
            nc.vector.tensor_reduce(gmax[:, 3:4], gmax[:, 0:3], AX, ALU.max).then_inc(q_c, 1)
            dve.wait_ge(q_c, 4)
            dve.wait_ge(q_fc, 1)
            fc = psum[:, 3, 0:2 * T].rearrange("p (t k) -> p t k", k=2)
            nc.vector.tensor_scalar(fdg, fc[:, :, 1], gmax[:, 3:4], None, ALU.subtract).then_inc(q_t, 1)
            nc.vector.tensor_copy(fdc[:], fc[:, :, 1]).then_inc(q_fcs, 1)
            nc.vector.tensor_scalar(tAC[:, 2, :], fc[:, :, 0], gmax[:, 3:4], None, ALU.add).then_inc(q_fcs, 1)
            dve.wait_ge(q_fcs, 2)
            nc.vector.tensor_scalar(tAC[:, 0, :], tAC[:, 2, :], 1.0 - SLOPE, 0.0, ALU.mult,
                                    ALU.min).then_inc(q_t, 1)
            nc.vector.tensor_scalar(tAC[:, 1, :], tAC[:, 2, :], SLOPE - 1.0, 0.0, ALU.mult,
                                    ALU.min).then_inc(q_t, 1)
            dve.wait_ge(q_hrs, 3)
            halves = tuple(zip(vr1, (f1[:, 3, :], f1[:, 1, :]), (VS, 0)))
            for k, ((v1, r1), f, at) in enumerate(halves):
                dve.wait_ge(q_fac, k + 1)
                nc.vector.tensor_tensor(v1[:, :, 0:C], hrow[:], f.unsqueeze(2).to_broadcast([P, T, C]),
                                        ALU.mult).then_inc(q_v, 1)
                nc.vector.tensor_copy(v1[:, :, C], f).then_inc(q_v, 1)
            for k, ((v1, r1), f, at) in enumerate(halves):
                dve.wait_ge(q_v, 2 * (k + 1))
                dve.wait_ge(q_sa, k + 1)
                nc.vector.tensor_tensor(r1, v1, X1[:, :, at:at + V1], ALU.subtract).then_inc(q_sd, 1)
            for k, ((v1, r1), f, at) in enumerate(halves):
                dve.wait_ge(q_sd, k + 1)
                dve.wait_ge(q_sa, k + 3)
                nc.vector.tensor_tensor(X1[:, :, at + 2 * V1:at + 3 * V1], r1, X1[:, :, at + V1:at + 2 * V1],
                                        ALU.subtract).then_inc(q_sd, 1)

        layernorm(nc, ln_signals, ln_mem, 1, lambda pool, p: pool.wait_ge(var3, LN_TILES * (p + 1)),
                  sync=project_sync, pool_start=gather, pool_end=spread, dve_start=combine,
                  dve_end=project_dve, act_start=lambda act: nc.scalar.preload_act_table(ACT.Exp),
                  act_end=project_act, pe_start=gather_busy, product=project2, pe_end=project_pe)

        CT = CW // P
        w_c, w_n, w_e, var4 = sem("p6_wc"), sem("p6_wn"), sem("p6_we"), sem("p6_var")

        def chunks_dve(dve):
            dve.sem_inc(z_gfree, 2)

            def sums(n):
                dve.wait_ge(z_g, n + (CT + 1))
                nc.vector.tensor_reduce(num1[:, n, :],
                                        G1[n % 2][:, 0:2 * PARTS * V1].rearrange("p (k c) -> p c k", c=V1), AX,
                                        ALU.add).then_inc(z_gfree, 1)

            links = [0]

            def link(ins):
                links[0] += 1
                ins.then_inc(w_c, 1)
                dve.wait_ge(w_c, links[0])

            def rows(c):
                ts = slice(CT * c, CT * c + CT)
                for k in range(CT):
                    if c == N // CW - 1 and k == CT - 1:
                        finish(c - 1)
                    sums(CT * c + k)
                dve.wait_ge(z_gfree, 2 + CT * (c + 1))
                link(nc.vector.tensor_tensor(emp[:, ts], dg[:, 0, ts], dg[:, 1, ts], ALU.add))
                link(nc.vector.tensor_scalar(emp[:, ts], emp[:, ts], 0.0, None, ALU.is_equal))
                link(nc.vector.scalar_tensor_tensor(deg[:, ts], emp[:, ts], float(N), num1[:, ts, C], ALU.mult,
                                                    ALU.add))
                link(nc.vector.reciprocal(deg[:, ts], deg[:, ts]))
                for t in range(CT * c, CT * c + CT):
                    last = nc.vector.scalar_tensor_tensor(hrow[:, t, :], hsum[:], emp[:, t:t + 1],
                                                          num1[:, t, 0:C], ALU.mult, ALU.add)
                link(last)
                link(nc.vector.tensor_tensor(hrow[:, ts, :], hrow[:, ts, :],
                                             deg[:, ts].unsqueeze(2).to_broadcast([P, CT, C]), ALU.mult))
                nc.vector.tensor_scalar(xn[:, ts, :], hrow[:, ts, :], 0.0, None, ALU.min).then_inc(w_n, 1)
                link(nc.vector.scalar_tensor_tensor(xr[:, ts, :], hrow[:, ts, :], 0.0, xr[:, ts, :], ALU.max,
                                                    ALU.add))

            def finish(c):
                ts = slice(CT * c, CT * c + CT)
                dve.wait_ge(w_e, c + 1)
                link(nc.vector.scalar_tensor_tensor(xr[:, ts, :], xn[:, ts, :], -1.0, xr[:, ts, :], ALU.add,
                                                    ALU.add))
                for t in range(CT * c, CT * c + CT):
                    last = nc.vector.bn_stats(st[:, t, :], xr[:, t, :])
                link(last)
                for t in range(CT * c, CT * c + CT):
                    last = nc.vector.bn_aggr(mv[:, t, :], st[:, t, :])
                last.then_inc(var4, 1)

            for c in range(N // CW):
                hh, cols_ = c % 2, slice(CW * c, CW * c + CW)
                for h in range(2):
                    ts = slice(6 * h, 6 * h + 6)
                    dve.wait_ge(z_t, T * c + 6 * h + 6)
                    nc.vector.tensor_scalar(U1[:, 1 - hh, ts, :], U1[:, 1 - hh, ts, :], 0.0, None,
                                            ALU.is_gt).then_inc(z_m, 1)
                    dve.wait_ge(z_m, 2 * c + h + 1)
                    nc.vector.tensor_tensor(U1[:, 1 - hh, ts, :], U1[:, 1 - hh, ts, :], M2[:, ts, cols_],
                                            ALU.mult).then_inc(z_u, 1)
                    dve.wait_ge(z_u, 2 * c + h + 1)
                    nc.vector.tensor_tensor(V[hh][:, ts, :], M2[:, ts, cols_], U1[:, 1 - hh, ts, :],
                                            ALU.subtract).then_inc(z_v, 1)
                if c > 0:
                    rows(c - 1)
                if c > 1:
                    finish(c - 2)
            rows(N // CW - 1)
            finish(N // CW - 1)

        def chunks_pe(pe):
            pe.sem_inc(z_used, 2)
            with pe.Fori(0, 2) as i:
                for hh in range(2):
                    for k in range(CT):
                        pe.wait_ge(z_g, 2 * CT * i + (CT * hh + k + 1))
                        for t in range(T):
                            if k == 0 and t % 6 == 0:
                                pe.wait_ge(z_v, 4 * i + (2 * hh + t // 6 + 1))
                            nc.tensor.matmul(psum[:, 2 * k, 0:VS], U1[:, 1 - hh, t, P * k:P * k + P],
                                             X1[:, t, 0:VS], start=(t == 0), stop=(t == T - 1),
                                             skip_group_check=True)
                            last = nc.tensor.matmul(psum[:, 2 * k + 1, 0:VS], V[hh][:, t, P * k:P * k + P],
                                                    X1[:, t, VS:2 * VS], start=(t == 0), stop=(t == T - 1),
                                                    skip_group_check=True)
                        last.then_inc(z_full, 1)
                    nc.tensor.matmul(psum[:, 7, 0:2], onesb[:], onesb[:, 0:2], start=True,
                                     stop=True).then_inc(z_used, 1)
            pe.wait_ge(var4, N // CW)
            keep_busy(pe, 32, 7)

        def chunks_act(act):
            act.sem_inc(z_g, CT)

            def exps(c):
                ts = slice(CT * c, CT * c + CT)
                act.wait_ge(w_n, c + 1)
                nc.scalar.activation(xn[:, ts, :], xn[:, ts, :], ACT.Exp).then_inc(w_e, 1)

            scores(act, 0, T // 2)
            scores(act, 1)
            for c in range(N // CW):
                for k in range(CT):
                    if c > 0 and k == CT - 1:
                        exps(c - 1)
                    n = CT * c + k
                    g = G1[n % 2]
                    act.wait_ge(z_full, n + 1)
                    act.wait_ge(z_gfree, n + 1)
                    for m in range(2):
                        nc.scalar.activation(dg[:, m, n:n + 1], psum[:, 2 * k + m, VS - 1:VS], ACT.Copy)
                    nc.scalar.activation(g[:, 0:VS - 1], psum[:, 2 * k, 0:VS - 1], ACT.Copy,
                                         scale=f1[:, 0, n:n + 1])
                    nc.scalar.activation(g[:, VS - 1:2 * VS - 2], psum[:, 2 * k + 1, 0:VS - 1], ACT.Copy,
                                         scale=f1[:, 2, n:n + 1]).then_inc(z_g, 1)
                if c + 2 < N // CW:
                    scores(act, c + 2)
            exps(N // CW - 1)

        h0 = region(150.5, (KC, N), F32)
        h0s = region(72, (KC, FT * TS), F32)
        h2s = region(97, (KC, FT * TS), F32)
        h2 = region(72, (KC, N), F32)
        ring = region(123, (RING, 4 * HID + 4), F32)
        h1r = region(139.25, (2, KC, TS), F32)
        late = bump(143.25, 150.5)
        WsI = late([P, 4 * HID + 4], F32)
        Wi_sb, Wo_sb, bi_sb, boB = (late(k, F32) for k in ([P, HID], [P, KC, C], [P, KC], [P, C]))

        def preload_last(sp):
            sp.wait_ge(z_used, 2 + N // CW)
            for dst, src in ((WsI, WsT), (Wi_sb, WiT), (Wo_sb, WoT), (bi_sb, bi),
                             (boB, bo.squeeze(0).partition_broadcast(P))):
                sp.dma_start(dst, src).then_inc(l_in, 16)

        m_h0p, m_h0a, m_h0d, m_h1p, m_h1, m_h2p, m_ring, m_wsi, m_out, m_bo, m_perm_d, m_perm_a, \
            m_rows, m_done, m_h2w = (sem(f"m_{n}") for n in (
                "h0p", "h0a", "h0d", "h1p", "h1", "h2p", "ring", "wsi", "out", "bo", "perm_d",
                "perm_a", "rows", "done", "h2w"))
        GB = 8

        def group_starts(eng, b):
            return nc.values_load_multi_w_load_instructions(
                gpos_i[0:1, GB * b:GB * b + GB], engines=[eng], min_val=0, max_val=(FT - 1) * TS + TS - GT,
                skip_runtime_bounds_check_because="below the slots' end as made")[1]

        starts = {}

        def first_starts(kind, b):
            starts[b] = group_starts(kind, b)
            starts[b + 2] = group_starts(kind, b + 2)

        def first_layer(pe, q):
            pe.wait_ge(l_in, 80)
            for m in range(KC):
                nc.tensor.matmul(psum[:, H0_BANKS[q][m], :], Wi_sb[:, P * m:P * m + P],
                                 xT[:, 512 * q:512 * q + 512], start=True, stop=True).then_inc(m_h0p, 1)

        def into_slots(kind, eng, first, relu, copy, done):
            eng.wait_ge(l_in, 80)
            for q in range(3):
                eng.wait_ge(m_h0p, KC * q + first + 1)
                relu(h0[:, first, 512 * q:512 * q + 512], psum[:, H0_BANKS[q][first], :])
                for b in range(first, GROUPS // GB, 2):
                    if not 512 * q < GT * GB * (b + 1) <= 512 * (q + 1):
                        continue
                    eng.wait_ge(cleared, 1)
                    eng.wait_ge(m_h0a, q + 1)
                    eng.wait_ge(m_h0d, q + 1)
                    g = starts[b] if b in starts else group_starts(kind, b)
                    for j in range(GB):
                        at = GT * (GB * b + j)
                        copy(h0s[:, :, bass.ds(g[j], GT)], h0[:, :, at:at + GT]).then_inc(done, 1)

        def add_bo(pool):
            pool.wait_ge(ln_signals[1], 3 * T)
            nc.gpsimd.tensor_tensor(xr[:], xr[:], boB.unsqueeze(1).to_broadcast([P, T, C]),
                                    ALU.add).then_inc(m_bo, 1)
            pool.wait_ge(m_bo, 1)

        def experts4(first, count):
            return nc.values_load_multi_w_load_instructions(
                ge[0:1, bass.ds(first, count)], engines=[mybir.EngineType.DVE], min_val=0,
                max_val=E - 1, skip_runtime_bounds_check_because="clamped when made")[1]

        def weights4(k, e):
            nc.vector.tensor_tensor(ring[:, k, :], Wall[:, bass.ds(e, 1), :].squeeze(1), WsI,
                                    ALU.add).then_inc(m_ring, 1)

        def slots_dve(dve):
            into_slots(mybir.EngineType.DVE, dve, 0,
                       lambda dst, src: nc.vector.tensor_scalar(dst, src, bi_sb[:, 0:1], 0.0, ALU.add, ALU.max)
                       .then_inc(m_h0d, 1), nc.vector.tensor_copy, m_perm_d)
            dve.wait_ge(wall_in, 16)
            dve.wait_ge(m_wsi, 2 * KC)
            weights4(0, experts4(0, 1)[0])
            tiles_dve(dve)

        def slots_act(act):
            into_slots(mybir.EngineType.Activation, act, 1,
                       lambda dst, src: nc.scalar.activation(dst, src, ACT.Relu, bias=bi_sb[:, 1:2])
                       .then_inc(m_h0a, 1), lambda dst, src: nc.scalar.activation(dst, src, ACT.Copy), m_perm_a)
            tiles_act(act)

        H0_BANKS = ((3, 4), (5, 6), (7, 0))

        def clear_slots(pool):
            pool.wait_ge(z_v, 2 * (N // CW))
            nc.gpsimd.memset(h0s, 0.0).then_inc(cleared, 1)

        def last_dve(dve):
            chunks_dve(dve)
            first_starts(mybir.EngineType.DVE, 0)

        def last_act(act):
            chunks_act(act)
            first_starts(mybir.EngineType.Activation, 1)

        def shared_weights(pool):
            pool.wait_ge(l_in, 80)
            for l in range(2):
                for k in range(KC):
                    at = l * KC * HID + k * HID + k * P
                    nc.gpsimd.tensor_tensor(WsI[:, at:at + P], WsI[:, at:at + P], ident, ALU.add)\
                        .then_inc(m_wsi, 1)
            add_bo(pool)

        def tiles_dve(dve):
            with dve.Fori(0, (FT - 2) // RING) as i:
                e = experts4(i * RING + 1, RING)
                for j in range(RING):
                    dve.wait_ge(m_h2w, RING * i + (j + 2))
                    weights4((1 + j) % RING, e[j])
            e = experts4(FT - 1, 1)
            dve.wait_ge(m_h2w, FT)
            weights4((FT - 1) % RING, e[0])

        def tiles_pe(pe):
            pe.wait_ge(m_perm_d, 2 * GB)
            keep_busy(pe, 64, 2)
            pe.wait_ge(m_perm_d, GROUPS // 2)
            pe.wait_ge(m_perm_a, GROUPS // 2)
            def layer(l, k, src, bank):
                for o in range(KC):
                    for m in range(KC):
                        at = l * KC * HID + m * HID + o * P
                        last = nc.tensor.matmul(psum[:, bank, TS * o:TS * o + TS], ring[:, k, at:at + P],
                                                src(m), start=(m == 0), stop=(m == KC - 1),
                                                skip_group_check=True)
                return last

            def second(n, k):
                pe.wait_ge(m_ring, n + 1)
                pe.wait_ge(m_h1, n + 1)
                layer(0, k, lambda m: h0s[:, m, bass.ds(n * TS, TS)], 2 + k % 2).then_inc(m_h1p, 1)

            def third(n, k):
                pe.wait_ge(m_h1, n + (2 + 1))
                pe.wait_ge(m_h2w, n + (RING - 2 + 1))
                layer(1, k, lambda m: h1r[:, k % 2, m, :], 4 + k % 2).then_inc(m_h2p, 1)

            second(0, 0)
            with pe.Fori(0, (FT - 2) // RING) as i:
                for j in range(RING):
                    second(RING * i + (1 + j), (1 + j) % RING)
                    third(RING * i + j, j % RING)
            second(FT - 1, (FT - 1) % RING)
            third(FT - 2, (FT - 2) % RING)
            third(FT - 1, (FT - 1) % RING)

        def tiles_act(act):
            act.sem_inc(m_h1, 2)
            act.sem_inc(m_h2w, RING)

            def second(n, k):
                act.wait_ge(m_h1p, n + 1)
                for o in range(KC):
                    last = nc.scalar.activation(h1r[:, k % 2, o, :], psum[:, 2 + k % 2, TS * o:TS * o + TS],
                                                ACT.Relu, bias=ring[:, k, 4 * HID + o:4 * HID + o + 1])
                last.then_inc(m_h1, 1)

            def third(n, k):
                act.wait_ge(m_h2p, n + 1)
                for o in range(KC):
                    last = nc.scalar.activation(
                        h2s[:, o, bass.ds(n * TS, TS)], psum[:, 4 + k % 2, TS * o:TS * o + TS],
                        ACT.Relu, bias=ring[:, k, 4 * HID + KC + o:4 * HID + KC + o + 1])
                last.then_inc(m_h2w, 1)

            second(0, 0)
            with act.Fori(0, (FT - 2) // RING) as i:
                for j in range(RING):
                    second(RING * i + (1 + j), (1 + j) % RING)
                    third(RING * i + j, j % RING)
            second(FT - 1, (FT - 1) % RING)
            third(FT - 2, (FT - 2) % RING)
            third(FT - 1, (FT - 1) % RING)

        layernorm(nc, ln_signals, ln_mem, 2, lambda pool, p: pool.wait_ge(var4, p + 1),
                  sync=preload_last, pool_start=clear_slots, dve_start=last_dve, act_start=last_act,
                  pe_start=chunks_pe, product=first_layer, pool_end=shared_weights, dve_end=slots_dve,
                  act_end=slots_act, pe_end=tiles_pe)

        with nc.Block() as block:
            @block.vector
            def _(dve):
                for b in range(0, GROUPS // GB, 2):
                    g = group_starts(mybir.EngineType.DVE, b)
                    for j in range(GB):
                        nc.vector.tensor_copy(h2[:, :, GT * (GB * b + j):GT * (GB * b + j) + GT],
                                              h2s[:, :, bass.ds(g[j], GT)]).then_inc(m_perm_d, 1)
                for q in range(3):
                    dve.wait_ge(m_out, q + 1)
                    nc.vector.tensor_tensor(xr[:, 4 * q:4 * q + 4, :], xr[:, 4 * q:4 * q + 4, :],
                                            psum[:, q, :].rearrange("p (t c) -> p t c", c=C),
                                            ALU.add).then_inc(m_rows, 1)

            @block.scalar
            def _(act):
                for b in range(1, GROUPS // GB, 2):
                    g = group_starts(mybir.EngineType.Activation, b)
                    for j in range(GB):
                        nc.scalar.activation(h2[:, :, GT * (GB * b + j):GT * (GB * b + j) + GT],
                                             h2s[:, :, bass.ds(g[j], GT)], ACT.Copy).then_inc(m_perm_a, 1)

            @block.tensor
            def _(pe):
                for t in range(T):
                    if t % 3 == 0:
                        pe.wait_ge(m_perm_d, GROUPS // 2 + GB * (t // 3 + 1))
                        pe.wait_ge(m_perm_a, GROUPS // 2 + GB * (t // 3 + 1))
                    for m in range(KC):
                        last = nc.tensor.matmul(psum[:, t // 4, P * (t % 4):P * (t % 4) + P],
                                                h2[:, m, P * t:P * t + P], Wo_sb[:, m, :], start=(m == 0),
                                                stop=(m == KC - 1), skip_group_check=True)
                    if t % 4 == 3:
                        last.then_inc(m_out, 1)

            @block.sync
            def _(sp):
                out_v = out.rearrange("(t p) c -> p t c", p=P)
                for q in range(3):
                    sp.wait_ge(m_rows, q + 1)
                    sp.dma_start(out_v[:, 4 * q:4 * q + 4, :], xr[:, 4 * q:4 * q + 4, :]).then_inc(m_done, 16)
                sp.wait_ge(m_done, 48)


def constants():
    import numpy as np
    c = np.zeros((P, K_END), np.float32)
    c[:, K_ID:K_ID + P] = np.eye(P)
    c[:, K_TRI:K_TRI + P] = np.triu(np.ones((P, P)), 1)
    c[:, K_HM:K_HM + H] = np.arange(P)[:, None] // D == np.arange(H)[None, :]
    c[:, K_IOTA:K_IOTA + E] = np.arange(E)
    c[:, K_SLOT:K_SLOT + SLOT_TILES] = np.arange(SLOT_TILES) * P
    c[:, K_FT:K_FT + FT] = np.arange(FT) * TS
    return c


def kernel(**inputs):
    import numpy as np
    import concourse.bacc as bacc
    from concourse.bass_utils import run_bass_kernel_spmd

    a = {k: np.asarray(v) for k, v in inputs.items()}
    turned = lambda v, *axes: np.ascontiguousarray(np.transpose(v, axes))
    arrays = {
        "x": a["x"], "adjT": turned(a["adj"], 1, 0),
        "gW": turned(a["L0_gnn_W"], 1, 0), "gb": a["L0_gnn_bW"].reshape(C, 1),
        "ga1": np.tile(a["L0_gnn_a1"], H).reshape(C, 1), "ga2": np.tile(a["L0_gnn_a2"], H).reshape(C, 1),
        "gab": a["L0_gnn_ab"].reshape(1), "gate_w": a["L0_ffn_gate_w"],
        "gate_b": a["L0_ffn_gate_b"].reshape(1, E),
        "w1": turned(a["L0_ffn_w1"], 1, 0, 2), "w2": turned(a["L0_ffn_w2"], 1, 0, 2),
        "w3": turned(a["L0_ffn_w3"].reshape(E, KC, P, C), 2, 0, 1, 3).reshape(P, E, HID),
        "uW": a["L1_gnn_W"], "uas": a["L1_gnn_a_src"], "uad": a["L1_gnn_a_dst"],
        "route": a["L1_ffn_route_id"].reshape(GROUPS, 1),
        "WiT": turned(a["L1_ffn_Wi"], 1, 0), "bi": turned(a["L1_ffn_bi"].reshape(KC, P), 1, 0),
        "WrT": np.concatenate([
            turned(a["L1_ffn_Wr"].reshape(2, E, HID, KC, P), 4, 1, 0, 3, 2).reshape(P, E, 4 * HID),
            turned(a["L1_ffn_br"].reshape(2, E, KC, P), 3, 1, 0, 2).reshape(P, E, 4)], axis=2),
        "WsT": np.concatenate([
            turned(a["L1_ffn_Ws"].reshape(2, HID, KC, P), 3, 0, 2, 1).reshape(P, 4 * HID),
            turned(a["L1_ffn_bs"].reshape(2, KC, P), 2, 0, 1).reshape(P, 4)], axis=1),
        "WoT": turned(a["L1_ffn_Wo"].reshape(C, KC, P), 2, 1, 0), "bo": a["L1_ffn_bo"].reshape(1, C),
        "consts": constants(),
    }
    nc = bacc.Bacc("TRN2", target_bir_lowering=False, num_devices=1)
    maps, args = {}, {}
    for name, v in arrays.items():
        v = np.ascontiguousarray(v)
        maps[f"in_{name}"] = v
        args[name] = nc.dram_tensor(f"in_{name}", v.shape, mybir.dt.from_np(v.dtype), kind="ExternalInput").ap()
    args["out"] = nc.dram_tensor("out_rows", (N, C), F32, kind="ExternalOutput").ap()
    build(nc, **args)
    r = run_bass_kernel_spmd(nc, [maps], core_ids=[0])
    return r.results[0]["out_rows"]
```
